# Optimizing a Trainium2 kernel written in Bass

```python
import numpy as np
import jax
import jax.numpy as jnp

def _softmax(x, axis=-1):
    return jax.nn.softmax(x, axis=axis)

def _gelu(x):
    return jax.nn.gelu(x, approximate=True)

def _silu(x):
    return jax.nn.silu(x)

def _sigmoid(x):
    return jax.nn.sigmoid(x)

def _layernorm(x, axis=-1, eps=1e-05):
    m = jnp.mean(x, axis=axis, keepdims=True)
    v = jnp.var(x, axis=axis, keepdims=True)
    return (x - m) / jnp.sqrt(v + eps)

def _scatter_add(tgt, idx, src, axis=0):
    return tgt.at[idx].add(src)

def _segment_sum(src, seg, n):
    return jax.ops.segment_sum(src, seg, n)
kernel_name = 'mk_decoder_preln_d1_seqx_r8_14fb7f'

def setup_inputs(seed: int=0):
    np.random.seed(seed)
    _w = jnp.asarray

    def _rec_inputs():
        import jax
        import jax.numpy as jnp
        _rk = jax.random.key(seed)
        x = -0.0002928 + 1 * jax.random.normal(jax.random.fold_in(_rk, 1), (8, 128, 256), jnp.float32)
        _lenS = 128 - jax.random.randint(jax.random.fold_in(_rk, 7), (8,), 0, max(1, 128 // 4) + 1, jnp.int32)
        _lenS2 = 128 - jax.random.randint(jax.random.fold_in(_rk, 8), (8,), 0, max(1, 128 // 4) + 1, jnp.int32)
        _ctx_2048P = jax.random.normal(jax.random.fold_in(_rk, 11), (8, 16, 256), jnp.float32)
        _ctx_2048c = jax.random.dirichlet(jax.random.fold_in(_rk, 511), 0.3 * jnp.ones((16,), jnp.float32), (8, 128))
        _ctx_2048t = jnp.einsum('bsk,bkd->bsd', _ctx_2048c, _ctx_2048P)
        _ctx_2048t = _ctx_2048t * jax.lax.rsqrt(jnp.mean(jnp.square(_ctx_2048t)) + 1e-12) * 0.953939
        ctx_2048 = -1.39393e-06 + 0.999914 * (_ctx_2048t + 0.3 * jax.random.normal(jax.random.fold_in(_rk, 611), (8, 128, 256), jnp.float32))
        _validS = jnp.arange(128)[None, :] < _lenS[:, None]
        _validS2 = jnp.arange(128)[None, :] < _lenS2[:, None]
        _causal = jnp.tril(jnp.ones((128, 128), dtype=bool))
        mask_Bx1x2048_fk1 = jnp.where(jnp.ones((8, 1, 256), dtype=bool), 1.0, 0.0).astype(jnp.float32)
        return (x, ctx_2048, mask_Bx1x2048_fk1)
    x, ctx_2048, mask_Bx1x2048_fk1 = _rec_inputs()

    def _L0_attn_setup():
        import jax, jax.numpy as jnp
        import numpy as np
        EMB = 256
        HEADS = 16
        HEAD_DIM = EMB // HEADS
        MIN_WINDOW = 64
        MAX_WINDOW = 32
        ROPE_BASE = 10000.0

        def _rotate_half(t):
            x1 = t[..., ::2]
            x2 = t[..., 1::2]
            return jnp.stack((-x2, x1), axis=-1).reshape(t.shape)

        def _rope_tables(seq_len, dtype):
            inv_freq = 1.0 / ROPE_BASE ** (jnp.arange(0, HEAD_DIM, 2, dtype=jnp.float32) / HEAD_DIM)
            pos = jnp.arange(seq_len, dtype=jnp.float32)
            freqs = jnp.outer(pos, inv_freq)
            emb = jnp.concatenate([freqs, freqs], axis=-1)
            return (jnp.cos(emb)[None, None].astype(dtype), jnp.sin(emb)[None, None].astype(dtype))

        def _forward(x, w_qkv, w_out, w_c1, w_c2):
            B, S, _ = x.shape
            scale = HEAD_DIM ** (-0.5)
            qkv = x @ w_qkv.T
            qkv = qkv.reshape(B, S, 3, HEADS, HEAD_DIM).transpose(2, 0, 3, 1, 4)
            q, k, v = (qkv[0], qkv[1], qkv[2])
            cos, sin = _rope_tables(S, x.dtype)
            q = q * cos + _rotate_half(q) * sin
            k = k * cos + _rotate_half(k) * sin
            scores = jnp.einsum('bhqd,bhkd->bhqk', q, k) * scale
            var = jnp.var(x.reshape(B, -1), axis=1, ddof=1)
            var_norm = jax.nn.sigmoid(var * 10.0 - 5.0)
            x_mean = x.mean(axis=1)
            hidden = jax.nn.silu(x_mean @ w_c1.T)
            learned = jax.nn.sigmoid(hidden @ w_c2.T)[:, 0]
            complexity = (var_norm + learned) / 2.0
            window_f = MIN_WINDOW + complexity * (MAX_WINDOW - MIN_WINDOW)
            window = window_f.mean().astype(jnp.int32)
            window = jnp.maximum(jnp.minimum(window, S), MIN_WINDOW)
            pos = jnp.arange(S)
            rel = pos[:, None] - pos[None, :]
            keep = (rel >= 0) & (rel < window)
            scores = jnp.where(keep[None, None], scores, -jnp.inf)
            attn = jax.nn.softmax(scores, axis=-1)
            out = jnp.einsum('bhqk,bhkd->bhqd', attn, v)
            out = out.transpose(0, 2, 1, 3).reshape(B, S, EMB)
            return out @ w_out.T
        key = jax.random.key(seed)
        ks = jax.random.split(key, 5)
        B, S = (2, 256)
        x = jax.random.normal(ks[0], (B, S, EMB), dtype=jnp.float32)
        w_qkv = jax.random.normal(ks[1], (3 * EMB, EMB), dtype=jnp.float32) * EMB ** (-0.5)
        w_out = jax.random.normal(ks[2], (EMB, EMB), dtype=jnp.float32) * EMB ** (-0.5)
        w_c1 = jax.random.normal(ks[3], (EMB // 4, EMB), dtype=jnp.float32) * 0.1 * EMB ** (-0.5)
        w_c2 = jax.random.normal(ks[4], (1, EMB // 4), dtype=jnp.float32) * 0.1 * (EMB // 4) ** (-0.5)
        return {'x': x, 'w_qkv': w_qkv, 'w_out': w_out, 'w_c1': w_c1, 'w_c2': w_c2}
    _L0_attn_all = _L0_attn_setup()
    _L0_attn_in = {k: v for k, v in _L0_attn_all.items() if k in ('w_qkv', 'w_out', 'w_c1', 'w_c2')}
    del _L0_attn_all

    def _L0_xattn_setup():
        import math
        import jax, jax.numpy as jnp
        import numpy as np
        SIZE = 128
        HEADS = 16
        HEAD_DIM = SIZE // HEADS
        B, T, S = (2, 256, 256)
        NEG = 1000000.0
        key = jax.random.key(seed)
        ks = jax.random.split(key, 10)
        target = jax.random.normal(ks[0], (B, SIZE, T), dtype=jnp.float32)
        source = jax.random.normal(ks[1], (B, SIZE, S), dtype=jnp.float32)
        target_mask = (jax.random.uniform(ks[2], (B, 1, T)) > 0.1).astype(jnp.float32)
        source_mask = (jax.random.uniform(ks[3], (B, 1, S)) > 0.1).astype(jnp.float32)
        scale = 1.0 / math.sqrt(SIZE)
        Wq = jax.random.normal(ks[4], (SIZE, SIZE), dtype=jnp.float32) * scale
        Wk = jax.random.normal(ks[5], (SIZE, SIZE), dtype=jnp.float32) * scale
        Wv = jax.random.normal(ks[6], (SIZE, SIZE), dtype=jnp.float32) * scale
        bq = jax.random.normal(ks[7], (SIZE,), dtype=jnp.float32) * 0.01
        bk = jax.random.normal(ks[8], (SIZE,), dtype=jnp.float32) * 0.01
        bv = jax.random.normal(ks[9], (SIZE,), dtype=jnp.float32) * 0.01
        return {'target': target, 'source': source, 'target_mask': target_mask, 'source_mask': source_mask, 'Wq': Wq, 'bq': bq, 'Wk': Wk, 'bk': bk, 'Wv': Wv, 'bv': bv}
    _L0_xattn_all = _L0_xattn_setup()
    _L0_xattn_in = {k: v for k, v in _L0_xattn_all.items() if k in ('Wq', 'bq', 'Wk', 'bk', 'Wv', 'bv')}
    del _L0_xattn_all

    def _L0_ffn_setup():
        import jax, jax.numpy as jnp
        import numpy as np
        DIM = 256
        HID = 128
        E = 8
        K = 2
        SHID = HID * 1
        INIT = 0.02
        key = jax.random.key(seed)
        ks = jax.random.split(key, 9)
        return {'x': jax.random.normal(ks[0], (2, 128, DIM), jnp.float32), 'expert_bias': jnp.zeros((E,), jnp.float32), 'gate_w': jax.random.normal(ks[1], (E, DIM), jnp.float32) * INIT, 'w1': jax.random.normal(ks[2], (E, HID, DIM), jnp.float32) * INIT, 'w2': jax.random.normal(ks[3], (E, DIM, HID), jnp.float32) * INIT, 'w3': jax.random.normal(ks[4], (E, HID, DIM), jnp.float32) * INIT, 'sw1': jax.random.normal(ks[5], (SHID, DIM), jnp.float32) * INIT, 'sw2': jax.random.normal(ks[6], (DIM, SHID), jnp.float32) * INIT, 'sw3': jax.random.normal(ks[7], (SHID, DIM), jnp.float32) * INIT}
    _L0_ffn_all = _L0_ffn_setup()
    _L0_ffn_in = {k: v for k, v in _L0_ffn_all.items() if k in ('expert_bias', 'gate_w', 'w1', 'w2', 'w3', 'sw1', 'sw2', 'sw3')}
    del _L0_ffn_all
    return {'x': x, 'ctx_2048': ctx_2048, 'mask_Bx1x2048_fk1': mask_Bx1x2048_fk1, 'L0_attn_w_qkv': _L0_attn_in['w_qkv'], 'L0_attn_w_out': _L0_attn_in['w_out'], 'L0_attn_w_c1': _L0_attn_in['w_c1'], 'L0_attn_w_c2': _L0_attn_in['w_c2'], 'L0_xattn_Wq': _L0_xattn_in['Wq'], 'L0_xattn_bq': _L0_xattn_in['bq'], 'L0_xattn_Wk': _L0_xattn_in['Wk'], 'L0_xattn_bk': _L0_xattn_in['bk'], 'L0_xattn_Wv': _L0_xattn_in['Wv'], 'L0_xattn_bv': _L0_xattn_in['bv'], 'L0_ffn_expert_bias': _L0_ffn_in['expert_bias'], 'L0_ffn_gate_w': _L0_ffn_in['gate_w'], 'L0_ffn_w1': _L0_ffn_in['w1'], 'L0_ffn_w2': _L0_ffn_in['w2'], 'L0_ffn_w3': _L0_ffn_in['w3'], 'L0_ffn_sw1': _L0_ffn_in['sw1'], 'L0_ffn_sw2': _L0_ffn_in['sw2'], 'L0_ffn_sw3': _L0_ffn_in['sw3']}

def reference(x, ctx_2048, mask_Bx1x2048_fk1, L0_attn_w_qkv, L0_attn_w_out, L0_attn_w_c1, L0_attn_w_c2, L0_xattn_Wq, L0_xattn_bq, L0_xattn_Wk, L0_xattn_bk, L0_xattn_Wv, L0_xattn_bv, L0_ffn_expert_bias, L0_ffn_gate_w, L0_ffn_w1, L0_ffn_w2, L0_ffn_w3, L0_ffn_sw1, L0_ffn_sw2, L0_ffn_sw3):
    import jax
    import jax.numpy as jnp

    def _L0_attn_ref(x, w_qkv, w_out, w_c1, w_c2):
        import jax, jax.numpy as jnp
        import numpy as np
        EMB = 256
        HEADS = 16
        HEAD_DIM = EMB // HEADS
        MIN_WINDOW = 64
        MAX_WINDOW = 32
        ROPE_BASE = 10000.0

        def _rotate_half(t):
            x1 = t[..., ::2]
            x2 = t[..., 1::2]
            return jnp.stack((-x2, x1), axis=-1).reshape(t.shape)

        def _rope_tables(seq_len, dtype):
            inv_freq = 1.0 / ROPE_BASE ** (jnp.arange(0, HEAD_DIM, 2, dtype=jnp.float32) / HEAD_DIM)
            pos = jnp.arange(seq_len, dtype=jnp.float32)
            freqs = jnp.outer(pos, inv_freq)
            emb = jnp.concatenate([freqs, freqs], axis=-1)
            return (jnp.cos(emb)[None, None].astype(dtype), jnp.sin(emb)[None, None].astype(dtype))

        def _forward(x, w_qkv, w_out, w_c1, w_c2):
            B, S, _ = x.shape
            scale = HEAD_DIM ** (-0.5)
            qkv = x @ w_qkv.T
            qkv = qkv.reshape(B, S, 3, HEADS, HEAD_DIM).transpose(2, 0, 3, 1, 4)
            q, k, v = (qkv[0], qkv[1], qkv[2])
            cos, sin = _rope_tables(S, x.dtype)
            q = q * cos + _rotate_half(q) * sin
            k = k * cos + _rotate_half(k) * sin
            scores = jnp.einsum('bhqd,bhkd->bhqk', q, k) * scale
            var = jnp.var(x.reshape(B, -1), axis=1, ddof=1)
            var_norm = jax.nn.sigmoid(var * 10.0 - 5.0)
            x_mean = x.mean(axis=1)
            hidden = jax.nn.silu(x_mean @ w_c1.T)
            learned = jax.nn.sigmoid(hidden @ w_c2.T)[:, 0]
            complexity = (var_norm + learned) / 2.0
            window_f = MIN_WINDOW + complexity * (MAX_WINDOW - MIN_WINDOW)
            window = window_f.mean().astype(jnp.int32)
            window = jnp.maximum(jnp.minimum(window, S), MIN_WINDOW)
            pos = jnp.arange(S)
            rel = pos[:, None] - pos[None, :]
            keep = (rel >= 0) & (rel < window)
            scores = jnp.where(keep[None, None], scores, -jnp.inf)
            attn = jax.nn.softmax(scores, axis=-1)
            out = jnp.einsum('bhqk,bhkd->bhqd', attn, v)
            out = out.transpose(0, 2, 1, 3).reshape(B, S, EMB)
            return out @ w_out.T
        return _forward(x, w_qkv, w_out, w_c1, w_c2)

    def _L0_xattn_ref(target, source, target_mask, source_mask, Wq, bq, Wk, bk, Wv, bv):
        import math
        import jax, jax.numpy as jnp
        import numpy as np
        SIZE = 128
        HEADS = 16
        HEAD_DIM = SIZE // HEADS
        B, T, S = (2, 256, 256)
        NEG = 1000000.0
        b, _, t = target.shape
        s = source.shape[-1]
        q = jnp.einsum('oc,bct->bot', Wq, target) + bq[None, :, None]
        k = jnp.einsum('oc,bcs->bos', Wk, source) + bk[None, :, None]
        v = jnp.einsum('oc,bcs->bos', Wv, source) + bv[None, :, None]
        q = q.reshape(b, HEADS, HEAD_DIM, t)
        k = k.reshape(b, HEADS, HEAD_DIM, s)
        v = v.reshape(b, HEADS, HEAD_DIM, s)
        dot = jnp.einsum('bhdt,bhds->bhts', q, k) / math.sqrt(HEAD_DIM)
        mask = target_mask[:, :, :, None] * source_mask[:, :, None, :]
        dot = mask * dot - (1.0 - mask) * NEG
        amap = jax.nn.softmax(dot, axis=-1) * mask
        out = jnp.einsum('bhts,bhds->bhdt', amap, v)
        return out.reshape(b, HEADS * HEAD_DIM, t)

    def _L0_ffn_ref(x, expert_bias, gate_w, w1, w2, w3, sw1, sw2, sw3):
        import jax, jax.numpy as jnp
        import numpy as np
        DIM = 256
        HID = 128
        E = 8
        K = 2
        SHID = HID * 1
        INIT = 0.02
        B, S, D = x.shape
        xf = x.reshape(-1, D)
        N = xf.shape[0]
        scores = jax.nn.sigmoid((xf @ gate_w.T).astype(jnp.float32))
        _, sel = jax.lax.top_k(scores + expert_bias[None, :], K)
        top_scores = jnp.take_along_axis(scores, sel, axis=1)
        flat_exp = sel.reshape(-1)
        order = jnp.argsort(flat_exp, stable=True)
        sorted_exp = flat_exp[order]
        tok_idx = order // K
        sc_sorted = top_scores.reshape(-1)[order]
        rin = xf[tok_idx] * sc_sorted[:, None].astype(x.dtype)
        out_sorted = jnp.zeros_like(rin)
        for e in range(E):
            m = (sorted_exp == e)[:, None].astype(rin.dtype)
            h = jax.nn.silu(rin @ w1[e].T) * (rin @ w3[e].T)
            out_sorted = out_sorted + m * (h @ w2[e].T)
        routed = jnp.zeros((N, D), x.dtype).at[tok_idx].add(out_sorted)
        shared = jax.nn.silu(xf @ sw1.T) * (xf @ sw3.T) @ sw2.T
        return (routed + shared).reshape(B, S, D)
    x = x + _L0_attn_ref(_layernorm(x, axis=-1), L0_attn_w_qkv, L0_attn_w_out, L0_attn_w_c1, L0_attn_w_c2)
    x = x + _L0_xattn_ref(_layernorm(x, axis=-1), ctx_2048, mask_Bx1x2048_fk1, mask_Bx1x2048_fk1, L0_xattn_Wq, L0_xattn_bq, L0_xattn_Wk, L0_xattn_bk, L0_xattn_Wv, L0_xattn_bv)
    x = x + _L0_ffn_ref(_layernorm(x, axis=-1), L0_ffn_expert_bias, L0_ffn_gate_w, L0_ffn_w1, L0_ffn_w2, L0_ffn_w3, L0_ffn_sw1, L0_ffn_sw2, L0_ffn_sw3)
    return x

_drawn_inputs = setup_inputs


def setup_inputs(seed=0):
    import zlib

    import numpy as np

    out = dict(_drawn_inputs(seed))
    spreads = {'L0_ffn_expert_bias': (0.0, 0.8)}
    factors = {'L0_xattn_bq': 8.0,
     'L0_xattn_bk': 64.0,
     'L0_xattn_bv': 33.248,
     'L0_ffn_gate_w': 8.0,
     'L0_ffn_w1': 8.0,
     'L0_ffn_w2': 8.0,
     'L0_ffn_w3': 8.0,
     'L0_ffn_sw1': 5.396,
     'L0_ffn_sw2': 5.333,
     'L0_ffn_sw3': 5.327}
    for name, (base, spread) in spreads.items():
        noise = np.random.default_rng([zlib.crc32(name.encode()), seed]).standard_normal(out[name].shape)
        drawn = base * np.exp(spread * noise) if base else spread * noise
        out[name] = jnp.asarray(drawn.astype(out[name].dtype))
    for name, factor in factors.items():
        out[name] = (out[name] * factor).astype(out[name].dtype)
    return out
```

```python
from contextlib import ExitStack

import concourse.bass as bass
from concourse import mybir
import numpy as np

F32 = mybir.dt.float32
BF16 = mybir.dt.bfloat16
ALU = mybir.AluOpType
ACT = mybir.ActivationFunctionType
AX = mybir.AxisListType

P = 128
B, D = 8, 256
PAIRS = B // 2
H = 16
HD1, HD2 = D // H, P // H
E = 8
KT = D // P
WINDOW = 64
NEG = 1.0e6
MASKED = -1.0e30
EPS = 1e-5

COMBOS = ((0, 1, 2, 0, 1, 0), (0, 0, 0, 1, 1, 2))
MASK_ROW, MASK_ROWS = len(COMBOS[0]) * HD2, 12
MAX_ROW = 96
A_ROWS, B_ROWS = MAX_ROW, MAX_ROW + 3

A0, A1, B0, B1, PV, F0, F1 = 0, 1, 2, 3, 4, 6, 7

ORDER = (E,) + tuple(range(E))


def wait(engine, sem, count):
    if not (isinstance(count, int) and count == 0):
        engine.wait_ge(sem, count)


class Chain:

    def __init__(self, engine, sem, links):
        self.engine, self.sem, self.links = engine, sem, links

    def start(self, turn):
        self.base, self.n = turn * self.links, 0

    def link(self, instruction):
        instruction.then_inc(self.sem, 1)
        self.n += 1
        self.engine.wait_ge(self.sem, self.base + self.n)

    def end(self):
        assert self.n == self.links, self.n


def decoder(nc, x, ctx_in, mask, wqkv, wout, wq, wk, wv, bq, bk, bv, ebias, gate, w13, w2,
            cos, sin, keep_qk, keep_kq, ident, lower, out):
    with ExitStack() as stack:
        def sb(name, shape, dt=F32):
            return stack.enter_context(nc.sbuf_tensor(name, shape, dt))

        def sem(name):
            return stack.enter_context(nc.semaphore(name))

        ps = stack.enter_context(nc.psum_tensor("ps", [P, 8, 512], F32))

        wqkv_sb = sb("wqkv_sb", [P, KT, 5 * D])
        wout_sb = sb("wout_sb", [P, KT, D])
        wx_sb = sb("wx_sb", [P, 3, P])
        bqk_sb = sb("bqk_sb", [P, 2])
        bv_sb = sb("bv_sb", [P, P])
        ebias_sb = sb("ebias_sb", [P, E])
        gate_sb = sb("gate_sb", [P, KT, E])
        w13_sb = sb("w13_sb", [P, E + 1, KT, 2, P])
        w2_sb = sb("w2_sb", [P, E + 1, D])
        cos_sb = sb("cos_sb", [P, P])
        sin_sb = sb("sin_sb", [P, P])
        keep_f = sb("keep_f", [P, 2, P])
        keep_sb = sb("keep_sb", [P, 2, 4, P], BF16)
        id_f = sb("id_f", [P, P])
        id_b = sb("id_b", [P, P], BF16)
        lower_sb = sb("lower_sb", [P, E, E])

        x_in = sb("x_in", [P, 2, D])
        ctx_sb = sb("ctx_sb", [P, 2, D])
        x1 = sb("x1", [P, 2, D])
        x2 = sb("x2", [P, 2, D])
        x3 = sb("x3", [P, 2, D])
        xn = sb("xn", [P, 2, D])
        xn1T = sb("xn1T", [P, KT, D])
        xn3T = sb("xn3T", [P, KT, D])
        stats = sb("stats", [P, 2, 6])
        moments = sb("moments", [P, 2, 2])
        settled = sb("settled", [P, 1])
        var_eps = sb("var_eps", [P, 2, 1])
        one = sb("one", [P, 1])
        minus_half = sb("minus_half", [P, 2, 1])
        rstd = sb("rstd", [P, 2, 1])

        prob = sb("prob", [P, 8, 512])
        qk = sb("qk", [P, 2, 512])
        rest = sb("rest", [P, 2, 512])
        parts = sb("parts", [P, 6, 512], BF16)
        heads_out = sb("heads_out", [P, 4, D])

        rope_t = prob[:, 0:4, :].rearrange("p (n m) s -> p n m s", n=2)
        qk1, rest1 = qk, rest
        parts1 = parts[:].rearrange("p (c n) s -> p c n s", c=3)
        stack1 = [sb(f"stack1_{n}", [P, H, D], BF16) for n in "qk"]
        v1 = sb("v1", [P, 2, H, 32])
        max1 = sb("max1", [P, 2, H])
        mrest1 = sb("mrest1", [P, 2, H])
        mparts1 = sb("mparts1", [P, 2, P], BF16)
        mT1 = sb("mT1", [3 * H, D], BF16)
        prob1 = prob
        o1 = heads_out
        o1d = sb("o1d", [P, KT, D])
        o1s = sb("o1s", [P, KT, D])
        attnT = sb("attnT", [P, KT, D])

        m_all = sb("m_all", [B, D])
        m_pen = sb("m_pen", [B, D])
        m_r = sb("m_r", [B, 2, D])
        m_bc = sb("m_bc", [P, 2, D])
        m_bcs = sb("m_bcs", [P, 2, D])
        m_col = sb("m_col", [P, 2, 2])
        qk2 = qk[:].rearrange("p a (n t) -> p a n t", n=2)
        rest2 = rest[:].rearrange("p a (n t) -> p a n t", n=2)
        parts2 = parts[:].rearrange("p (a c) (n t) -> p a c n t", a=2, n=2)
        stack2 = [[sb(f"stack2_{a}{n}", [P, H, D], BF16) for n in "qk"] for a in range(2)]
        v2t = sb("v2t", [P, 4, P])
        v2 = sb("v2", [P, 4, H, 32])
        max2 = sb("max2", [P, 2, 2, H])
        mrest2 = sb("mrest2", [P, 2, 2, H])
        mparts2 = sb("mparts2", [P, 2, 2, P], BF16)
        mT2 = sb("mT2", [3 * H, 2, D], BF16)
        prob2 = prob
        o2 = heads_out
        o2d = sb("o2d", [P, 2, D])
        o2s = sb("o2s", [P, 2, D])

        ez = sb("ez", [P, 2, E])
        den = sb("den", [P, 2, E])
        score = sb("score", [P, 2, E])
        biased = sb("biased", [P, 2, E])
        above = sb("above", [P, 2, E, E])
        equal = sb("equal", [P, 2, E, E])
        rank = sb("rank", [P, 2, E])
        gates = sb("gates", [P, 2, E])
        gT = sb("gT", [E, D])
        g_bc = sb("g_bc", [P, E, D])
        mrow_q = g_bc[0:B, 0:6, :].bitcast(BF16).rearrange("b e (u t) -> b (e u) t", u=2)
        mrow_k = prob[0:B, 4:7, :].bitcast(BF16).rearrange("b e (u t) -> b (e u) t", u=4)
        u13 = sb("u13", [P, 2, 2, D])
        eu = sb("eu", [P, 2, D])
        du = sb("du", [P, 2, D])
        wu = sb("wu", [P, 2, D])
        ru = sb("ru", [P, 2, D])
        hT = sb("hT", [P, 2, D])

        d_parts1 = nc.dram_tensor("d_parts1", [3, 2, 2, P, D], BF16).ap()
        d_parts2 = nc.dram_tensor("d_parts2", [2, 3, 2, P, D], BF16).ap()
        d_mT1 = nc.dram_tensor("d_mT1", [3 * H, D], BF16).ap()
        d_mT2 = nc.dram_tensor("d_mT2", [2, 3 * H, D], BF16).ap()
        d_o1 = nc.dram_tensor("d_o1", [H, 32, D], F32).ap()
        d_o2 = nc.dram_tensor("d_o2", [2, H, 16, D], F32).ap()
        d_mrow = nc.dram_tensor("d_mrow", [2, B, MASK_ROWS, D], BF16).ap()
        d_g = nc.dram_tensor("d_g", [E, D], F32).ap()

        ld_first = sem("ld_first")
        ld_rest = sem("ld_rest")
        x_ld = sem("x_ld")
        ctx_ld = sem("ctx_ld")
        mbc_ld = sem("mbc_ld")
        mall_ld = sem("mall_ld")
        fills = sem("fills")
        consts = sem("consts")
        mrow_chain = sem("mrow_chain")
        mrow_st = sem("mrow_st")
        var_ready = [sem(f"var_ready{n}") for n in range(3)]
        rstd_ready = [sem(f"rstd_ready{n}") for n in range(3)]
        ln1_chain = sem("ln1_chain")
        xn1_ready = sem("xn1_ready")
        xT1_ps = sem("xT1_ps")
        xT1_sb = sem("xT1_sb")
        proj1 = sem("proj1")
        rope_read = sem("rope_read")
        rope_done = sem("rope_done")
        v1_ready = sem("v1_ready")
        high1 = sem("high1")
        rest1_ready = sem("rest1_ready")
        mid1 = sem("mid1")
        parts1_ready = sem("parts1_ready")
        parts1_st = sem("parts1_st")
        stack1_ld = sem("stack1_ld")
        sa1 = sem("sa1")
        max1_done = sem("max1_done")
        mp1_chain = sem("mp1_chain")
        mparts1_ready = sem("mparts1_ready")
        mT1_ps = sem("mT1_ps")
        mT1_sb = sem("mT1_sb")
        mT1_st = sem("mT1_st")
        mrow1_ld = sem("mrow1_ld")
        sb1 = sem("sb1")
        exp1 = sem("exp1")
        pv1 = sem("pv1")
        o1_sb = sem("o1_sb")
        o1_st = sem("o1_st")
        o1_ld = sem("o1_ld")
        o1_inverse = sem("o1_inverse")
        attn_ready = sem("attn_ready")
        oproj = sem("oproj")
        x1_ready = sem("x1_ready")
        ln2_chain = sem("ln2_chain")
        xn2_ready = sem("xn2_ready")
        mbcs_ready = sem("mbcs_ready")
        proj2 = sem("proj2")
        q2_done = sem("q2_done")
        qk2_done = sem("qk2_done")
        v2t_ready = sem("v2t_ready")
        v2_ready = sem("v2_ready")
        high2 = sem("high2")
        rest2_ready = sem("rest2_ready")
        mid2 = sem("mid2")
        parts2_ready = sem("parts2_ready")
        parts2_st = sem("parts2_st")
        stack2_ld = [sem(f"stack2_ld{a}") for a in range(2)]
        sa2 = sem("sa2")
        max2_done = sem("max2_done")
        mp2_chain = sem("mp2_chain")
        mparts2_ready = sem("mparts2_ready")
        mT2_ps = sem("mT2_ps")
        mT2_sb = sem("mT2_sb")
        mT2_st = sem("mT2_st")
        mrow2_ld = [sem(f"mrow2_ld{a}") for a in range(2)]
        sb2 = sem("sb2")
        exp2 = sem("exp2")
        pv2g = sem("pv2g")
        o2_sb = sem("o2_sb")
        o2_st = sem("o2_st")
        o2_ld = [sem(f"o2_ld{a}") for a in range(2)]
        x2_chain = sem("x2_chain")
        x2_ready = sem("x2_ready")
        ln3_chain = sem("ln3_chain")
        xn3_ready = sem("xn3_ready")
        xT3_ps = sem("xT3_ps")
        xT3_sb = sem("xT3_sb")
        logits = sem("logits")
        ez_ready = sem("ez_ready")
        route_chain = sem("route_chain")
        gates_ready = sem("gates_ready")
        gT_ps = sem("gT_ps")
        gT_sb = sem("gT_sb")
        gT_st = sem("gT_st")
        g_ld = sem("g_ld")
        up = sem("up")
        u_ready = sem("u_ready")
        eu_ready = sem("eu_ready")
        wu_ready = sem("wu_ready")
        du_ready = sem("du_ready")
        ru_ready = sem("ru_ready")
        h_ready = sem("h_ready")
        down = sem("down")
        x3_ready = sem("x3_ready")
        out_st = sem("out_st")

        block = stack.enter_context(nc.Block())

        N_STACK1 = 16 * 2 * len(COMBOS[0])
        N_STACK2 = 16 * (2 * len(COMBOS[0]) + 2)
        FIRST, REST = 6, 12

        @block.sync
        def _(sp):
            def load_x(j):
                sp.dma_start(x_in[:], x[bass.ds(2 * j, 2)].rearrange("a s d -> s a d")).then_inc(x_ld, 16)

            def load_ctx(i):
                sp.dma_start(ctx_sb[:], ctx_in[bass.ds(2 * i, 2)].rearrange("a s d -> s a d")).then_inc(ctx_ld, 16)
                sp.dma_start(m_bc[:], mask[bass.ds(2 * i, 2)].rearrange("a o t -> o a t").broadcast_to([P, 2, D])
                             ).then_inc(mbc_ld, 16)
                for a in range(2):
                    sp.dma_start(m_col[:, a, :], mask[bass.ds(2 * i + a, 1)].rearrange("a o (k p) -> p (a o k)", p=P),
                                 allow_slow_non_contiguous=True).then_inc(mbc_ld, 16)

            load_x(0)
            sp.dma_start(id_f[:], ident).then_inc(ld_first, 16)
            sp.dma_start(wqkv_sb[:], wqkv.rearrange("(k p) n -> p k n", p=P)).then_inc(ld_first, 16)
            sp.dma_start(cos_sb[:], cos).then_inc(ld_first, 16)
            sp.dma_start(sin_sb[:], sin).then_inc(ld_first, 16)
            sp.dma_start(keep_f[:, 0, :], keep_qk).then_inc(ld_first, 16)
            sp.dma_start(keep_f[:, 1, :], keep_kq).then_inc(ld_first, 16)
            sp.dma_start(m_all[:], mask.rearrange("b o t -> b (o t)")).then_inc(mall_ld, 16)
            sp.dma_start(wout_sb[:], wout.rearrange("(k p) n -> p k n", p=P)).then_inc(ld_rest, 16)
            load_ctx(0)
            for n, w in enumerate((wq, wk, wv)):
                sp.dma_start(wx_sb[:, n, :], w).then_inc(ld_rest, 16)
            sp.dma_start(bqk_sb[:, 0:1], bq).then_inc(ld_rest, 16)
            sp.dma_start(bqk_sb[:, 1:2], bk).then_inc(ld_rest, 16)
            sp.dma_start(bv_sb[:], bv.broadcast_to([P, P])).then_inc(ld_rest, 16)
            sp.dma_start(ebias_sb[:], ebias.broadcast_to([P, E])).then_inc(ld_rest, 16)
            sp.dma_start(gate_sb[:], gate.rearrange("(k p) n -> p k n", p=P)).then_inc(ld_rest, 16)
            sp.dma_start(lower_sb[:].rearrange("p e f -> p (e f)"), lower.broadcast_to([P, E * E])).then_inc(ld_rest, 16)
            sp.dma_start(w13_sb[:], w13).then_inc(ld_rest, 16)
            sp.dma_start(w2_sb[:], w2).then_inc(ld_rest, 16)
            sp.wait_ge(mrow_chain, 11)
            sp.dma_start(d_mrow[0], mrow_q).then_inc(mrow_st, 16)
            sp.dma_start(d_mrow[1], mrow_k).then_inc(mrow_st, 16)

            def self_stacks(j):
                sp.wait_ge(parts1_ready, j + 1)
                sp.dma_start(d_parts1.rearrange("c n t p s -> p (c n t) s"),
                             parts1.rearrange("p c n (t s) -> p (c n t) s", t=2)).then_inc(parts1_st, 16)
                sp.wait_ge(parts1_st, 16 * (j + 1))
                for n in range(2):
                    for g, c in enumerate(COMBOS[n]):
                        sp.dma_start(stack1[n][HD1 * g:HD1 * (g + 1)].rearrange("d h s -> d (h s)"),
                                     d_parts1[c, n].rearrange("t (d h) s -> (t d) (h s)", h=H)).then_inc(stack1_ld, 16)

            def self_max(j):
                sp.wait_ge(mT1_sb, j + 1)
                sp.dma_start(d_mT1, mT1[:]).then_inc(mT1_st, 16)
                sp.wait_ge(mT1_st, 16 * (j + 1))
                sp.dma_start(stack1[0][MAX_ROW:B_ROWS].rearrange("c h s -> c (h s)"),
                             d_mT1.rearrange("(c h) s -> c (h s)", h=H)).then_inc(mrow1_ld, 16)

            def self_out(j):
                sp.wait_ge(o1_sb, j + 1)
                for q in range(4):
                    sp.dma_start(d_o1.rearrange("(g q) r s -> q r g s", q=4)[q],
                                 o1[32 * q:32 * q + 32]).then_inc(o1_st, 16)
                sp.wait_ge(o1_st, 64 * (j + 1))
                for k in range(KT):
                    half = d_o1[8 * k:8 * k + 8]
                    sp.dma_start(o1d[:, k, :], half[:, 0:HD1, :]).then_inc(o1_ld, 16)
                    sp.dma_start(o1s[:, k, :], half[:, HD1:2 * HD1, :]).then_inc(o1_ld, 16)

            def cross_stacks(i):
                sp.wait_ge(parts2_ready, i + 1)
                sp.dma_start(d_parts2.rearrange("a c n p t -> p (a c n) t"),
                             parts2.rearrange("p a c n t -> p (a c n) t")).then_inc(parts2_st, 16)
                sp.wait_ge(parts2_st, 16 * (i + 1))
                for a in range(2):
                    for n in range(2):
                        for g, c in enumerate(COMBOS[n]):
                            sp.dma_start(stack2[a][n][HD2 * g:HD2 * (g + 1)].rearrange("d h t -> d (h t)"),
                                         d_parts2[a, c, n].rearrange("(d h) t -> d (h t)", h=H)
                                         ).then_inc(stack2_ld[a], 16)

            def cross_mask_rows(i):
                for a in range(2):
                    for n in range(2):
                        rows = d_mrow[n, bass.ds(2 * i + a, 1)].rearrange("a r (o t) -> (a r) o t", o=1)
                        sp.dma_start(stack2[a][n][MASK_ROW:MASK_ROW + MASK_ROWS],
                                     rows.broadcast_to([MASK_ROWS, H, D])).then_inc(stack2_ld[a], 16)

            def cross_max(i, a):
                sp.wait_ge(mT2_sb, 2 * i + a + 1)
                sp.dma_start(d_mT2[a], mT2[:, a, :]).then_inc(mT2_st, 16)
                sp.wait_ge(mT2_st, 16 * (2 * i + a + 1))
                sp.dma_start(stack2[a][0][MAX_ROW:B_ROWS].rearrange("c h t -> c (h t)"),
                             d_mT2[a].rearrange("(c h) t -> c (h t)", h=H)).then_inc(mrow2_ld[a], 16)

            def cross_out(i, a):
                sp.wait_ge(o2_sb, 2 * i + a + 1)
                for q in range(4):
                    sp.dma_start(d_o2[a].rearrange("(g q) r t -> q r g t", q=4)[q],
                                 o2[32 * q:32 * q + 16]).then_inc(o2_st, 16)
                sp.wait_ge(o2_st, 64 * (2 * i + a + 1))
                sp.dma_start(o2d[:, a, :], d_o2[a, :, 0:HD2, :]).then_inc(o2_ld[a], 16)
                sp.dma_start(o2s[:, a, :], d_o2[a, :, HD2:2 * HD2, :]).then_inc(o2_ld[a], 16)

            def self_stage(j):
                self_stacks(j)
                self_max(j)
                self_out(j)

            def cross_stage(i):
                wait(sp, exp2, 32 * i)
                cross_mask_rows(i)
                cross_stacks(i)
                cross_max(i, 0)
                cross_max(i, 1)
                cross_out(i, 0)
                cross_out(i, 1)

            def experts_stage(i):
                sp.wait_ge(gT_sb, i + 1)
                sp.dma_start(d_g, gT[:]).then_inc(gT_st, 16)
                sp.wait_ge(gT_st, 16 * (i + 1))
                sp.dma_start(g_bc[:].rearrange("p e t -> p (e t)"),
                             d_g.rearrange("(o e) t -> o (e t)", o=1).broadcast_to([P, E * D])).then_inc(g_ld, 16)
                sp.wait_ge(x3_ready, i + 1)
                sp.dma_start(out[bass.ds(2 * i, 2)].rearrange("a s d -> s a d"), x3[:]).then_inc(out_st, 16)

            self_stage(0)
            sp.wait_ge(mrow_st, 32)

            def turn(i):
                sp.wait_ge(x1_ready, i + 1)
                load_x(i + 1)
                cross_stage(i)
                self_stage(i + 1)
                sp.wait_ge(v2_ready, i + 1)
                sp.wait_ge(x2_ready, 2 * i + 2)
                load_ctx(i + 1)
                experts_stage(i)

            turn(0)
            with sp.Fori(1, PAIRS - 1) as i:
                turn(i)
            cross_stage(PAIRS - 1)
            experts_stage(PAIRS - 1)
            sp.wait_ge(out_st, 16 * PAIRS)

        @block.tensor
        def _(pe):
            def self_project(j):
                pe.wait_ge(xn1_ready, j + 1)
                wait(pe, exp2, 32 * j)
                for k in range(KT):
                    for a in range(2):
                        mm = pe.transpose(ps[:, B0, D * k + P * a:D * k + P * (a + 1)],
                                          xn[:, a, P * k:P * (k + 1)], id_f[:])
                mm.then_inc(xT1_ps, 1)
                pe.wait_ge(xT1_sb, j + 1)
                wait(pe, mT2_sb, 2 * j)
                for n, bank in enumerate((A0, A1, B0, B1)):
                    for t in range(2):
                        for k in range(KT):
                            mm = pe.matmul(ps[:, bank, D * t:D * (t + 1)],
                                           wqkv_sb[:, k, D * n + P * t:D * n + P * (t + 1)], xn1T[:, k, :],
                                           start=(k == 0), stop=(k == KT - 1))
                    mm.then_inc(proj1, 1)
                wait(pe, o2_sb, 2 * j)
                for a in range(2):
                    for k in range(KT):
                        mm = pe.matmul(ps[:, PV, D * a:D * (a + 1)], xn1T[:, k, P * a:P * (a + 1)],
                                       wqkv_sb[:, k, 4 * D:5 * D], start=(k == 0), stop=(k == KT - 1))
                mm.then_inc(proj1, 1)

            def self_scores(j):
                pe.wait_ge(stack1_ld, N_STACK1 * (j + 1))
                for c in range(8):
                    a, h0 = c // 4, 4 * (c % 4)
                    if c < 2:
                        pe.wait_ge(rope_read, 4 * j + 2)
                    else:
                        pe.wait_ge(max1_done, 8 * j + c - 1)
                    bank = ps[:, A0 + c % 2, :]
                    pe.matmul(bank, id_b[:], keep_sb[:, 0].rearrange("p g s -> p (g s)"), start=True, stop=False,
                              skip_group_check=True)
                    for n in range(4):
                        cols = slice(P * a, P * (a + 1))
                        mm = pe.matmul(bank[:, P * n:P * (n + 1)], stack1[0][0:A_ROWS, h0 + n, cols],
                                       stack1[1][0:A_ROWS, h0 + n, cols], start=False, stop=(n == 3),
                                       skip_group_check=True)
                    mm.then_inc(sa1, 1)
                pe.wait_ge(mparts1_ready, j + 1)
                mT = ps[:, A0, :].bitcast(BF16)
                for a in range(2):
                    mm = pe.transpose(mT[:, P * a:P * (a + 1)], mparts1[:, a], id_b[:])
                mm.then_inc(mT1_ps, 1)

            def self_values(j):
                pe.wait_ge(mrow1_ld, 16 * (j + 1))
                pe.wait_ge(rope_read, 4 * j + 4)
                pe.wait_ge(v1_ready, j + 1)

                def scores(c):
                    a, h0 = c % 2, 4 * (c // 2)
                    if c >= 2:
                        pe.wait_ge(exp1, 8 * j + c - 1)
                    bank = ps[:, B0 + c % 2, :]
                    pe.matmul(bank, id_b[:], keep_sb[:, 1].rearrange("p g s -> p (g s)"), start=True, stop=False,
                              skip_group_check=True)
                    for n in range(4):
                        cols = slice(P * a, P * (a + 1))
                        mm = pe.matmul(bank[:, P * n:P * (n + 1)], stack1[1][0:B_ROWS, h0 + n, cols],
                                       stack1[0][0:B_ROWS, h0 + n, cols], start=False, stop=(n == 3),
                                       skip_group_check=True)
                    mm.then_inc(sb1, 1)

                def values(c):
                    a, g = c % 2, c // 2
                    pe.wait_ge(exp1, 8 * j + c + 1)
                    for n in range(4):
                        at = D * (g % 2) + P * a
                        mm = pe.matmul(ps[32 * n:32 * n + 32, PV + g // 2, at:at + P], v1[:, a, 4 * g + n, :],
                                       prob1[:, c % 4, P * n:P * (n + 1)], start=True, stop=True)
                    mm.then_inc(pv1, 1)

                scores(0)
                for c in range(8):
                    if c < 7:
                        scores(c + 1)
                    values(c)

            def self_project_out(j):
                pe.wait_ge(attn_ready, j + 1)
                pe.wait_ge(mT1_sb, j + 1)
                for a in range(2):
                    for k in range(KT):
                        mm = pe.matmul(ps[:, A0, D * a:D * (a + 1)], attnT[:, k, P * a:P * (a + 1)],
                                       wout_sb[:, k, :], start=(k == 0), stop=(k == KT - 1))
                mm.then_inc(oproj, 1)

            def cross_project(i):
                pe.wait_ge(xn2_ready, i + 1)
                pe.wait_ge(ctx_ld, 16 * (i + 1))
                pe.wait_ge(x1_ready, i + 1)
                pe.wait_ge(exp1, 8 * (i + 1))
                for a in range(2):
                    pe.matmul(ps[:, A0 + a, 0:D], wx_sb[:, 0, :], xn[:, a, :], start=True, stop=True)
                    pe.matmul(ps[:, A0 + a, D:2 * D], wx_sb[:, 1, :], ctx_sb[:, a, :],
                              start=True, stop=True).then_inc(proj2, 1)
                for n in range(4):
                    mm = pe.matmul(ps[:, B0, P * n:P * (n + 1)], ctx_sb[:, n // 2, P * (n % 2):P * (n % 2 + 1)],
                                   wx_sb[:, 2, :], start=True, stop=True)
                mm.then_inc(proj2, 1)

            def cross_max_scores(i, a, chunks):
                for c in chunks:
                    u = 16 * a + c
                    if u < 2:
                        pe.wait_ge(qk2_done, 2 * i + 2)
                    else:
                        pe.wait_ge(max2_done, 32 * i + u - 1)
                    if c == 0:
                        pe.wait_ge(stack2_ld[a], N_STACK2 * (i + 1))
                    for n in range(2):
                        h = 2 * (c % 8) + n
                        mm = pe.matmul(ps[:, A0 + c % 2, D * n:D * (n + 1)],
                                       stack2[a][0][0:A_ROWS, h, P * (c // 8):P * (c // 8 + 1)],
                                       stack2[a][1][0:A_ROWS, h, :], start=True, stop=True)
                    mm.then_inc(sa2, 1)

            def cross_turn_max(i, a):
                pe.wait_ge(mparts2_ready, 2 * i + a + 1)
                if a == 0:
                    pe.wait_ge(o1_sb, i + 1)
                mT = ps[:, (PV, A0)[a], :].bitcast(BF16)
                for t in range(2):
                    mm = pe.transpose(mT[:, P * t:P * (t + 1)], mparts2[:, a, t], id_b[:])
                mm.then_inc(mT2_ps, 1)

            def cross_exp_scores(i, a, g):
                if g == 0:
                    pe.wait_ge(mrow2_ld[a], 16 * (i + 1))
                    if a == 0:
                        pe.wait_ge(v2t_ready, i + 1)
                for h in range(4 * g, 4 * g + 4):
                    u = 16 * a + h
                    if u >= 2:
                        pe.wait_ge(exp2, 32 * i + u - 1)
                    for t in range(2):
                        mm = pe.matmul(ps[:, B0 + h % 2, D * t:D * (t + 1)],
                                       stack2[a][1][0:B_ROWS, h, P * t:P * (t + 1)],
                                       stack2[a][0][0:B_ROWS, h, :], start=True, stop=True)
                    mm.then_inc(sb2, 1)

            def cross_values(i, a, g):
                pe.wait_ge(exp2, 32 * i + 16 * a + 4 * g + 4)
                if g == 0:
                    pe.wait_ge(v2_ready, i + 1)
                    if a == 0:
                        pe.wait_ge(mT2_sb, 2 * i + 1)
                    else:
                        pe.wait_ge(o2_sb, 2 * i + 1)
                for t in range(2):
                    for n in range(4):
                        h = 4 * g + n
                        mm = pe.matmul(ps[32 * n:32 * n + 32, PV + g // 2, D * (g % 2):D * (g % 2 + 1)],
                                       v2[:, 2 * a + t, h, :], prob2[:, h % 8, D * t:D * (t + 1)],
                                       start=(t == 0), stop=(t == 1))
                mm.then_inc(pv2g, 1)

            def experts_prepare(i):
                pe.wait_ge(xn3_ready, i + 1)
                for k in range(KT):
                    for a in range(2):
                        mm = pe.transpose(ps[:, F0, D * k + P * a:D * k + P * (a + 1)],
                                          xn[:, a, P * k:P * (k + 1)], id_f[:])
                mm.then_inc(xT3_ps, 1)
                pe.wait_ge(xT3_sb, i + 1)
                wait(pe, x3_ready, i)
                for a in range(2):
                    for k in range(KT):
                        mm = pe.matmul(ps[:, F1, E * a:E * (a + 1)], xn3T[:, k, P * a:P * (a + 1)], gate_sb[:, k, :],
                                       start=(k == 0), stop=(k == KT - 1))
                mm.then_inc(logits, 1)

            def expert_up(i, n):
                e, u = ORDER[n], 9 * i + n
                if n > 0:
                    pe.wait_ge(u_ready, u)
                for w in range(2):
                    for k in range(KT):
                        mm = pe.matmul(ps[:, F0, D * w:D * (w + 1)], w13_sb[:, e, k, w, :], xn3T[:, k, :],
                                       start=(k == 0), stop=(k == KT - 1))
                mm.then_inc(up, 1)

            def experts_turn_gates(i):
                pe.wait_ge(gates_ready, i + 1)
                for a in range(2):
                    mm = pe.transpose(ps[0:E, F1, P * a:P * (a + 1)], gates[:, a, :], id_f[:])
                mm.then_inc(gT_ps, 1)

            def expert_down(i, n):
                e = ORDER[n]
                pe.wait_ge(h_ready, 9 * i + n + 1)
                if n == 0:
                    pe.wait_ge(gT_sb, i + 1)
                for a in range(2):
                    mm = pe.matmul(ps[:, F1, D * a:D * (a + 1)], hT[:, n % 2, P * a:P * (a + 1)], w2_sb[:, e, :],
                                   start=(n == 0 and a == 0), stop=(n == E), skip_group_check=True)
                mm.then_inc(down, 1)

            def self_stage(j):
                self_project(j)
                self_scores(j)
                self_values(j)
                self_project_out(j)

            def cross_stage(i):
                cross_project(i)
                cross_max_scores(i, 0, range(16))
                cross_max_scores(i, 1, range(4))
                cross_turn_max(i, 0)
                cross_max_scores(i, 1, range(4, 14))
                cross_exp_scores(i, 0, 0)
                cross_max_scores(i, 1, range(14, 16))
                cross_exp_scores(i, 0, 1)
                cross_values(i, 0, 0)
                cross_turn_max(i, 1)
                for g in (1, 2):
                    cross_exp_scores(i, 0, g + 1)
                    cross_values(i, 0, g)
                cross_values(i, 0, 3)
                for g in range(4):
                    cross_exp_scores(i, 1, g)
                    if g:
                        cross_values(i, 1, g - 1)
                cross_values(i, 1, 3)

            def experts_stage(i):
                experts_prepare(i)
                expert_up(i, 0)
                experts_turn_gates(i)
                for n in range(1, E + 1):
                    expert_up(i, n)
                    expert_down(i, n - 1)
                expert_down(i, E)

            pe.wait_ge(ld_first, 16 * FIRST)
            pe.wait_ge(consts, 2)
            pe.wait_ge(fills, 15)
            self_project(0)
            self_scores(0)
            self_values(0)
            pe.wait_ge(ld_rest, 16 * REST)
            self_project_out(0)
            cross_stage(0)
            self_stage(1)
            experts_stage(0)
            with pe.Fori(1, PAIRS - 1) as i:
                cross_stage(i)
                self_stage(i + 1)
                experts_stage(i)
            cross_stage(PAIRS - 1)
            experts_stage(PAIRS - 1)

        @block.scalar
        def _(act):
            def self_stage(j):
                act.wait_ge(xT1_ps, j + 1)
                act.copy(xn1T[:].rearrange("p k s -> p (k s)"), ps[:, B0, :]).then_inc(xT1_sb, 1)
                act.wait_ge(proj1, 5 * j + 5)
                act.copy(v1[:, :, :, 0:HD1], ps[:, PV, :].rearrange("p (a h d) -> p a h d", a=2, h=H)
                         ).then_inc(v1_ready, 1)
                act.wait_ge(rope_done, 2 * j + 2)
                act.copy(parts1[:, 0], qk1[:]).then_inc(high1, 1)
                act.wait_ge(rest1_ready, j + 1)
                act.copy(parts1[:, 1], rest1[:]).then_inc(mid1, 1)
                act.wait_ge(mT1_ps, j + 1)
                act.copy(mT1[:], ps[0:3 * H, A0, :].bitcast(BF16)[:, 0:D]).then_inc(mT1_sb, 1)
                for c in range(8):
                    act.wait_ge(sb1, 8 * j + c + 1)
                    if c >= 4:
                        act.wait_ge(pv1, 8 * j + c - 3)
                    act.activation(prob1[:, c % 4, :], ps[:, B0 + c % 2, :], ACT.Exp,
                                   scale=float(HD1) ** -0.5).then_inc(exp1, 1)
                act.wait_ge(pv1, 8 * (j + 1))
                wait(act, o2_st, 128 * j)
                act.copy(o1[:].rearrange("p g s -> p (g s)"), ps[:, PV:PV + 2, :].rearrange("p b n -> p (b n)")
                         ).then_inc(o1_sb, 1)

            def turn_max(i, a):
                act.wait_ge(mT2_ps, 2 * i + a + 1)
                act.copy(mT2[:, a, :], ps[0:3 * H, (PV, A0)[a], :].bitcast(BF16)[:, 0:D]).then_inc(mT2_sb, 1)

            def exponentials(i, a, heads):
                for h in heads:
                    u = 16 * a + h
                    act.wait_ge(sb2, 32 * i + u + 1)
                    if u < 8:
                        wait(act, pv2g, 8 * i)
                    elif h % 4 == 0:
                        act.wait_ge(pv2g, 8 * i + u // 4 - 1)
                    act.activation(prob2[:, h % 8, :], ps[:, B0 + h % 2, :], ACT.Exp).then_inc(exp2, 1)

            def cross_out(i, a):
                act.wait_ge(pv2g, 8 * i + 4 * a + 4)
                act.wait_ge(o1_st, 64 * (i + 1))
                wait(act, o2_st, 64 * (2 * i + a))
                act.copy(o2[:].rearrange("p g s -> p (g s)"), ps[:, PV:PV + 2, :].rearrange("p b n -> p (b n)")
                         ).then_inc(o2_sb, 1)

            def cross_stage(i):
                act.wait_ge(qk2_done, 2 * i + 2)
                for a in range(2):
                    ins = act.copy(parts2[:, a, 0], qk2[:, a])
                ins.then_inc(high2, 1)
                act.wait_ge(rest2_ready, i + 1)
                for a in range(2):
                    ins = act.copy(parts2[:, a, 1], rest2[:, a])
                ins.then_inc(mid2, 1)
                turn_max(i, 0)
                exponentials(i, 0, range(8))
                turn_max(i, 1)
                exponentials(i, 0, range(8, 16))
                cross_out(i, 0)
                exponentials(i, 1, range(16))
                cross_out(i, 1)

            def experts_stage(i):
                act.wait_ge(xT3_ps, i + 1)
                act.copy(xn3T[:].rearrange("p k s -> p (k s)"), ps[:, F0, :]).then_inc(xT3_sb, 1)
                act.wait_ge(logits, i + 1)
                act.activation(ez[:].rearrange("p a e -> p (a e)"), ps[:, F1, 0:2 * E], ACT.Exp, scale=-1.0
                               ).then_inc(ez_ready, 1)

                def exp_up(n):
                    act.wait_ge(u_ready, 9 * i + n + 1)
                    if n >= 2:
                        act.wait_ge(du_ready, 9 * i + n - 1)
                    act.activation(eu[:, n % 2, :], u13[:, n % 2, 0, :], ACT.Exp, scale=-1.0).then_inc(eu_ready, 1)

                exp_up(0)
                act.wait_ge(gT_ps, i + 1)
                act.copy(gT[:], ps[0:E, F1, 0:D]).then_inc(gT_sb, 1)
                for n in range(1, E + 1):
                    exp_up(n)

            self_stage(0)
            cross_stage(0)
            self_stage(1)
            experts_stage(0)
            with act.Fori(1, PAIRS - 1) as i:
                cross_stage(i)
                self_stage(i + 1)
                experts_stage(i)
            cross_stage(PAIRS - 1)
            experts_stage(PAIRS - 1)

        @block.gpsimd
        def _(pool):
            for n in range(2):
                nc.gpsimd.memset(stack1[n][:], 0.0).then_inc(fills, 1)
            for a in range(2):
                for n in range(2):
                    nc.gpsimd.memset(stack2[a][n][:], 0.0).then_inc(fills, 1)
            nc.gpsimd.memset(v1[:], 1.0).then_inc(fills, 1)
            nc.gpsimd.memset(v2[:], 1.0).then_inc(fills, 1)
            nc.gpsimd.memset(minus_half[:], -0.5).then_inc(fills, 1)
            nc.gpsimd.memset(mparts1[:], 0.0).then_inc(fills, 1)
            nc.gpsimd.memset(mparts2[:], 0.0).then_inc(fills, 1)
            nc.gpsimd.memset(one[:], 1.0).then_inc(fills, 1)
            pool.wait_ge(fills, 12)
            nc.gpsimd.memset(stack1[1][MAX_ROW:P], 1.0).then_inc(fills, 1)
            for a in range(2):
                nc.gpsimd.memset(stack2[a][1][MAX_ROW:P], 1.0).then_inc(fills, 1)

            def inverse_deviation(which, turn):
                pool.wait_ge(var_ready[which], turn + 1)
                nc.gpsimd.tensor_tensor(rstd[:], var_eps[:], minus_half[:], ALU.pow).then_inc(rstd_ready[which], 1)

            def cross_stage(i):
                inverse_deviation(1, i)
                pool.wait_ge(v2t_ready, i + 1)
                pool.wait_ge(mbc_ld, 48 * (i + 1))
                wait(pool, pv2g, 8 * i)
                for n in range(4):
                    keep = m_col[:, n // 2, n % 2:n % 2 + 1].rearrange("p (o u) -> p o u", o=1)
                    ins = nc.gpsimd.tensor_tensor(v2[:, n, :, 0:HD2], v2t[:, n, :].rearrange("p (h d) -> p h d", h=H),
                                                  keep.broadcast_to([P, H, HD2]), ALU.mult)
                ins.then_inc(v2_ready, 1)

            def experts_stage(i):
                inverse_deviation(2, i)
                for n in range(E + 1):
                    u = 9 * i + n
                    pool.wait_ge(u_ready, u + 1)
                    if n >= 2:
                        pool.wait_ge(h_ready, u - 1)
                    nc.gpsimd.tensor_tensor(wu[:, n % 2, :], u13[:, n % 2, 0, :], u13[:, n % 2, 1, :], ALU.mult
                                            ).then_inc(wu_ready, 1)
                    pool.wait_ge(eu_ready, u + 1)
                    nc.gpsimd.tensor_tensor(du[:, n % 2, :], eu[:, n % 2, :], one[:].broadcast_to([P, D]), ALU.add
                                            ).then_inc(du_ready, 1)

            pool.wait_ge(fills, 15)
            inverse_deviation(0, 0)
            cross_stage(0)
            inverse_deviation(0, 1)
            experts_stage(0)
            with pool.Fori(1, PAIRS - 1) as i:
                cross_stage(i)
                inverse_deviation(0, i + 1)
                experts_stage(i)
            cross_stage(PAIRS - 1)
            experts_stage(PAIRS - 1)

        @block.vector
        def _(dve):
            v = nc.vector
            dve.wait_ge(ld_first, 16 * FIRST)
            v.tensor_copy(id_b[:], id_f[:]).then_inc(consts, 1)
            v.tensor_copy(keep_sb[:], keep_f[:].rearrange("p n (o s) -> p n o s", o=1).broadcast_to([P, 2, 4, P])
                          ).then_inc(consts, 1)

            ln = [Chain(dve, s, 2) for s in (ln1_chain, ln2_chain, ln3_chain)]

            def layer_norm(which, turn, src, ready):
                chain = ln[which]
                chain.start(turn)
                for a in range(2):
                    ins = v.bn_stats(stats[:, a, :], src[:, a, :])
                chain.link(ins)
                v.memset(settled[:], 0.0)
                for a in range(2):
                    ins = v.bn_aggr(moments[:, a, :], stats[:, a, :])
                chain.link(ins)
                v.tensor_scalar(var_eps[:], moments[:, :, 1:2], EPS, None, ALU.add).then_inc(var_ready[which], 1)
                dve.wait_ge(rstd_ready[which], turn + 1)
                for a in range(2):
                    ins = v.tensor_scalar(xn[:, a, :], src[:, a, :], moments[:, a, 0:1], rstd[:, a, :],
                                          ALU.subtract, ALU.mult)
                ins.then_inc(ready, 1)
                chain.end()

            mrow = Chain(dve, mrow_chain, 11)

            def mask_rows():
                mrow.start(0)
                dve.wait_ge(mall_ld, 16)
                v.memset(mrow_k[:, 0:3, :], 1.0)
                mrow.link(v.tensor_scalar(m_pen[:], m_all[:], -1.0, 1.0, ALU.mult, ALU.add))
                mrow.link(v.tensor_scalar(m_pen[:], m_pen[:], -NEG, None, ALU.mult))
                for n, src in enumerate((m_pen, m_all)):
                    part = [mrow_q[:, 3 * n + c, :] for c in range(3)]
                    mrow.link(v.tensor_copy(part[0], src[:]))
                    mrow.link(v.tensor_tensor(m_r[:, n, :], src[:], part[0], ALU.subtract))
                    mrow.link(v.tensor_copy(part[1], m_r[:, n, :]))
                    if n == 0:
                        mrow.link(v.tensor_tensor(part[2], m_r[:, n, :], part[1], ALU.subtract))
                v.tensor_tensor(mrow_q[:, 5, :], m_r[:, 1, :], mrow_q[:, 4, :], ALU.subtract).then_inc(mrow_chain, 1)
                mrow.n += 1
                dve.wait_ge(mrow_chain, mrow.n)
                for r in (2, 3):
                    v.tensor_copy(mrow_q[:, 3 * r:3 * r + 3, :], mrow_q[:, 3:6, :])
                for c in range(3):
                    src = mrow_q[:, c:c + 1, :]
                    ins = v.tensor_copy(mrow_k[:, 3 + 3 * c:6 + 3 * c, :], src.broadcast_to([B, 3, D]))
                assert mrow.n == 10
                ins.then_inc(mrow_chain, 1)

            mp1 = Chain(dve, mp1_chain, 3)
            mp2 = Chain(dve, mp2_chain, 3)

            def max_parts(chain, turn, top, rest, parts, ready):
                parts = parts[:, :, 0:3 * H].rearrange("p t (c h) -> p t c h", c=3)
                chain.start(turn)
                chain.link(v.tensor_scalar(parts[:, :, 0, :], top, -1.0, None, ALU.mult))
                chain.link(v.scalar_tensor_tensor(rest, top, -1.0, parts[:, :, 0, :], ALU.mult, ALU.subtract))
                chain.link(v.tensor_copy(parts[:, :, 1, :], rest))
                v.tensor_tensor(parts[:, :, 2, :], rest, parts[:, :, 1, :], ALU.subtract).then_inc(ready, 1)
                chain.end()

            def self_stage(j):
                dve.wait_ge(x_ld, 16 * (j + 1))
                wait(dve, proj2, 3 * j)
                layer_norm(0, j, x_in, xn1_ready)
                wait(dve, pv2g, 8 * j)
                for n in range(2):
                    for m, table in enumerate((cos_sb, sin_sb)):
                        dve.wait_ge(proj1, 5 * j + 2 * n + m + 1)
                        v.tensor_tensor(rope_t[:, n, m, :].rearrange("p (g s) -> p g s", g=4),
                                        ps[:, A0 + 2 * n + m, :].rearrange("p (g s) -> p g s", g=4),
                                        table[:].rearrange("p (o s) -> p o s", o=1).broadcast_to([P, 4, P]), ALU.mult
                                        ).then_inc(rope_read, 1)
                    dve.wait_ge(rope_read, 4 * j + 2 * n + 2)
                    v.tensor_tensor(qk1[:, n, :], rope_t[:, n, 0, :], rope_t[:, n, 1, :], ALU.add
                                    ).then_inc(rope_done, 1)
                dve.wait_ge(high1, j + 1)
                dve.wait_ge(rope_done, 2 * j + 2)
                v.tensor_tensor(rest1[:], qk1[:], parts1[:, 0], ALU.subtract).then_inc(rest1_ready, 1)
                dve.wait_ge(mid1, j + 1)
                dve.wait_ge(rest1_ready, j + 1)
                v.tensor_tensor(parts1[:, 2], rest1[:], parts1[:, 1], ALU.subtract).then_inc(parts1_ready, 1)
                for c in range(8):
                    a, h0 = c // 4, 4 * (c % 4)
                    dve.wait_ge(sa1, 8 * j + c + 1)
                    v.tensor_reduce(max1[:, a, h0:h0 + 4], ps[:, A0 + c % 2, :].rearrange("p (g s) -> p g s", g=4),
                                    AX.X, ALU.max).then_inc(max1_done, 1)
                dve.wait_ge(max1_done, 8 * (j + 1))
                max_parts(mp1, j, max1[:], mrest1[:], mparts1, mparts1_ready)
                dve.wait_ge(o1_ld, 64 * (j + 1))
                v.reciprocal(o1s[:], o1s[:]).then_inc(o1_inverse, 1)
                dve.wait_ge(o1_inverse, j + 1)
                v.tensor_tensor(attnT[:], o1d[:], o1s[:], ALU.mult).then_inc(attn_ready, 1)
                dve.wait_ge(oproj, j + 1)
                v.tensor_tensor(x1[:].rearrange("p a d -> p (a d)"), ps[:, A0, :],
                                x_in[:].rearrange("p a d -> p (a d)"), ALU.add).then_inc(x1_ready, 1)

            x2c = Chain(dve, x2_chain, 3)

            def cross_project(i):
                dve.wait_ge(x1_ready, i + 1)
                dve.wait_ge(xT1_ps, i + 1)
                wait(dve, xT3_ps, i)
                layer_norm(1, i, x1, xn2_ready)
                dve.wait_ge(mbc_ld, 48 * (i + 1))
                v.tensor_scalar(m_bcs[:], m_bc[:], float(HD2) ** -0.5, None, ALU.mult).then_inc(mbcs_ready, 1)
                dve.wait_ge(mbcs_ready, i + 1)
                for a in range(2):
                    dve.wait_ge(proj2, 3 * i + a + 1)
                    v.scalar_tensor_tensor(qk2[:, a, 0, :], ps[:, A0 + a, 0:D], bqk_sb[:, 0:1], m_bcs[:, a, :],
                                           ALU.add, ALU.mult)
                    v.scalar_tensor_tensor(qk2[:, a, 1, :], ps[:, A0 + a, D:2 * D], bqk_sb[:, 1:2], m_bc[:, a, :],
                                           ALU.add, ALU.mult).then_inc(qk2_done, 1)
                dve.wait_ge(proj2, 3 * i + 3)
                wait(dve, v2_ready, i)
                v.tensor_tensor(v2t[:], ps[:, B0, :].rearrange("p (n c) -> p n c", n=4),
                                bv_sb[:].rearrange("p (o c) -> p o c", o=1).broadcast_to([P, 4, P]), ALU.add
                                ).then_inc(v2t_ready, 1)
                dve.wait_ge(high2, i + 1)
                for a in range(2):
                    ins = v.tensor_tensor(rest2[:, a], qk2[:, a], parts2[:, a, 0], ALU.subtract)
                ins.then_inc(rest2_ready, 1)
                dve.wait_ge(mid2, i + 1)
                dve.wait_ge(rest2_ready, i + 1)
                for a in range(2):
                    ins = v.tensor_tensor(parts2[:, a, 2], rest2[:, a], parts2[:, a, 1], ALU.subtract)
                ins.then_inc(parts2_ready, 1)

            def cross_max(i, a):
                for c in range(16):
                    dve.wait_ge(sa2, 32 * i + 16 * a + c + 1)
                    v.tensor_reduce(max2[:, a, c // 8, 2 * (c % 8):2 * (c % 8) + 2],
                                    ps[:, A0 + c % 2, :].rearrange("p (g s) -> p g s", g=2), AX.X, ALU.max
                                    ).then_inc(max2_done, 1)
                dve.wait_ge(max2_done, 32 * i + 16 * a + 16)
                max_parts(mp2, 2 * i + a, max2[:, a], mrest2[:, a], mparts2[:, a], mparts2_ready)

            def cross_out(i, a):
                x2c.start(2 * i + a)
                dve.wait_ge(o2_ld[a], 32 * (i + 1))
                x2c.link(v.reciprocal(o2s[:, a, :], o2s[:, a, :]))
                x2c.link(v.tensor_tensor(o2d[:, a, :], o2d[:, a, :], o2s[:, a, :], ALU.mult))
                x2c.link(v.tensor_tensor(o2d[:, a, :], o2d[:, a, :], m_bc[:, a, :], ALU.mult))
                v.tensor_tensor(x2[:, a, :], x1[:, a, :], o2d[:, a, :], ALU.add).then_inc(x2_ready, 1)
                x2c.end()

            def cross_stage(i):
                cross_project(i)
                cross_max(i, 0)
                cross_max(i, 1)
                cross_out(i, 0)
                cross_out(i, 1)

            route = Chain(dve, route_chain, 7)

            def experts_stage(i, ready1):
                dve.wait_ge(x2_ready, 2 * i + 2)
                dve.wait_ge(proj2, 3 * (i + 1))
                dve.wait_ge(xT1_ps, ready1)
                layer_norm(2, i, x2, xn3_ready)

                def read_up(n):
                    dve.wait_ge(up, 9 * i + n + 1)
                    if n >= 2:
                        dve.wait_ge(eu_ready, 9 * i + n - 1)
                        dve.wait_ge(wu_ready, 9 * i + n - 1)
                    src = ps[:, F0, :].rearrange("p (w t) -> p w t", w=2)
                    if ORDER[n] == E:
                        ins = v.tensor_copy(u13[:, n % 2], src)
                    else:
                        ins = v.tensor_tensor(u13[:, n % 2], src,
                                              g_bc[:, ORDER[n]:ORDER[n] + 1, :].broadcast_to([P, 2, D]), ALU.mult)
                    ins.then_inc(u_ready, 1)

                def hidden(n):
                    dve.wait_ge(du_ready, 9 * i + n + 1)
                    dve.wait_ge(wu_ready, 9 * i + n + 1)
                    if n >= 2:
                        dve.wait_ge(down, 9 * i + n - 1)
                    v.reciprocal(ru[:, n % 2, :], du[:, n % 2, :]).then_inc(ru_ready, 1)
                    dve.wait_ge(ru_ready, 9 * i + n + 1)
                    v.tensor_tensor(hT[:, n % 2, :], wu[:, n % 2, :], ru[:, n % 2, :], ALU.mult).then_inc(h_ready, 1)

                dve.wait_ge(ez_ready, i + 1)
                route.start(i)
                route.link(v.tensor_scalar(den[:], ez[:], 1.0, None, ALU.add))
                route.link(v.reciprocal(score[:], den[:]))
                route.link(v.tensor_tensor(biased[:], score[:],
                                           ebias_sb[:].rearrange("p (o e) -> p o e", o=1).broadcast_to([P, 2, E]),
                                           ALU.add))
                other = biased[:].rearrange("p a (o f) -> p a o f", o=1).broadcast_to([P, 2, E, E])
                own = biased[:].rearrange("p a (e o) -> p a e o", o=1).broadcast_to([P, 2, E, E])
                v.tensor_tensor(above[:], other, own, ALU.is_gt)
                route.link(v.tensor_tensor(equal[:], other, own, ALU.is_equal))
                route.link(v.tensor_tensor(equal[:], equal[:],
                                           lower_sb[:].rearrange("p (o e) f -> p o e f", o=1)
                                           .broadcast_to([P, 2, E, E]), ALU.mult))
                route.link(v.tensor_tensor(above[:], above[:], equal[:], ALU.add))
                route.link(v.tensor_reduce(rank[:], above[:], AX.X, ALU.add))
                v.scalar_tensor_tensor(gates[:], rank[:], 2.0, score[:], ALU.is_lt, ALU.mult
                                       ).then_inc(gates_ready, 1)
                route.end()
                read_up(0)
                dve.wait_ge(g_ld, 16 * (i + 1))
                for n in range(1, E + 1):
                    read_up(n)
                    hidden(n - 1)
                hidden(E)
                dve.wait_ge(down, 9 * (i + 1))
                wait(dve, out_st, 16 * i)
                v.tensor_tensor(x3[:].rearrange("p a d -> p (a d)"), ps[:, F1, :],
                                x2[:].rearrange("p a d -> p (a d)"), ALU.add).then_inc(x3_ready, 1)

            mask_rows()
            dve.wait_ge(fills, 12)
            self_stage(0)
            dve.wait_ge(ld_rest, 16 * REST)
            cross_stage(0)
            self_stage(1)
            experts_stage(0, 2)
            with dve.Fori(1, PAIRS - 1) as i:
                cross_stage(i)
                self_stage(i + 1)
                experts_stage(i, i + 2)
            cross_stage(PAIRS - 1)
            experts_stage(PAIRS - 1, PAIRS)


def _tables():
    inv = 1.0 / 10000.0 ** (np.arange(0, HD1, 2, dtype=np.float32) / HD1)
    angle = np.outer(inv, np.arange(P, dtype=np.float32)).astype(np.float32)
    sign = np.where(np.arange(HD1 // 2) % 2 == 0, -1.0, 1.0)[:, None]
    cos = np.repeat(np.cos(angle), H, axis=0).astype(np.float32)
    sin = np.repeat(np.sin(angle) * sign, H, axis=0).astype(np.float32)
    q, k = np.arange(P)[:, None], np.arange(P)[None, :]
    keep = np.where((q - k >= 0) & (q - k < WINDOW), 0.0, MASKED).astype(np.float32)
    lower = (np.arange(E)[None, :] < np.arange(E)[:, None]).astype(np.float32).reshape(1, E * E)
    return cos, sin, keep, np.ascontiguousarray(keep.T), np.eye(P, dtype=np.float32), lower


def kernel(**inputs):
    import concourse.bacc as _bacc
    from concourse.bass_utils import run_bass_kernel_spmd as _run

    get = {k: np.asarray(v) for k, v in inputs.items()}
    depth, head = np.arange(HD1)[:, None], np.arange(H)[None, :]
    own = (head * HD1 + depth).reshape(-1)
    swapped = (head * HD1 + (depth ^ 1)).reshape(-1)
    wqkv = get["L0_attn_w_qkv"]
    rows = np.concatenate([own, swapped, D + own, D + swapped, 2 * D + np.arange(D)])
    cross = (np.arange(H)[None, :] * HD2 + np.arange(HD2)[:, None]).reshape(-1)
    w1 = np.concatenate([get["L0_ffn_w1"], get["L0_ffn_sw1"][None]])
    w3 = np.concatenate([get["L0_ffn_w3"], get["L0_ffn_sw3"][None]])
    w2 = np.concatenate([get["L0_ffn_w2"], get["L0_ffn_sw2"][None]])
    w13 = np.stack([w1, w3]).reshape(2, E + 1, P, KT, P).transpose(4, 1, 3, 0, 2)
    arrays = {
        "x": get["x"], "ctx": get["ctx_2048"], "mask": get["mask_Bx1x2048_fk1"],
        "wqkv": wqkv[rows].T, "wout": get["L0_attn_w_out"].T,
        "wq": get["L0_xattn_Wq"][cross].T, "wk": get["L0_xattn_Wk"][cross].T, "wv": get["L0_xattn_Wv"].T,
        "bq": get["L0_xattn_bq"][cross][:, None], "bk": get["L0_xattn_bk"][cross][:, None],
        "bv": get["L0_xattn_bv"][None], "ebias": get["L0_ffn_expert_bias"][None],
        "gate": get["L0_ffn_gate_w"].T, "w13": w13, "w2": w2.transpose(2, 0, 1),
    }
    arrays.update(zip(("cos", "sin", "keep_qk", "keep_kq", "ident", "lower"), _tables()))
    nc = _bacc.Bacc("TRN2", target_bir_lowering=False, num_devices=1)
    feed, args = {}, []
    for name, a in arrays.items():
        a = np.ascontiguousarray(a)
        feed[f"in_{name}"] = a
        args.append(nc.dram_tensor(f"in_{name}", a.shape, mybir.dt.from_np(a.dtype), kind="ExternalInput").ap())
    args.append(nc.dram_tensor("out_0", (B, P, D), F32, kind="ExternalOutput").ap())
    decoder(nc, *args)
    r = _run(nc, [feed], core_ids=[0])
    return r.results[0]["out_0"]
```

```python
from contextlib import ExitStack

import concourse.bass as bass
from concourse import mybir
import numpy as np

F32 = mybir.dt.float32
BF16 = mybir.dt.bfloat16
ALU = mybir.AluOpType
ACT = mybir.ActivationFunctionType
AX = mybir.AxisListType

P = 128
B, D = 8, 256
PAIRS = B // 2
H = 16
HD1, HD2 = D // H, P // H
E = 8
KT = D // P
WINDOW = 64
NEG = 1.0e6
MASKED = -1.0e30
EPS = 1e-5

COMBOS = ((0, 1, 2, 0, 1, 0), (0, 0, 0, 1, 1, 2))
MASK_ROW, MASK_ROWS = len(COMBOS[0]) * HD2, 12
MAX_ROW = 96
A_ROWS, B_ROWS = MAX_ROW, MAX_ROW + 3

A0, A1, B0, B1, PV, F0, F1 = 0, 1, 2, 3, 4, 6, 7

ORDER = (E,) + tuple(range(E))


def wait(engine, sem, count):
    if not (isinstance(count, int) and count == 0):
        engine.wait_ge(sem, count)


class Chain:

    def __init__(self, engine, sem, links):
        self.engine, self.sem, self.links = engine, sem, links

    def start(self, turn):
        self.base, self.n = turn * self.links, 0

    def link(self, instruction):
        instruction.then_inc(self.sem, 1)
        self.n += 1
        self.engine.wait_ge(self.sem, self.base + self.n)

    def end(self):
        assert self.n == self.links, self.n


def decoder(nc, x, ctx_in, mask, wqkv, wout, wq, wk, wv, bq, bk, bv, ebias, gate, w13, w2,
            cos, sin, keep_qk, keep_kq, ident, lower, out):
    with ExitStack() as stack:
        def sb(name, shape, dt=F32):
            return stack.enter_context(nc.sbuf_tensor(name, shape, dt))

        def sem(name):
            return stack.enter_context(nc.semaphore(name))

        ps = stack.enter_context(nc.psum_tensor("ps", [P, 8, 512], F32))

        wqkv_sb = sb("wqkv_sb", [P, KT, 5 * D])
        wout_sb = sb("wout_sb", [P, KT, D])
        wx_sb = sb("wx_sb", [P, 3, P])
        bqk_sb = sb("bqk_sb", [P, 2])
        bv_sb = sb("bv_sb", [P, P])
        ebias_sb = sb("ebias_sb", [P, E])
        gate_sb = sb("gate_sb", [P, KT, E])
        w13_sb = sb("w13_sb", [P, E + 1, KT, 2, P])
        w2_sb = sb("w2_sb", [P, E + 1, D])
        cos_sb = sb("cos_sb", [P, P])
        sin_sb = sb("sin_sb", [P, P])
        keep_f = sb("keep_f", [P, 2, P])
        keep_sb = sb("keep_sb", [P, 2, 4, P], BF16)
        id_f = sb("id_f", [P, P])
        id_b = sb("id_b", [P, P], BF16)
        lower_sb = sb("lower_sb", [P, E, E])

        x_in = sb("x_in", [P, 2, D])
        ctx_sb = sb("ctx_sb", [P, 2, D])
        x1 = sb("x1", [P, 2, D])
        x2 = sb("x2", [P, 2, D])
        xn1 = sb("xn1", [P, 2, D])
        xn2 = sb("xn2", [P, 2, D])
        xn3 = xn1
        xn1T = sb("xn1T", [P, KT, D])
        xn3T = xn1T
        stats = sb("stats", [P, 2, 6])
        moments = sb("moments", [P, 2, 2])
        settled = sb("settled", [P, 1])
        var_eps = sb("var_eps", [P, 2, 1])
        one = sb("one", [P, 1])
        minus_half = sb("minus_half", [P, 2, 1])
        rstd = sb("rstd", [P, 2, 1])

        qk1 = sb("qk1", [P, 2, 512])
        parts1 = sb("parts1", [P, 3, 2, 512], BF16)
        stack1 = [sb(f"stack1_{n}", [P, H, D], BF16) for n in "qk"]
        v1 = sb("v1", [P, 2, H, 32])
        max1 = sb("max1", [P, 2, H])
        mrest1 = sb("mrest1", [P, 2, H])
        mparts1 = sb("mparts1", [P, 2, P], BF16)
        mT1 = sb("mT1", [3 * H, D], BF16)
        prob1 = sb("prob1", [P, 2, 512])
        rope_t = prob1
        o1 = sb("o1", [P, 4, D])
        o1d = sb("o1d", [P, KT, D])
        o1s = sb("o1s", [P, KT, D])
        attnT = o1d

        m_bc = sb("m_bc", [P, 2, D])
        m_bcs = sb("m_bcs", [P, 2, D])
        m_col = sb("m_col", [P, 2, 2])
        qk2 = sb("qk2", [P, 2, 2, D])
        parts2 = sb("parts2", [P, 2, 3, 2, D], BF16)
        stack2 = [[sb(f"stack2_{a}{n}", [P, H, D], BF16) for n in "qk"] for a in range(2)]
        v2t = sb("v2t", [P, 4, P])
        v2 = sb("v2", [P, 4, H, 32])
        max2 = sb("max2", [P, 2, 2, H])
        mrest2 = sb("mrest2", [P, 2, 2, H])
        mparts2 = sb("mparts2", [P, 2, 2, P], BF16)
        mT2 = sb("mT2", [3 * H, 2, D], BF16)
        prob2 = sb("prob2", [P, 8, 512])
        o2 = sb("o2", [P, 4, D])
        o2d = sb("o2d", [P, 2, D])
        o2s = sb("o2s", [P, 2, D])

        ez = sb("ez", [P, 2, E])
        den = sb("den", [P, 2, E])
        score = sb("score", [P, 2, E])
        biased = sb("biased", [P, 2, E])
        above = sb("above", [P, 2, E, E])
        equal = sb("equal", [P, 2, E, E])
        rank = sb("rank", [P, 2, E])
        gates = sb("gates", [P, 2, E])
        gT = sb("gT", [E, D])
        g_bc = sb("g_bc", [P, E, D])
        mrow_q = g_bc[0:B, 0:6, :].bitcast(BF16).rearrange("b e (u t) -> b (e u) t", u=2)
        mrow_k = prob2[0:B, 4:7, :].bitcast(BF16).rearrange("b e (u t) -> b (e u) t", u=4)
        u13 = sb("u13", [P, 2, 2, D])
        m_all, m_pen, m_r = u13[0:B, 0, 0], u13[0:B, 0, 1], u13[0:B, 1]
        th = sb("th", [P, 2, D])
        wu = sb("wu", [P, 2, D])
        hT = sb("hT", [P, 2, D])

        d_parts1 = nc.dram_tensor("d_parts1", [3, 2, 2, P, D], BF16).ap()
        d_parts2 = nc.dram_tensor("d_parts2", [2, 3, 2, P, D], BF16).ap()
        d_mT1 = nc.dram_tensor("d_mT1", [3 * H, D], BF16).ap()
        d_mT2 = nc.dram_tensor("d_mT2", [2, 3 * H, D], BF16).ap()
        d_o1 = nc.dram_tensor("d_o1", [H, 32, D], F32).ap()
        d_o2 = nc.dram_tensor("d_o2", [2, H, 16, D], F32).ap()
        d_mrow = nc.dram_tensor("d_mrow", [2, B, MASK_ROWS, D], BF16).ap()
        d_g = nc.dram_tensor("d_g", [E, D], F32).ap()

        ld_first = sem("ld_first")
        ld_rest = sem("ld_rest")
        x_ld = sem("x_ld")
        ctx_ld = sem("ctx_ld")
        mbc_ld = sem("mbc_ld")
        mall_ld = sem("mall_ld")
        fills = sem("fills")
        consts = sem("consts")
        mrow_chain = sem("mrow_chain")
        mrow_st = sem("mrow_st")
        var_ready = [sem(f"var_ready{n}") for n in range(3)]
        rstd_ready = [sem(f"rstd_ready{n}") for n in range(3)]
        ln1_chain = sem("ln1_chain")
        xn1_ready = sem("xn1_ready")
        xT1_ps = sem("xT1_ps")
        xT1_sb = sem("xT1_sb")
        proj1 = sem("proj1")
        rope_read = sem("rope_read")
        rope_done = sem("rope_done")
        v1_ready = sem("v1_ready")
        high1 = sem("high1")
        rest1_ready = sem("rest1_ready")
        mid1 = sem("mid1")
        parts1_ready = sem("parts1_ready")
        parts1_st = sem("parts1_st")
        stack1_ld = sem("stack1_ld")
        sa1 = sem("sa1")
        max1_done = sem("max1_done")
        mp1_chain = sem("mp1_chain")
        mparts1_ready = sem("mparts1_ready")
        mT1_ps = sem("mT1_ps")
        mT1_sb = sem("mT1_sb")
        mT1_st = sem("mT1_st")
        mrow1_ld = sem("mrow1_ld")
        sb1 = sem("sb1")
        exp1 = sem("exp1")
        pv1 = sem("pv1")
        o1_sb = sem("o1_sb")
        o1_st = sem("o1_st")
        o1_ld = sem("o1_ld")
        o1_inverse = sem("o1_inverse")
        attn_ready = sem("attn_ready")
        oproj = sem("oproj")
        x1_ready = sem("x1_ready")
        ln2_chain = sem("ln2_chain")
        xn2_ready = sem("xn2_ready")
        mbcs_ready = sem("mbcs_ready")
        proj2 = sem("proj2")
        q2_done = sem("q2_done")
        qk2_done = sem("qk2_done")
        v2t_ready = sem("v2t_ready")
        v2_ready = sem("v2_ready")
        high2 = sem("high2")
        rest2_ready = sem("rest2_ready")
        mid2 = sem("mid2")
        parts2_ready = sem("parts2_ready")
        parts2_st = sem("parts2_st")
        stack2_ld = [sem(f"stack2_ld{a}") for a in range(2)]
        sa2 = sem("sa2")
        max2_done = sem("max2_done")
        mp2_chain = sem("mp2_chain")
        mparts2_ready = sem("mparts2_ready")
        mT2_ps = sem("mT2_ps")
        mT2_sb = sem("mT2_sb")
        mT2_st = sem("mT2_st")
        mrow2_ld = [sem(f"mrow2_ld{a}") for a in range(2)]
        sb2 = sem("sb2")
        exp2 = sem("exp2")
        pv2g = sem("pv2g")
        o2_sb = sem("o2_sb")
        o2_st = sem("o2_st")
        o2_ld = [sem(f"o2_ld{a}") for a in range(2)]
        x2_chain = sem("x2_chain")
        x2_ready = sem("x2_ready")
        ln3_chain = sem("ln3_chain")
        xn3_ready = sem("xn3_ready")
        xT3_ps = sem("xT3_ps")
        xT3_sb = sem("xT3_sb")
        logits = sem("logits")
        ez_ready = sem("ez_ready")
        route_chain = sem("route_chain")
        gates_ready = sem("gates_ready")
        gT_ps = sem("gT_ps")
        gT_sb = sem("gT_sb")
        gT_st = sem("gT_st")
        g_ld = sem("g_ld")
        up = sem("up")
        u_ready = sem("u_ready")
        th_ready = sem("th_ready")
        wu_ready = sem("wu_ready")
        h_ready = sem("h_ready")
        down = sem("down")
        x3_ready = sem("x3_ready")
        out_st = sem("out_st")

        block = stack.enter_context(nc.Block())

        N_STACK1 = 16 * 2 * len(COMBOS[0])
        N_STACK2 = 16 * (2 * len(COMBOS[0]) + 2)
        FIRST, REST = 6, 12

        @block.sync
        def _(sp):
            def load_x(j):
                sp.dma_start(x_in[:], x[bass.ds(2 * j, 2)].rearrange("a s d -> s a d")).then_inc(x_ld, 16)

            def load_ctx(i):
                sp.dma_start(ctx_sb[:], ctx_in[bass.ds(2 * i, 2)].rearrange("a s d -> s a d")).then_inc(ctx_ld, 16)

            def load_masks(i):
                sp.dma_start(m_bc[:], mask[bass.ds(2 * i, 2)].rearrange("a o t -> o a t").broadcast_to([P, 2, D])
                             ).then_inc(mbc_ld, 16)
                for a in range(2):
                    sp.dma_start(m_col[:, a, :], mask[bass.ds(2 * i + a, 1)].rearrange("a o (k p) -> p (a o k)", p=P),
                                 allow_slow_non_contiguous=True).then_inc(mbc_ld, 16)

            load_x(0)
            sp.dma_start(id_f[:], ident).then_inc(ld_first, 16)
            sp.dma_start(wqkv_sb[:], wqkv.rearrange("(k p) n -> p k n", p=P)).then_inc(ld_first, 16)
            sp.dma_start(cos_sb[:], cos).then_inc(ld_first, 16)
            sp.dma_start(sin_sb[:], sin).then_inc(ld_first, 16)
            sp.dma_start(keep_f[:, 0, :], keep_qk).then_inc(ld_first, 16)
            sp.dma_start(keep_f[:, 1, :], keep_kq).then_inc(ld_first, 16)
            sp.dma_start(m_all[:], mask.rearrange("b o t -> b (o t)")).then_inc(mall_ld, 16)
            sp.dma_start(wout_sb[:], wout.rearrange("(k p) n -> p k n", p=P)).then_inc(ld_rest, 16)
            load_ctx(0)
            load_masks(0)
            for n, w in enumerate((wq, wk, wv)):
                sp.dma_start(wx_sb[:, n, :], w).then_inc(ld_rest, 16)
            sp.dma_start(bqk_sb[:, 0:1], bq).then_inc(ld_rest, 16)
            sp.dma_start(bqk_sb[:, 1:2], bk).then_inc(ld_rest, 16)
            sp.dma_start(bv_sb[:], bv.broadcast_to([P, P])).then_inc(ld_rest, 16)
            sp.dma_start(ebias_sb[:], ebias.broadcast_to([P, E])).then_inc(ld_rest, 16)
            sp.dma_start(gate_sb[:], gate.rearrange("(k p) n -> p k n", p=P)).then_inc(ld_rest, 16)
            sp.dma_start(lower_sb[:].rearrange("p e f -> p (e f)"), lower.broadcast_to([P, E * E])).then_inc(ld_rest, 16)
            sp.dma_start(w13_sb[:], w13).then_inc(ld_rest, 16)
            sp.dma_start(w2_sb[:], w2).then_inc(ld_rest, 16)
            sp.wait_ge(mrow_chain, 11)
            sp.dma_start(d_mrow[0], mrow_q).then_inc(mrow_st, 16)
            sp.dma_start(d_mrow[1], mrow_k).then_inc(mrow_st, 16)

            def self_stacks(j):
                sp.wait_ge(parts1_ready, j + 1)
                sp.dma_start(d_parts1.rearrange("c n t p s -> p (c n t) s"),
                             parts1[:].rearrange("p c n (t s) -> p (c n t) s", t=2)).then_inc(parts1_st, 16)
                sp.wait_ge(parts1_st, 16 * (j + 1))
                for n in range(2):
                    for g, c in enumerate(COMBOS[n]):
                        sp.dma_start(stack1[n][HD1 * g:HD1 * (g + 1)].rearrange("d h s -> d (h s)"),
                                     d_parts1[c, n].rearrange("t (d h) s -> (t d) (h s)", h=H)).then_inc(stack1_ld, 16)

            def self_max(j):
                sp.wait_ge(mT1_sb, j + 1)
                sp.dma_start(d_mT1, mT1[:]).then_inc(mT1_st, 16)
                sp.wait_ge(mT1_st, 16 * (j + 1))
                sp.dma_start(stack1[0][MAX_ROW:B_ROWS].rearrange("c h s -> c (h s)"),
                             d_mT1.rearrange("(c h) s -> c (h s)", h=H)).then_inc(mrow1_ld, 16)

            def self_out(j):
                sp.wait_ge(o1_sb, 2 * j + 2)
                for q in range(4):
                    sp.dma_start(d_o1.rearrange("(g q) r s -> q r g s", q=4)[q],
                                 o1[32 * q:32 * q + 32]).then_inc(o1_st, 16)
                sp.wait_ge(o1_st, 64 * (j + 1))
                for k in range(KT):
                    half = d_o1[8 * k:8 * k + 8]
                    sp.dma_start(o1d[:, k, :], half[:, 0:HD1, :]).then_inc(o1_ld, 16)
                    sp.dma_start(o1s[:, k, :], half[:, HD1:2 * HD1, :]).then_inc(o1_ld, 16)

            def cross_stacks(i):
                sp.wait_ge(parts2_ready, i + 1)
                sp.dma_start(d_parts2[:].rearrange("a c n p t -> p (a c n) t"),
                             parts2[:].rearrange("p a c n t -> p (a c n) t")).then_inc(parts2_st, 16)
                sp.wait_ge(parts2_st, 16 * (i + 1))
                for a in range(2):
                    for n in range(2):
                        for g, c in enumerate(COMBOS[n]):
                            sp.dma_start(stack2[a][n][HD2 * g:HD2 * (g + 1)].rearrange("d h t -> d (h t)"),
                                         d_parts2[a, c, n].rearrange("(d h) t -> d (h t)", h=H)
                                         ).then_inc(stack2_ld[a], 16)

            def cross_mask_rows(i):
                for a in range(2):
                    for n in range(2):
                        rows = d_mrow[n, bass.ds(2 * i + a, 1)].rearrange("a r (o t) -> (a r) o t", o=1)
                        sp.dma_start(stack2[a][n][MASK_ROW:MASK_ROW + MASK_ROWS],
                                     rows.broadcast_to([MASK_ROWS, H, D])).then_inc(stack2_ld[a], 16)

            def cross_max(i, a):
                sp.wait_ge(mT2_sb, 2 * i + a + 1)
                sp.dma_start(d_mT2[a], mT2[:, a, :]).then_inc(mT2_st, 16)
                sp.wait_ge(mT2_st, 16 * (2 * i + a + 1))
                sp.dma_start(stack2[a][0][MAX_ROW:B_ROWS].rearrange("c h t -> c (h t)"),
                             d_mT2[a].rearrange("(c h) t -> c (h t)", h=H)).then_inc(mrow2_ld[a], 16)

            def cross_out(i, a):
                sp.wait_ge(o2_sb, 2 * i + a + 1)
                for q in range(4):
                    sp.dma_start(d_o2[a].rearrange("(g q) r t -> q r g t", q=4)[q],
                                 o2[32 * q:32 * q + 16]).then_inc(o2_st, 16)
                sp.wait_ge(o2_st, 64 * (2 * i + a + 1))
                sp.dma_start(o2d[:, a, :], d_o2[a, :, 0:HD2, :]).then_inc(o2_ld[a], 16)
                sp.dma_start(o2s[:, a, :], d_o2[a, :, HD2:2 * HD2, :]).then_inc(o2_ld[a], 16)

            def body(i, has_self, has_experts):
                if has_self:
                    sp.wait_ge(x1_ready, i + 1)
                    load_x(i + 1)
                wait(sp, exp2, 32 * i)
                cross_mask_rows(i)
                cross_stacks(i)
                if has_self:
                    sp.wait_ge(proj2, 3 * i + 3)
                    load_ctx(i + 1)
                if has_experts:
                    store(i - 1)
                cross_max(i, 0)
                if has_self:
                    self_stacks(i + 1)
                cross_max(i, 1)
                if has_self:
                    self_max(i + 1)
                cross_out(i, 0)
                if has_self:
                    self_out(i + 1)
                cross_out(i, 1)
                if has_self:
                    sp.wait_ge(x2_ready, 2 * i + 2)
                    load_masks(i + 1)

            def store(i):
                sp.wait_ge(x3_ready, i + 1)
                sp.dma_start(out[bass.ds(2 * i, 2)].rearrange("a s d -> s a d"), x2[:]).then_inc(out_st, 16)

            self_stacks(0)
            self_max(0)
            self_out(0)
            sp.wait_ge(mrow_st, 32)
            body(0, True, False)
            with sp.Fori(1, PAIRS - 1) as i:
                body(i, True, True)
            body(PAIRS - 1, False, True)
            store(PAIRS - 1)
            sp.wait_ge(out_st, 16 * PAIRS)

        @block.tensor
        def _(pe):
            def self_turn(j):
                pe.wait_ge(xn1_ready, j + 1)
                for k in range(KT):
                    for a in range(2):
                        mm = pe.transpose(ps[:, F0, D * k + P * a:D * k + P * (a + 1)],
                                          xn1[:, a, P * k:P * (k + 1)], id_f[:])
                mm.then_inc(xT1_ps, 1)

            def self_project(j, n):
                if n < 2:
                    pe.wait_ge(xT1_sb, j + 1)
                else:
                    pe.wait_ge(rope_read, 4 * j + n - 1)
                for t in range(2):
                    for k in range(KT):
                        mm = pe.matmul(ps[:, (F1, F0)[n % 2], D * t:D * (t + 1)],
                                       wqkv_sb[:, k, D * n + P * t:D * n + P * (t + 1)], xn1T[:, k, :],
                                       start=(k == 0), stop=(k == KT - 1))
                mm.then_inc(proj1, 1)

            def self_project_v(j):
                pe.wait_ge(rope_read, 4 * j + 3)
                for a in range(2):
                    for k in range(KT):
                        mm = pe.matmul(ps[:, F1, D * a:D * (a + 1)], xn1T[:, k, P * a:P * (a + 1)],
                                       wqkv_sb[:, k, 4 * D:5 * D], start=(k == 0), stop=(k == KT - 1))
                mm.then_inc(proj1, 1)

            def self_max_scores(j, chunks):
                for c in chunks:
                    a, h0 = c // 4, 4 * (c % 4)
                    if c == 0:
                        pe.wait_ge(stack1_ld, N_STACK1 * (j + 1))
                        pe.wait_ge(rope_read, 4 * j + 4)
                    elif c == 1:
                        pe.wait_ge(v1_ready, j + 1)
                    else:
                        pe.wait_ge(max1_done, 8 * j + c - 1)
                    bank = ps[:, (F0, F1)[c % 2], :]
                    pe.matmul(bank, id_b[:], keep_sb[:, 0].rearrange("p g s -> p (g s)"), start=True, stop=False,
                              skip_group_check=True)
                    for n in range(4):
                        cols = slice(P * a, P * (a + 1))
                        mm = pe.matmul(bank[:, P * n:P * (n + 1)], stack1[0][0:A_ROWS, h0 + n, cols],
                                       stack1[1][0:A_ROWS, h0 + n, cols], start=False, stop=(n == 3),
                                       skip_group_check=True)
                    mm.then_inc(sa1, 1)

            def self_turn_max(j):
                pe.wait_ge(mparts1_ready, j + 1)
                mT = ps[:, F0, :].bitcast(BF16)
                for a in range(2):
                    mm = pe.transpose(mT[:, P * a:P * (a + 1)], mparts1[:, a], id_b[:])
                mm.then_inc(mT1_ps, 1)

            def self_exp_scores(j, c):
                a, h0 = c // 4, 4 * (c % 4)
                if c == 0:
                    pe.wait_ge(mrow1_ld, 16 * (j + 1))
                    pe.wait_ge(mT1_sb, j + 1)
                else:
                    pe.wait_ge(exp1, 8 * j + c)
                bank = ps[:, F0, :]
                pe.matmul(bank, id_b[:], keep_sb[:, 1].rearrange("p g s -> p (g s)"), start=True, stop=False,
                          skip_group_check=True)
                for n in range(4):
                    cols = slice(P * a, P * (a + 1))
                    mm = pe.matmul(bank[:, P * n:P * (n + 1)], stack1[1][0:B_ROWS, h0 + n, cols],
                                   stack1[0][0:B_ROWS, h0 + n, cols], start=False, stop=(n == 3),
                                   skip_group_check=True)
                mm.then_inc(sb1, 1)

            def self_values(j, c):
                a, g = c // 4, c % 4
                pe.wait_ge(exp1, 8 * j + c + 1)
                if c == 4:
                    pe.wait_ge(o1_sb, 2 * j + 1)
                for n in range(4):
                    mm = pe.matmul(ps[32 * n:32 * n + 32, F1, P * g:P * (g + 1)], v1[:, a, 4 * g + n, :],
                                   prob1[:, c % 2, P * n:P * (n + 1)], start=True, stop=True)
                mm.then_inc(pv1, 1)

            def self_project_out(j):
                pe.wait_ge(attn_ready, j + 1)
                for a in range(2):
                    for k in range(KT):
                        mm = pe.matmul(ps[:, F0, D * a:D * (a + 1)], attnT[:, k, P * a:P * (a + 1)],
                                       wout_sb[:, k, :], start=(k == 0), stop=(k == KT - 1))
                mm.then_inc(oproj, 1)

            def cross_project(i):
                pe.wait_ge(xn2_ready, i + 1)
                pe.wait_ge(ctx_ld, 16 * (i + 1))
                wait(pe, mT2_sb, 2 * i)
                wait(pe, exp2, 32 * i)
                for a in range(2):
                    pe.matmul(ps[:, A0 + a, 0:D], wx_sb[:, 0, :], xn2[:, a, :], start=True, stop=True)
                    pe.matmul(ps[:, A0 + a, D:2 * D], wx_sb[:, 1, :], ctx_sb[:, a, :],
                              start=True, stop=True).then_inc(proj2, 1)
                for n in range(4):
                    mm = pe.matmul(ps[:, B0, P * n:P * (n + 1)], ctx_sb[:, n // 2, P * (n % 2):P * (n % 2 + 1)],
                                   wx_sb[:, 2, :], start=True, stop=True)
                mm.then_inc(proj2, 1)

            def cross_max_scores(i, a, chunks):
                for c in chunks:
                    u = 16 * a + c
                    if u < 2:
                        pe.wait_ge(qk2_done, 2 * i + 2)
                    else:
                        pe.wait_ge(max2_done, 32 * i + u - 1)
                    if c == 0:
                        pe.wait_ge(stack2_ld[a], N_STACK2 * (i + 1))
                    for n in range(2):
                        h = 2 * (c % 8) + n
                        mm = pe.matmul(ps[:, A0 + c % 2, D * n:D * (n + 1)],
                                       stack2[a][0][0:A_ROWS, h, P * (c // 8):P * (c // 8 + 1)],
                                       stack2[a][1][0:A_ROWS, h, :], start=True, stop=True)
                    mm.then_inc(sa2, 1)

            def cross_turn_max(i, a):
                pe.wait_ge(mparts2_ready, 2 * i + a + 1)
                if a == 0:
                    wait(pe, o2_sb, 2 * i)
                mT = ps[:, (PV, A0)[a], :].bitcast(BF16)
                for t in range(2):
                    mm = pe.transpose(mT[:, P * t:P * (t + 1)], mparts2[:, a, t], id_b[:])
                mm.then_inc(mT2_ps, 1)

            def cross_exp_scores(i, a, g):
                if g == 0:
                    pe.wait_ge(mrow2_ld[a], 16 * (i + 1))
                    if a == 0:
                        pe.wait_ge(v2t_ready, i + 1)
                for h in range(4 * g, 4 * g + 4):
                    u = 16 * a + h
                    if u >= 2:
                        pe.wait_ge(exp2, 32 * i + u - 1)
                    for t in range(2):
                        mm = pe.matmul(ps[:, B0 + h % 2, D * t:D * (t + 1)],
                                       stack2[a][1][0:B_ROWS, h, P * t:P * (t + 1)],
                                       stack2[a][0][0:B_ROWS, h, :], start=True, stop=True)
                    mm.then_inc(sb2, 1)

            def cross_values(i, a, g):
                pe.wait_ge(exp2, 32 * i + 16 * a + 4 * g + 4)
                if g == 0:
                    pe.wait_ge(v2_ready, i + 1)
                    if a == 0:
                        pe.wait_ge(mT2_sb, 2 * i + 1)
                    else:
                        pe.wait_ge(o2_sb, 2 * i + 1)
                for t in range(2):
                    for n in range(4):
                        h = 4 * g + n
                        mm = pe.matmul(ps[32 * n:32 * n + 32, PV + g // 2, D * (g % 2):D * (g % 2 + 1)],
                                       v2[:, 2 * a + t, h, :], prob2[:, h % 8, D * t:D * (t + 1)],
                                       start=(t == 0), stop=(t == 1))
                mm.then_inc(pv2g, 1)

            def experts_prepare(i):
                pe.wait_ge(xn3_ready, i + 1)
                for k in range(KT):
                    for a in range(2):
                        mm = pe.transpose(ps[:, F0, D * k + P * a:D * k + P * (a + 1)],
                                          xn3[:, a, P * k:P * (k + 1)], id_f[:])
                mm.then_inc(xT3_ps, 1)
                pe.wait_ge(xT3_sb, i + 1)
                for a in range(2):
                    for k in range(KT):
                        mm = pe.matmul(ps[:, F1, E * a:E * (a + 1)], xn3T[:, k, P * a:P * (a + 1)], gate_sb[:, k, :],
                                       start=(k == 0), stop=(k == KT - 1))
                mm.then_inc(logits, 1)

            def expert_up(i, n):
                e, u = ORDER[n], 9 * i + n
                if n > 0:
                    pe.wait_ge(u_ready, u)
                for w in range(2):
                    for k in range(KT):
                        mm = pe.matmul(ps[:, F0, D * w:D * (w + 1)], w13_sb[:, e, k, w, :], xn3T[:, k, :],
                                       start=(k == 0), stop=(k == KT - 1))
                mm.then_inc(up, 1)

            def experts_turn_gates(i):
                pe.wait_ge(gates_ready, i + 1)
                for a in range(2):
                    mm = pe.transpose(ps[0:E, F1, P * a:P * (a + 1)], gates[:, a, :], id_f[:])
                mm.then_inc(gT_ps, 1)

            def expert_down(i, n):
                e = ORDER[n]
                pe.wait_ge(h_ready, 9 * i + n + 1)
                if n == 0:
                    pe.wait_ge(gT_sb, i + 1)
                for a in range(2):
                    mm = pe.matmul(ps[:, F1, D * a:D * (a + 1)], hT[:, n % 2, P * a:P * (a + 1)], w2_sb[:, e, :],
                                   start=(n == 0 and a == 0), stop=(n == E), skip_group_check=True)
                mm.then_inc(down, 1)

            def experts_first(i):
                experts_prepare(i)
                expert_up(i, 0)
                experts_turn_gates(i)

            def experts_rest(i):
                for n in range(1, E + 1):
                    expert_up(i, n)
                    expert_down(i, n - 1)
                expert_down(i, E)

            def body(i, has_self, has_experts):
                j = i + 1
                cross_project(i)
                if has_experts:
                    pe.wait_ge(x1_ready, i + 1)
                    experts_first(i - 1)
                    experts_rest(i - 1)
                    pe.wait_ge(x3_ready, i)
                if has_self:
                    if not has_experts:
                        pe.wait_ge(x1_ready, j)
                    self_turn(j)
                for step in range(5):
                    cross_max_scores(i, 0, range(3 * step, 3 * step + 3))
                    if has_self:
                        if step < 4:
                            self_project(j, step)
                        else:
                            self_project_v(j)
                cross_max_scores(i, 0, range(15, 16))
                cross_max_scores(i, 1, range(4))
                cross_turn_max(i, 0)
                cross_max_scores(i, 1, range(4, 14))
                cross_exp_scores(i, 0, 0)
                cross_max_scores(i, 1, range(14, 16))
                cross_exp_scores(i, 0, 1)
                cross_values(i, 0, 0)
                cross_turn_max(i, 1)
                for g in (1, 2):
                    if has_self:
                        self_max_scores(j, range(4 * (g - 1), 4 * g))
                    cross_exp_scores(i, 0, g + 1)
                    cross_values(i, 0, g)
                cross_values(i, 0, 3)
                cross_exp_scores(i, 1, 0)
                if has_self:
                    self_turn_max(j)
                cross_exp_scores(i, 1, 1)
                cross_values(i, 1, 0)
                cross_exp_scores(i, 1, 2)
                cross_values(i, 1, 1)
                if has_self:
                    self_exp_scores(j, 0)
                cross_exp_scores(i, 1, 3)
                cross_values(i, 1, 2)
                if has_self:
                    self_exp_scores(j, 1)
                    self_values(j, 0)
                cross_values(i, 1, 3)
                if has_self:
                    for c in range(2, 8):
                        self_exp_scores(j, c)
                        self_values(j, c - 1)
                    self_values(j, 7)
                    self_project_out(j)

            pe.wait_ge(ld_first, 16 * FIRST)
            pe.wait_ge(consts, 2)
            pe.wait_ge(fills, 15)
            self_turn(0)
            for n in range(4):
                self_project(0, n)
            self_project_v(0)
            self_max_scores(0, range(8))
            self_turn_max(0)
            self_exp_scores(0, 0)
            for c in range(1, 8):
                self_exp_scores(0, c)
                self_values(0, c - 1)
            self_values(0, 7)
            pe.wait_ge(ld_rest, 16 * REST)
            self_project_out(0)
            body(0, True, False)
            with pe.Fori(1, PAIRS - 1) as i:
                body(i, True, True)
            body(PAIRS - 1, False, True)
            experts_first(PAIRS - 1)
            experts_rest(PAIRS - 1)

        @block.scalar
        def _(act):
            def self_split(j):
                act.wait_ge(xT1_ps, j + 1)
                act.copy(xn1T[:].rearrange("p k s -> p (k s)"), ps[:, F0, :]).then_inc(xT1_sb, 1)
                act.wait_ge(proj1, 5 * j + 5)
                act.copy(v1[:, :, :, 0:HD1], ps[:, F1, :].rearrange("p (a h d) -> p a h d", a=2, h=H)
                         ).then_inc(v1_ready, 1)
                act.wait_ge(rope_done, 2 * j + 2)
                act.copy(parts1[:, 0], qk1[:]).then_inc(high1, 1)
                act.wait_ge(rest1_ready, j + 1)
                act.copy(parts1[:, 1], qk1[:]).then_inc(mid1, 1)

            def self_turn_max(j):
                act.wait_ge(mT1_ps, j + 1)
                act.copy(mT1[:], ps[0:3 * H, F0, :].bitcast(BF16)[:, 0:D]).then_inc(mT1_sb, 1)

            def self_exponential(j, c):
                act.wait_ge(sb1, 8 * j + c + 1)
                if c >= 2:
                    act.wait_ge(pv1, 8 * j + c - 1)
                act.activation(prob1[:, c % 2, :], ps[:, F0, :], ACT.Exp,
                               scale=float(HD1) ** -0.5).then_inc(exp1, 1)

            def self_out(j, a):
                act.wait_ge(pv1, 8 * j + 4 * a + 4)
                wait(act, o1_st, 64 * j)
                act.copy(o1[:, :, P * a:P * (a + 1)], ps[:, F1, :].rearrange("p (g s) -> p g s", g=4)
                         ).then_inc(o1_sb, 1)

            def turn_max(i, a):
                act.wait_ge(mT2_ps, 2 * i + a + 1)
                act.copy(mT2[:, a, :], ps[0:3 * H, (PV, A0)[a], :].bitcast(BF16)[:, 0:D]).then_inc(mT2_sb, 1)

            def exponentials(i, a, heads):
                for h in heads:
                    u = 16 * a + h
                    act.wait_ge(sb2, 32 * i + u + 1)
                    if u < 8:
                        wait(act, pv2g, 8 * i)
                    elif h % 4 == 0:
                        act.wait_ge(pv2g, 8 * i + u // 4 - 1)
                    act.activation(prob2[:, h % 8, :], ps[:, B0 + h % 2, :], ACT.Exp).then_inc(exp2, 1)

            def cross_out(i, a):
                act.wait_ge(pv2g, 8 * i + 4 * a + 4)
                wait(act, o2_st, 64 * (2 * i + a))
                act.copy(o2[:].rearrange("p g s -> p (g s)"), ps[:, PV:PV + 2, :].rearrange("p b n -> p (b n)")
                         ).then_inc(o2_sb, 1)

            def cross_high(i):
                act.wait_ge(qk2_done, 2 * i + 2)
                for a in range(2):
                    ins = act.copy(parts2[:, a, 0], qk2[:, a])
                ins.then_inc(high2, 1)

            def cross_mid(i):
                act.wait_ge(rest2_ready, i + 1)
                for a in range(2):
                    ins = act.copy(parts2[:, a, 1], qk2[:, a])
                ins.then_inc(mid2, 1)

            def experts_tokens(i):
                act.wait_ge(xT3_ps, i + 1)
                act.copy(xn3T[:].rearrange("p k s -> p (k s)"), ps[:, F0, :]).then_inc(xT3_sb, 1)

            def experts_logits(i):
                act.wait_ge(logits, i + 1)
                act.activation(ez[:].rearrange("p a e -> p (a e)"), ps[:, F1, 0:2 * E], ACT.Exp, scale=-1.0
                               ).then_inc(ez_ready, 1)

            def tanh_up(i, n):
                act.wait_ge(u_ready, 9 * i + n + 1)
                if n >= 2:
                    act.wait_ge(h_ready, 9 * i + n - 1)
                act.activation(th[:, n % 2, :], u13[:, n % 2, 0, :], ACT.Tanh, scale=0.5).then_inc(th_ready, 1)

            def experts_gates(i):
                act.wait_ge(gT_ps, i + 1)
                act.copy(gT[:], ps[0:E, F1, 0:D]).then_inc(gT_sb, 1)
                act.wait_ge(gT_sb, i + 1)
                act.dma_start(d_g, gT[:]).then_inc(gT_st, 16)
                tanh_up(i, 0)
                act.wait_ge(gT_st, 16 * (i + 1))
                act.dma_start(g_bc[:].rearrange("p e t -> p (e t)"),
                              d_g.rearrange("(o e) t -> o (e t)", o=1).broadcast_to([P, E * D])).then_inc(g_ld, 16)

            def body(i, has_self, has_experts):
                j, f = i + 1, i - 1
                if has_experts:
                    experts_tokens(f)
                cross_high(i)
                if has_experts:
                    experts_logits(f)
                cross_mid(i)
                if has_experts:
                    experts_gates(f)
                    for n in range(1, E + 1):
                        tanh_up(f, n)
                if has_self:
                    self_split(j)
                turn_max(i, 0)
                exponentials(i, 0, range(8))
                turn_max(i, 1)
                exponentials(i, 0, range(8, 16))
                cross_out(i, 0)
                exponentials(i, 1, range(4))
                if has_self:
                    self_turn_max(j)
                exponentials(i, 1, range(4, 12))
                if has_self:
                    self_exponential(j, 0)
                exponentials(i, 1, range(12, 16))
                if has_self:
                    self_exponential(j, 1)
                cross_out(i, 1)
                if has_self:
                    self_exponential(j, 2)
                    self_exponential(j, 3)
                    self_out(j, 0)
                    for c in range(4, 8):
                        self_exponential(j, c)
                    self_out(j, 1)

            self_split(0)
            self_turn_max(0)
            for c in range(8):
                self_exponential(0, c)
                if c % 4 == 3:
                    self_out(0, c // 4)
            body(0, True, False)
            with act.Fori(1, PAIRS - 1) as i:
                body(i, True, True)
            body(PAIRS - 1, False, True)
            experts_tokens(PAIRS - 1)
            experts_logits(PAIRS - 1)
            experts_gates(PAIRS - 1)
            for n in range(1, E + 1):
                tanh_up(PAIRS - 1, n)

        @block.gpsimd
        def _(pool):
            for n in range(2):
                nc.gpsimd.memset(stack1[n][:], 0.0).then_inc(fills, 1)
            for a in range(2):
                for n in range(2):
                    nc.gpsimd.memset(stack2[a][n][:], 0.0).then_inc(fills, 1)
            nc.gpsimd.memset(v1[:], 1.0).then_inc(fills, 1)
            nc.gpsimd.memset(v2[:], 1.0).then_inc(fills, 1)
            nc.gpsimd.memset(minus_half[:], -0.5).then_inc(fills, 1)
            nc.gpsimd.memset(mparts1[:], 0.0).then_inc(fills, 1)
            nc.gpsimd.memset(mparts2[:], 0.0).then_inc(fills, 1)
            nc.gpsimd.memset(one[:], 1.0).then_inc(fills, 1)
            pool.wait_ge(fills, 12)
            nc.gpsimd.memset(stack1[1][MAX_ROW:P], 1.0).then_inc(fills, 1)
            for a in range(2):
                nc.gpsimd.memset(stack2[a][1][MAX_ROW:P], 1.0).then_inc(fills, 1)

            def inverse_deviation(which, turn):
                pool.wait_ge(var_ready[which], turn + 1)
                nc.gpsimd.tensor_tensor(rstd[:], var_eps[:], minus_half[:], ALU.pow).then_inc(rstd_ready[which], 1)

            def cross_mask_values(i):
                pool.wait_ge(v2t_ready, i + 1)
                pool.wait_ge(mbc_ld, 48 * (i + 1))
                wait(pool, pv2g, 8 * i)
                for n in range(4):
                    keep = m_col[:, n // 2, n % 2:n % 2 + 1].rearrange("p (o u) -> p o u", o=1)
                    ins = nc.gpsimd.tensor_tensor(v2[:, n, :, 0:HD2], v2t[:, n, :].rearrange("p (h d) -> p h d", h=H),
                                                  keep.broadcast_to([P, H, HD2]), ALU.mult)
                ins.then_inc(v2_ready, 1)

            def experts_products(i, meanwhile=None):
                for n in range(E + 1):
                    u = 9 * i + n
                    pool.wait_ge(u_ready, u + 1)
                    if n >= 2:
                        pool.wait_ge(h_ready, u - 1)
                    nc.gpsimd.tensor_tensor(wu[:, n % 2, :], u13[:, n % 2, 0, :], u13[:, n % 2, 1, :], ALU.mult
                                            ).then_inc(wu_ready, 1)
                    if n == 4 and meanwhile is not None:
                        inverse_deviation(0, meanwhile)

            def body(i, has_self, has_experts):
                inverse_deviation(1, i)
                if has_experts:
                    inverse_deviation(2, i - 1)
                cross_mask_values(i)
                if has_experts:
                    experts_products(i - 1, meanwhile=i + 1 if has_self else None)
                elif has_self:
                    inverse_deviation(0, i + 1)

            pool.wait_ge(fills, 15)
            inverse_deviation(0, 0)
            body(0, True, False)
            with pool.Fori(1, PAIRS - 1) as i:
                body(i, True, True)
            body(PAIRS - 1, False, True)
            inverse_deviation(2, PAIRS - 1)
            experts_products(PAIRS - 1)

        @block.vector
        def _(dve):
            v = nc.vector
            dve.wait_ge(ld_first, 16 * FIRST)
            v.tensor_copy(id_b[:], id_f[:]).then_inc(consts, 1)
            v.tensor_copy(keep_sb[:], keep_f[:].rearrange("p n (o s) -> p n o s", o=1).broadcast_to([P, 2, 4, P])
                          ).then_inc(consts, 1)

            ln = [Chain(dve, s, 2) for s in (ln1_chain, ln2_chain, ln3_chain)]

            def layer_norm(which, turn, src, xn, ready):
                chain = ln[which]
                chain.start(turn)
                for a in range(2):
                    ins = v.bn_stats(stats[:, a, :], src[:, a, :])
                chain.link(ins)
                v.memset(settled[:], 0.0)
                for a in range(2):
                    ins = v.bn_aggr(moments[:, a, :], stats[:, a, :])
                chain.link(ins)
                v.tensor_scalar(var_eps[:], moments[:, :, 1:2], EPS, None, ALU.add).then_inc(var_ready[which], 1)
                dve.wait_ge(rstd_ready[which], turn + 1)
                for a in range(2):
                    ins = v.tensor_scalar(xn[:, a, :], src[:, a, :], moments[:, a, 0:1], rstd[:, a, :],
                                          ALU.subtract, ALU.mult)
                ins.then_inc(ready, 1)
                chain.end()

            mrow = Chain(dve, mrow_chain, 11)

            def mask_rows():
                mrow.start(0)
                dve.wait_ge(mall_ld, 16)
                v.memset(mrow_k[:, 0:3, :], 1.0)
                mrow.link(v.tensor_scalar(m_pen[:], m_all[:], -1.0, 1.0, ALU.mult, ALU.add))
                mrow.link(v.tensor_scalar(m_pen[:], m_pen[:], -NEG, None, ALU.mult))
                for n, src in enumerate((m_pen, m_all)):
                    part = [mrow_q[:, 3 * n + c, :] for c in range(3)]
                    mrow.link(v.tensor_copy(part[0], src[:]))
                    mrow.link(v.tensor_tensor(m_r[:, n, :], src[:], part[0], ALU.subtract))
                    mrow.link(v.tensor_copy(part[1], m_r[:, n, :]))
                    if n == 0:
                        mrow.link(v.tensor_tensor(part[2], m_r[:, n, :], part[1], ALU.subtract))
                v.tensor_tensor(mrow_q[:, 5, :], m_r[:, 1, :], mrow_q[:, 4, :], ALU.subtract).then_inc(mrow_chain, 1)
                mrow.n += 1
                dve.wait_ge(mrow_chain, mrow.n)
                for r in (2, 3):
                    v.tensor_copy(mrow_q[:, 3 * r:3 * r + 3, :], mrow_q[:, 3:6, :])
                for c in range(3):
                    src = mrow_q[:, c:c + 1, :]
                    ins = v.tensor_copy(mrow_k[:, 3 + 3 * c:6 + 3 * c, :], src.broadcast_to([B, 3, D]))
                assert mrow.n == 10
                ins.then_inc(mrow_chain, 1)

            mp1 = Chain(dve, mp1_chain, 3)
            mp2 = Chain(dve, mp2_chain, 3)

            def max_parts(chain, turn, top, rest, parts, ready):
                parts = parts[:, :, 0:3 * H].rearrange("p t (c h) -> p t c h", c=3)
                chain.start(turn)
                chain.link(v.tensor_scalar(parts[:, :, 0, :], top, -1.0, None, ALU.mult))
                chain.link(v.scalar_tensor_tensor(rest, top, -1.0, parts[:, :, 0, :], ALU.mult, ALU.subtract))
                chain.link(v.tensor_copy(parts[:, :, 1, :], rest))
                v.tensor_tensor(parts[:, :, 2, :], rest, parts[:, :, 1, :], ALU.subtract).then_inc(ready, 1)
                chain.end()

            def self_norm(j):
                dve.wait_ge(x_ld, 16 * (j + 1))
                wait(dve, xT1_ps, j)
                layer_norm(0, j, x_in, xn1, xn1_ready)

            def self_rope(j, n):
                for m, table in enumerate((cos_sb, sin_sb)):
                    dve.wait_ge(proj1, 5 * j + 2 * n + m + 1)
                    if m == 0 and (n or not isinstance(j, int) or j):
                        dve.wait_ge(rope_done, 2 * j + n)
                    v.tensor_tensor(rope_t[:, m, :].rearrange("p (g s) -> p g s", g=4),
                                    ps[:, (F1, F0)[m], :].rearrange("p (g s) -> p g s", g=4),
                                    table[:].rearrange("p (o s) -> p o s", o=1).broadcast_to([P, 4, P]), ALU.mult
                                    ).then_inc(rope_read, 1)
                dve.wait_ge(rope_read, 4 * j + 2 * n + 2)
                v.tensor_tensor(qk1[:, n, :], rope_t[:, 0, :], rope_t[:, 1, :], ALU.add).then_inc(rope_done, 1)

            def self_rest(j):
                dve.wait_ge(high1, j + 1)
                dve.wait_ge(rope_done, 2 * j + 2)
                v.tensor_tensor(qk1[:], qk1[:], parts1[:, 0], ALU.subtract).then_inc(rest1_ready, 1)

            def self_low(j):
                dve.wait_ge(mid1, j + 1)
                dve.wait_ge(rest1_ready, j + 1)
                v.tensor_tensor(parts1[:, 2], qk1[:], parts1[:, 1], ALU.subtract).then_inc(parts1_ready, 1)

            def self_max(j):
                for c in range(8):
                    a, h0 = c // 4, 4 * (c % 4)
                    dve.wait_ge(sa1, 8 * j + c + 1)
                    v.tensor_reduce(max1[:, a, h0:h0 + 4], ps[:, (F0, F1)[c % 2], :].rearrange("p (g s) -> p g s", g=4),
                                    AX.X, ALU.max).then_inc(max1_done, 1)
                dve.wait_ge(max1_done, 8 * (j + 1))
                max_parts(mp1, j, max1[:], mrest1[:], mparts1, mparts1_ready)

            def self_normalise(j):
                dve.wait_ge(o1_ld, 64 * (j + 1))
                v.reciprocal(o1s[:], o1s[:]).then_inc(o1_inverse, 1)
                dve.wait_ge(o1_inverse, j + 1)
                v.tensor_tensor(attnT[:], o1d[:], o1s[:], ALU.mult).then_inc(attn_ready, 1)

            def self_residual(j):
                dve.wait_ge(oproj, j + 1)
                wait(dve, x2_ready, 2 * j)
                v.tensor_tensor(x1[:].rearrange("p a d -> p (a d)"), ps[:, F0, :],
                                x_in[:].rearrange("p a d -> p (a d)"), ALU.add).then_inc(x1_ready, 1)

            x2c = Chain(dve, x2_chain, 3)

            def cross_norm(i):
                dve.wait_ge(x1_ready, i + 1)
                wait(dve, proj2, 3 * i)
                layer_norm(1, i, x1, xn2, xn2_ready)
                dve.wait_ge(mbc_ld, 48 * (i + 1))
                v.tensor_scalar(m_bcs[:], m_bc[:], float(HD2) ** -0.5, None, ALU.mult).then_inc(mbcs_ready, 1)

            def cross_bias(i):
                dve.wait_ge(mbcs_ready, i + 1)
                for a in range(2):
                    dve.wait_ge(proj2, 3 * i + a + 1)
                    v.scalar_tensor_tensor(qk2[:, a, 0, :], ps[:, A0 + a, 0:D], bqk_sb[:, 0:1], m_bcs[:, a, :],
                                           ALU.add, ALU.mult)
                    v.scalar_tensor_tensor(qk2[:, a, 1, :], ps[:, A0 + a, D:2 * D], bqk_sb[:, 1:2], m_bc[:, a, :],
                                           ALU.add, ALU.mult).then_inc(qk2_done, 1)
                dve.wait_ge(proj2, 3 * i + 3)
                wait(dve, v2_ready, i)
                v.tensor_tensor(v2t[:], ps[:, B0, :].rearrange("p (n c) -> p n c", n=4),
                                bv_sb[:].rearrange("p (o c) -> p o c", o=1).broadcast_to([P, 4, P]), ALU.add
                                ).then_inc(v2t_ready, 1)

            def cross_rest(i):
                dve.wait_ge(high2, i + 1)
                for a in range(2):
                    ins = v.tensor_tensor(qk2[:, a], qk2[:, a], parts2[:, a, 0], ALU.subtract)
                ins.then_inc(rest2_ready, 1)

            def cross_low(i):
                dve.wait_ge(mid2, i + 1)
                dve.wait_ge(rest2_ready, i + 1)
                for a in range(2):
                    ins = v.tensor_tensor(parts2[:, a, 2], qk2[:, a], parts2[:, a, 1], ALU.subtract)
                ins.then_inc(parts2_ready, 1)

            def cross_max_parts(i, a):
                dve.wait_ge(max2_done, 32 * i + 16 * a + 16)
                max_parts(mp2, 2 * i + a, max2[:, a], mrest2[:, a], mparts2[:, a], mparts2_ready)

            def cross_max(i, a, chunks):
                for c in chunks:
                    dve.wait_ge(sa2, 32 * i + 16 * a + c + 1)
                    v.tensor_reduce(max2[:, a, c // 8, 2 * (c % 8):2 * (c % 8) + 2],
                                    ps[:, A0 + c % 2, :].rearrange("p (g s) -> p g s", g=2), AX.X, ALU.max
                                    ).then_inc(max2_done, 1)

            def cross_out(i, a):
                x2c.start(2 * i + a)
                dve.wait_ge(o2_ld[a], 32 * (i + 1))
                x2c.link(v.reciprocal(o2s[:, a, :], o2s[:, a, :]))
                x2c.link(v.tensor_tensor(o2d[:, a, :], o2d[:, a, :], o2s[:, a, :], ALU.mult))
                x2c.link(v.tensor_tensor(o2d[:, a, :], o2d[:, a, :], m_bc[:, a, :], ALU.mult))
                wait(dve, out_st, 16 * i)
                v.tensor_tensor(x2[:, a, :], x1[:, a, :], o2d[:, a, :], ALU.add).then_inc(x2_ready, 1)
                x2c.end()

            route = Chain(dve, route_chain, 7)

            def experts_norm(i):
                dve.wait_ge(x2_ready, 2 * i + 2)
                layer_norm(2, i, x2, xn3, xn3_ready)

            def read_up(i, n):
                dve.wait_ge(up, 9 * i + n + 1)
                if n >= 2:
                    dve.wait_ge(th_ready, 9 * i + n - 1)
                    dve.wait_ge(wu_ready, 9 * i + n - 1)
                src = ps[:, F0, :].rearrange("p (w t) -> p w t", w=2)
                if ORDER[n] == E:
                    ins = v.tensor_copy(u13[:, n % 2], src)
                else:
                    ins = v.tensor_tensor(u13[:, n % 2], src,
                                          g_bc[:, ORDER[n]:ORDER[n] + 1, :].broadcast_to([P, 2, D]), ALU.mult)
                ins.then_inc(u_ready, 1)

            def hidden(i, n):
                dve.wait_ge(th_ready, 9 * i + n + 1)
                dve.wait_ge(wu_ready, 9 * i + n + 1)
                if n >= 2:
                    dve.wait_ge(down, 9 * i + n - 1)
                v.scalar_tensor_tensor(hT[:, n % 2, :], th[:, n % 2, :], 1.0, wu[:, n % 2, :], ALU.add, ALU.mult
                                       ).then_inc(h_ready, 1)

            def experts_route(i):
                dve.wait_ge(ez_ready, i + 1)
                route.start(i)
                route.link(v.tensor_scalar(den[:], ez[:], 1.0, None, ALU.add))
                route.link(v.reciprocal(score[:], den[:]))
                route.link(v.tensor_tensor(biased[:], score[:],
                                           ebias_sb[:].rearrange("p (o e) -> p o e", o=1).broadcast_to([P, 2, E]),
                                           ALU.add))
                other = biased[:].rearrange("p a (o f) -> p a o f", o=1).broadcast_to([P, 2, E, E])
                own = biased[:].rearrange("p a (e o) -> p a e o", o=1).broadcast_to([P, 2, E, E])
                v.tensor_tensor(above[:], other, own, ALU.is_gt)
                route.link(v.tensor_tensor(equal[:], other, own, ALU.is_equal))
                route.link(v.tensor_tensor(equal[:], equal[:],
                                           lower_sb[:].rearrange("p (o e) f -> p o e f", o=1)
                                           .broadcast_to([P, 2, E, E]), ALU.mult))
                route.link(v.tensor_tensor(above[:], above[:], equal[:], ALU.add))
                route.link(v.tensor_reduce(rank[:], above[:], AX.X, ALU.add))
                v.scalar_tensor_tensor(gates[:], rank[:], 2.0, score[:], ALU.is_lt, ALU.mult
                                       ).then_inc(gates_ready, 1)
                route.end()

            def experts_hidden(i, meanwhile=None):
                read_up(i, 0)
                dve.wait_ge(g_ld, 16 * (i + 1))
                for n in range(1, E + 1):
                    read_up(i, n)
                    hidden(i, n - 1)
                    if n == 4 and meanwhile is not None:
                        self_norm(meanwhile)
                hidden(i, E)
                dve.wait_ge(down, 9 * (i + 1))
                v.scalar_tensor_tensor(x2[:].rearrange("p a d -> p (a d)"), ps[:, F1, :], 0.5,
                                       x2[:].rearrange("p a d -> p (a d)"), ALU.mult, ALU.add).then_inc(x3_ready, 1)

            def body(i, has_self, has_experts):
                j = i + 1
                cross_norm(i)
                if has_experts:
                    experts_norm(i - 1)
                cross_bias(i)
                if has_experts:
                    experts_route(i - 1)
                cross_rest(i)
                cross_low(i)
                if has_experts:
                    experts_hidden(i - 1, meanwhile=j if has_self else None)
                elif has_self:
                    self_norm(j)
                cross_max(i, 0, range(6))
                if has_self:
                    self_rope(j, 0)
                cross_max(i, 0, range(6, 12))
                if has_self:
                    self_rope(j, 1)
                cross_max(i, 0, range(12, 16))
                if has_self:
                    self_rest(j)
                cross_max_parts(i, 0)
                if has_self:
                    self_low(j)
                cross_max(i, 1, range(16))
                cross_max_parts(i, 1)
                if has_self:
                    self_max(j)
                cross_out(i, 0)
                if has_self:
                    self_normalise(j)
                cross_out(i, 1)
                if has_self:
                    self_residual(j)

            mask_rows()
            dve.wait_ge(fills, 12)
            self_norm(0)
            self_rope(0, 0)
            self_rope(0, 1)
            self_rest(0)
            self_low(0)
            self_max(0)
            self_normalise(0)
            self_residual(0)
            dve.wait_ge(ld_rest, 16 * REST)
            body(0, True, False)
            with dve.Fori(1, PAIRS - 1) as i:
                body(i, True, True)
            body(PAIRS - 1, False, True)
            experts_norm(PAIRS - 1)
            experts_route(PAIRS - 1)
            experts_hidden(PAIRS - 1)


def _tables():
    inv = 1.0 / 10000.0 ** (np.arange(0, HD1, 2, dtype=np.float32) / HD1)
    angle = np.outer(inv, np.arange(P, dtype=np.float32)).astype(np.float32)
    sign = np.where(np.arange(HD1 // 2) % 2 == 0, -1.0, 1.0)[:, None]
    cos = np.repeat(np.cos(angle), H, axis=0).astype(np.float32)
    sin = np.repeat(np.sin(angle) * sign, H, axis=0).astype(np.float32)
    q, k = np.arange(P)[:, None], np.arange(P)[None, :]
    keep = np.where((q - k >= 0) & (q - k < WINDOW), 0.0, MASKED).astype(np.float32)
    lower = (np.arange(E)[None, :] < np.arange(E)[:, None]).astype(np.float32).reshape(1, E * E)
    return cos, sin, keep, np.ascontiguousarray(keep.T), np.eye(P, dtype=np.float32), lower


def kernel(**inputs):
    import concourse.bacc as _bacc
    from concourse.bass_utils import run_bass_kernel_spmd as _run

    get = {k: np.asarray(v) for k, v in inputs.items()}
    depth, head = np.arange(HD1)[:, None], np.arange(H)[None, :]
    own = (head * HD1 + depth).reshape(-1)
    swapped = (head * HD1 + (depth ^ 1)).reshape(-1)
    wqkv = get["L0_attn_w_qkv"]
    rows = np.concatenate([own, swapped, D + own, D + swapped, 2 * D + np.arange(D)])
    cross = (np.arange(H)[None, :] * HD2 + np.arange(HD2)[:, None]).reshape(-1)
    w1 = np.concatenate([get["L0_ffn_w1"], get["L0_ffn_sw1"][None]])
    w3 = np.concatenate([get["L0_ffn_w3"], get["L0_ffn_sw3"][None]])
    w2 = np.concatenate([get["L0_ffn_w2"], get["L0_ffn_sw2"][None]])
    w13 = np.stack([w1, w3]).reshape(2, E + 1, P, KT, P).transpose(4, 1, 3, 0, 2)
    arrays = {
        "x": get["x"], "ctx": get["ctx_2048"], "mask": get["mask_Bx1x2048_fk1"],
        "wqkv": wqkv[rows].T, "wout": get["L0_attn_w_out"].T,
        "wq": get["L0_xattn_Wq"][cross].T, "wk": get["L0_xattn_Wk"][cross].T, "wv": get["L0_xattn_Wv"].T,
        "bq": get["L0_xattn_bq"][cross][:, None], "bk": get["L0_xattn_bk"][cross][:, None],
        "bv": get["L0_xattn_bv"][None], "ebias": get["L0_ffn_expert_bias"][None],
        "gate": get["L0_ffn_gate_w"].T, "w13": w13, "w2": w2.transpose(2, 0, 1),
    }
    arrays.update(zip(("cos", "sin", "keep_qk", "keep_kq", "ident", "lower"), _tables()))
    nc = _bacc.Bacc("TRN2", target_bir_lowering=False, num_devices=1)
    feed, args = {}, []
    for name, a in arrays.items():
        a = np.ascontiguousarray(a)
        feed[f"in_{name}"] = a
        args.append(nc.dram_tensor(f"in_{name}", a.shape, mybir.dt.from_np(a.dtype), kind="ExternalInput").ap())
    args.append(nc.dram_tensor("out_0", (B, P, D), F32, kind="ExternalOutput").ap())
    decoder(nc, *args)
    r = _run(nc, [feed], core_ids=[0])
    return r.results[0]["out_0"]
```

```python
from contextlib import ExitStack

import concourse.bass as bass
from concourse import mybir
import numpy as np

F32 = mybir.dt.float32
BF16 = mybir.dt.bfloat16
ALU = mybir.AluOpType
ACT = mybir.ActivationFunctionType
AX = mybir.AxisListType

P = 128
B, D = 8, 256
PAIRS = B // 2
H = 16
HD1, HD2 = D // H, P // H
E = 8
KT = D // P
WINDOW = 64
NEG = 1.0e6
MASKED = -1.0e30
EPS = 1e-5

SLOTS = 6
HOLDS = ((slice(0, 3), slice(3, 5)),
         (slice(1, 6, 2), slice(2, 5, 2)))
LOW = (5, 0)
UPPER = (slice(0, 5), slice(1, 6))
MASK_ROW, MASK_ROWS = SLOTS * HD2, 12
MAX_ROW = 96
A_ROWS, B_ROWS = MAX_ROW, MAX_ROW + 3

A0, A1, B0, B1, PV, F0, F1 = 0, 1, 2, 3, 4, 6, 7

BOTH, FIRST, SECOND = slice(0, 2), slice(0, 1), slice(1, 2)
TURN0, TURN1 = PAIRS - 1, PAIRS


def columns(batches):
    return slice(P * batches.start, P * batches.stop)


class Banks:

    def __init__(self, up, gates, down):
        self.up, self.gates, self.down = up, gates, down


def banks_of(batches):
    if batches == FIRST:
        return Banks((A0, A1), B0, F1)
    if batches == SECOND:
        return Banks((B1, PV), PV + 1, F0)
    return Banks((PV, B1), PV + 1, F1)


SELF_BANKS = (F0, A1, B0, B1)
A_BANKS = ((A0, A1, B0, B1), (A0, A1))

NORM_AT = 5
SECOND_AT = 2

ORDER = (E,) + tuple(range(E))


def wait(engine, sem, count):
    if not (isinstance(count, int) and count == 0):
        engine.wait_ge(sem, count)


class Chain:

    def __init__(self, engine, sem, links):
        self.engine, self.sem, self.links = engine, sem, links

    def start(self, turn):
        self.base, self.n = turn * self.links, 0

    def link(self, instruction):
        instruction.then_inc(self.sem, 1)
        self.n += 1
        self.engine.wait_ge(self.sem, self.base + self.n)

    def end(self):
        assert self.n == self.links, self.n


def decoder(nc, x, ctx_in, mask, wqkv, wout, wq, wk, wv, bq, bk, bv, ebias, gate, w13, w2,
            cos, sin, keep_qk, keep_kq, ident, lower, out):
    with ExitStack() as stack:
        def sb(name, shape, dt=F32):
            return stack.enter_context(nc.sbuf_tensor(name, shape, dt))

        def sem(name):
            return stack.enter_context(nc.semaphore(name))

        ps = stack.enter_context(nc.psum_tensor("ps", [P, 8, 512], F32))

        wqkv_sb = sb("wqkv_sb", [P, KT, 3 * D])
        wout_sb = sb("wout_sb", [P, KT, D])
        wx_sb = sb("wx_sb", [P, 3, P])
        bqk_sb = sb("bqk_sb", [P, 2])
        bv_sb = sb("bv_sb", [P, P])
        ebias_sb = sb("ebias_sb", [P, E])
        gate_sb = sb("gate_sb", [P, KT, E])
        w13_sb = sb("w13_sb", [P, E + 1, KT, 2, P])
        w2_sb = sb("w2_sb", [P, E + 1, D])
        cos_sb = sb("cos_sb", [P, P])
        sin_sb = sb("sin_sb", [P, P])
        keep_f = sb("keep_f", [P, 2, P])
        keep_sb = sb("keep_sb", [P, 2, 4, P], BF16)
        id_f = sb("id_f", [P, P])
        id_b = sb("id_b", [P, P], BF16)
        lower_sb = sb("lower_sb", [P, E, E])

        x_in = sb("x_in", [P, 2, D])
        ctx_sb = sb("ctx_sb", [P, 2, D])
        x1 = sb("x1", [P, 2, D])
        x2 = sb("x2", [P, 2, D])
        xn1 = sb("xn1", [P, 2, D])
        xn2 = sb("xn2", [P, 2, D])
        xn3 = xn1
        xn1T = sb("xn1T", [P, KT, D])
        xn3T = xn1T
        stats = sb("stats", [P, 2, 6])
        moments = sb("moments", [P, 2, 2])
        settled = sb("settled", [P, 1])
        var_eps = sb("var_eps", [P, 2, 1])
        minus_half = sb("minus_half", [P, 2, 1])
        rstd = sb("rstd", [P, 2, 1])

        qk1 = sb("qk1", [P, 2, 512])
        parts1 = sb("parts1", [P, 3, 2, 512], BF16)
        stack1 = [sb(f"stack1_{n}", [P, H, D], BF16) for n in "qk"]
        v1 = sb("v1", [P, 2, H, 32])
        max1 = sb("max1", [P, 2, H])
        mrest1 = sb("mrest1", [P, 2, H])
        mparts1 = sb("mparts1", [P, 2, P], BF16)
        mT1 = sb("mT1", [3 * H, D], BF16)
        swapped = sb("swapped", [P, 2, 512])
        o1 = sb("o1", [P, 4, D])
        o1d = sb("o1d", [P, KT, D])
        o1s = sb("o1s", [P, KT, D])
        attnT = o1d

        m_bc = sb("m_bc", [P, 2, D])
        m_bcs = sb("m_bcs", [P, 2, D])
        m_col = sb("m_col", [P, 2, 2])
        qk2 = sb("qk2", [P, 2, 2, D])
        parts2 = sb("parts2", [P, 3, 2, 2, D], BF16)
        stack2 = [[sb(f"stack2_{a}{n}", [P, H, D], BF16) for n in "qk"] for a in range(2)]
        v2t = sb("v2t", [P, 4, P])
        v2 = sb("v2", [P, 4, H, 32])
        max2 = sb("max2", [P, 2, 2, H])
        mrest2 = sb("mrest2", [P, 2, 2, H])
        mparts2 = sb("mparts2", [P, 2, 2, P], BF16)
        mT2 = sb("mT2", [3 * H, 2, D], BF16)
        prob = sb("prob", [P, 8, 512])
        o2 = sb("o2", [P, 4, D])
        o2d = sb("o2d", [P, 2, D])
        o2s = sb("o2s", [P, 2, D])

        ez = sb("ez", [P, 2, E])
        den = sb("den", [P, 2, E])
        score = sb("score", [P, 2, E])
        biased = sb("biased", [P, 2, E])
        above = sb("above", [P, 2, E, E])
        equal = sb("equal", [P, 2, E, E])
        rank = sb("rank", [P, 2, E])
        gates = sb("gates", [P, 2, E])
        g_bc = sb("g_bc", [P, E, D])
        mrow_q = g_bc[0:B, 0:6, :].bitcast(BF16).rearrange("b e (u t) -> b (e u) t", u=2)
        mrow_k = prob[0:B, 4:7, :].bitcast(BF16).rearrange("b e (u t) -> b (e u) t", u=4)
        u13 = sb("u13", [P, 2, 2, D])
        m_all, m_pen, m_r = u13[0:B, 0, 0], u13[0:B, 0, 1], u13[0:B, 1]
        tanh_u = sb("tanh_u", [P, 2, D])
        u_times_u3 = sb("u_times_u3", [P, 2, D])
        hT = sb("hT", [P, 2, D])

        d_stack1 = nc.dram_tensor("d_stack1", [2, SLOTS, P, 2, D], BF16).ap()
        d_stack2 = nc.dram_tensor("d_stack2", [2, SLOTS, P, 2, D], BF16).ap()
        d_o1 = nc.dram_tensor("d_o1", [H, 32, D], F32).ap()
        d_o2 = nc.dram_tensor("d_o2", [2, H, 32, D], F32).ap()
        d_mrow = nc.dram_tensor("d_mrow", [2, B, MASK_ROWS, D], BF16).ap()

        ld_ident = sem("ld_ident")
        ld_qkv = [sem(f"ld_qkv{n}") for n in range(3)]
        ld_tables = sem("ld_tables")
        ld_keep = sem("ld_keep")
        ld_rest = sem("ld_rest")
        x_ld = sem("x_ld")
        ctx_ld = sem("ctx_ld")
        mbc_ld = sem("mbc_ld")
        mall_ld = sem("mall_ld")
        small_fills = sem("small_fills")
        fills1 = sem("fills1")
        fills2 = sem("fills2")
        consts = sem("consts")
        mrow_chain = sem("mrow_chain")
        mrow_st = sem("mrow_st")
        var_ready = [sem(f"var_ready{n}") for n in range(3)]
        rstd_ready = [sem(f"rstd_ready{n}") for n in range(3)]
        ln1_chain = sem("ln1_chain")
        xn1_ready = sem("xn1_ready")
        xT1_ps = sem("xT1_ps")
        xT1_sb = sem("xT1_sb")
        proj1 = sem("proj1")
        rope_read = sem("rope_read")
        sin_done = sem("sin_done")
        rope_done = sem("rope_done")
        v1_ready = sem("v1_ready")
        high1 = sem("high1")
        rest1_ready = sem("rest1_ready")
        mid1 = sem("mid1")
        parts1_ready = sem("parts1_ready")
        parts1_st = sem("parts1_st")
        stack1_ld = sem("stack1_ld")
        scores_a1 = sem("scores_a1")
        max1_done = sem("max1_done")
        mp1_chain = sem("mp1_chain")
        mparts1_ready = sem("mparts1_ready")
        mT1_ps = sem("mT1_ps")
        mT1_sb = sem("mT1_sb")
        mrow1_ld = sem("mrow1_ld")
        scores_b1 = sem("scores_b1")
        exp1 = sem("exp1")
        values1 = sem("values1")
        o1_sb = sem("o1_sb")
        o1_st = [sem(f"o1_st{a}") for a in range(2)]
        o1_ld = [sem(f"o1_ld{a}") for a in range(2)]
        o1_inverse = sem("o1_inverse")
        attn_ready = sem("attn_ready")
        oproj = sem("oproj")
        x1_ready = sem("x1_ready")
        ln2_chain = sem("ln2_chain")
        xn2_ready = sem("xn2_ready")
        mbcs_ready = sem("mbcs_ready")
        ctx_proj = sem("ctx_proj")
        q2_proj = sem("q2_proj")
        qk2_done = sem("qk2_done")
        v2t_ready = sem("v2t_ready")
        v2_ready = sem("v2_ready")
        high2 = sem("high2")
        rest2_ready = sem("rest2_ready")
        mid2 = sem("mid2")
        parts2_ready = sem("parts2_ready")
        parts2_st = sem("parts2_st")
        stack2_ld = [sem(f"stack2_ld{a}") for a in range(2)]
        scores_a2 = sem("scores_a2")
        max2_done = sem("max2_done")
        mp2_chain = sem("mp2_chain")
        mparts2_ready = sem("mparts2_ready")
        mT2_ps = sem("mT2_ps")
        mT2_sb = sem("mT2_sb")
        mrow2_ld = [sem(f"mrow2_ld{a}") for a in range(2)]
        scores_b2 = sem("scores_b2")
        exp2 = sem("exp2")
        values2 = sem("values2")
        o2_sb = sem("o2_sb")
        o2_st = sem("o2_st")
        o2_ld = [sem(f"o2_ld{a}") for a in range(2)]
        x2_based = sem("x2_based")
        x2_chain = sem("x2_chain")
        x2_ready = sem("x2_ready")
        ln3_chain = sem("ln3_chain")
        xn3_ready = sem("xn3_ready")
        xT3_ps = sem("xT3_ps")
        xT3_sb = sem("xT3_sb")
        logits = sem("logits")
        ez_ready = sem("ez_ready")
        route_chain = sem("route_chain")
        gates_ready = sem("gates_ready")
        g_ps = sem("g_ps")
        g_sb = sem("g_sb")
        up = sem("up")
        u_ready = sem("u_ready")
        th_ready = sem("th_ready")
        wu_ready = sem("wu_ready")
        h_ready = sem("h_ready")
        down = sem("down")
        x3_ready = sem("x3_ready")
        out_st = sem("out_st")

        block = stack.enter_context(nc.Block())

        N_STACK1, N_STACK2 = 16 * 8, 16 * 6
        REST = 12

        def self_parts(engine, isa, j):
            engine.wait_ge(high1, j + 1)
            engine.wait_ge(rope_done, 2 * j + 2)
            isa.tensor_tensor(qk1[:], qk1[:], parts1[:, 0], ALU.subtract).then_inc(rest1_ready, 1)
            engine.wait_ge(mid1, j + 1)
            engine.wait_ge(rest1_ready, j + 1)
            isa.tensor_tensor(parts1[:, 2], qk1[:], parts1[:, 1], ALU.subtract).then_inc(parts1_ready, 1)

        @block.sync
        def _(sp):
            def load_x(j):
                sp.dma_start(x_in[:], x[bass.ds(2 * j, 2)].rearrange("a s d -> s a d")).then_inc(x_ld, 16)

            def load_ctx(i):
                sp.dma_start(ctx_sb[:], ctx_in[bass.ds(2 * i, 2)].rearrange("a s d -> s a d")).then_inc(ctx_ld, 16)

            def load_masks(i):
                sp.dma_start(m_bc[:], mask[bass.ds(2 * i, 2)].rearrange("a o t -> o a t").broadcast_to([P, 2, D])
                             ).then_inc(mbc_ld, 16)
                for a in range(2):
                    sp.dma_start(m_col[:, a, :], mask[bass.ds(2 * i + a, 1)].rearrange("a o (k p) -> p (a o k)", p=P),
                                 allow_slow_non_contiguous=True).then_inc(mbc_ld, 16)

            def self_part(j, c):
                sp.wait_ge((high1, mid1)[c], j + 1)
                for n in range(2):
                    slots = HOLDS[n][c]
                    k = len(range(*slots.indices(SLOTS)))
                    sp.dma_start(d_stack1[n, slots].rearrange("c p t s -> p c (t s)"),
                                 parts1[:, c, n:n + 1, :].broadcast_to([P, k, 2 * D])).then_inc(parts1_st, 16)

            def self_stacks(j):
                sp.wait_ge(parts1_ready, j + 1)
                for n in range(2):
                    for t in range(2):
                        row = MAX_ROW // 2 * t + HD2 * LOW[n]
                        sp.dma_start(stack1[n][row:row + HD2], parts1[:, 2, n, D * t:D * (t + 1)]
                                     ).then_inc(stack1_ld, 16)
                sp.wait_ge(parts1_st, 64 * (j + 1))
                for n in range(2):
                    for t in range(2):
                        row = MAX_ROW // 2 * t
                        sp.dma_start(stack1[n][row + HD2 * UPPER[n].start:row + HD2 * UPPER[n].stop],
                                     d_stack1[n, UPPER[n], :, t].rearrange("c (d h) s -> (c d) h s", h=H)
                                     ).then_inc(stack1_ld, 16)

            def self_max(j):
                sp.wait_ge(mT1_sb, j + 1)
                sp.dma_start(stack1[0][MAX_ROW:B_ROWS], mT1[:]).then_inc(mrow1_ld, 16)

            def self_out_store(j, a):
                sp.wait_ge(o1_sb, 2 * j + a + 1)
                sp.dma_start(d_o1[:, :, P * a:P * (a + 1)].rearrange("(g q) r s -> (q r) g s", q=4),
                             o1[:, :, P * a:P * (a + 1)]).then_inc(o1_st[a], 16)

            def self_out_load(j, a):
                cols = slice(P * a, P * (a + 1))
                sp.wait_ge(o1_st[a], 16 * (j + 1))
                for k in range(KT):
                    half = d_o1[8 * k:8 * k + 8, :, cols]
                    sp.dma_start(o1d[:, k, cols], half[:, 0:HD1, :]).then_inc(o1_ld[a], 16)
                    sp.dma_start(o1s[:, k, cols], half[:, HD1:2 * HD1, :]).then_inc(o1_ld[a], 16)

            def self_out(j):
                for a in range(2):
                    self_out_store(j, a)
                for a in range(2):
                    self_out_load(j, a)

            def cross_stacks(i):
                for c, done in enumerate((high2, mid2)):
                    sp.wait_ge(done, i + 1)
                    for n in range(2):
                        slots = HOLDS[n][c]
                        k = len(range(*slots.indices(SLOTS)))
                        sp.dma_start(d_stack2[n, slots].rearrange("c p a t -> p c (a t)"),
                                     parts2[:, c, n:n + 1].rearrange("p n a t -> p n (a t)")
                                     .broadcast_to([P, k, 2 * D])).then_inc(parts2_st, 16)
                sp.wait_ge(parts2_ready, i + 1)
                for a in range(2):
                    for n in range(2):
                        sp.dma_start(stack2[a][n][HD2 * LOW[n]:HD2 * (LOW[n] + 1)], parts2[:, 2, n, a, :]
                                     ).then_inc(stack2_ld[a], 16)
                sp.wait_ge(parts2_st, 64 * (i + 1))
                for a in range(2):
                    for n in range(2):
                        sp.dma_start(stack2[a][n][HD2 * UPPER[n].start:HD2 * UPPER[n].stop],
                                     d_stack2[n, UPPER[n], :, a].rearrange("c (d h) t -> (c d) h t", h=H)
                                     ).then_inc(stack2_ld[a], 16)

            def cross_mask_rows(i):
                for a in range(2):
                    for n in range(2):
                        rows = d_mrow[n, bass.ds(2 * i + a, 1)].rearrange("a r (o t) -> (a r) o t", o=1)
                        sp.dma_start(stack2[a][n][MASK_ROW:MASK_ROW + MASK_ROWS],
                                     rows.broadcast_to([MASK_ROWS, H, D])).then_inc(stack2_ld[a], 16)

            def cross_max(i, a):
                sp.wait_ge(mT2_sb, 2 * i + a + 1)
                sp.dma_start(stack2[a][0][MAX_ROW:B_ROWS], mT2[:, a, :]).then_inc(mrow2_ld[a], 16)

            def cross_out(i, a):
                sp.wait_ge(o2_sb, 2 * i + a + 1)
                sp.dma_start(d_o2[a].rearrange("(g q) r t -> (q r) g t", q=4), o2[:]).then_inc(o2_st, 16)
                sp.wait_ge(o2_st, 16 * (2 * i + a + 1))
                sp.dma_start(o2d[:, a, :], d_o2[a, :, 0:HD2, :]).then_inc(o2_ld[a], 16)
                sp.dma_start(o2s[:, a, :], d_o2[a, :, HD2:2 * HD2, :]).then_inc(o2_ld[a], 16)

            def body(i, has_self, has_experts):
                if has_self:
                    sp.wait_ge(x1_ready, i + 1)
                    load_x(i + 1)
                wait(sp, exp2, 32 * i)
                cross_mask_rows(i)
                cross_stacks(i)
                if has_self:
                    sp.wait_ge(ctx_proj, i + 1)
                    load_ctx(i + 1)
                if has_experts:
                    store(i - 1)
                if has_self:
                    self_part(i + 1, 0)
                cross_max(i, 0)
                if has_self:
                    self_part(i + 1, 1)
                    self_stacks(i + 1)
                cross_max(i, 1)
                cross_out(i, 0)
                if has_self:
                    self_max(i + 1)
                cross_out(i, 1)
                if has_self:
                    self_out(i + 1)
                if has_self:
                    sp.wait_ge(x2_ready, 2 * i + 2)
                    load_masks(i + 1)

            def store(i):
                sp.wait_ge(x3_ready, i + 1)
                sp.dma_start(out[bass.ds(2 * i, 2)].rearrange("a s d -> s a d"), x2[:]).then_inc(out_st, 16)

            def store_batch(turn, a):
                sp.wait_ge(x3_ready, turn + 1)
                sp.dma_start(out[2 * (PAIRS - 1) + a], x2[:, a, :]).then_inc(out_st, 16)

            load_x(0)
            sp.dma_start(id_f[:], ident).then_inc(ld_ident, 16)
            for n in range(3):
                cols = slice(D * n, D * (n + 1))
                sp.dma_start(wqkv_sb[:, :, cols], wqkv[:, cols].rearrange("(k p) n -> p k n", p=P)
                             ).then_inc(ld_qkv[n], 16)
            sp.dma_start(w13_sb[:], w13).then_inc(ld_rest, 16)
            sp.dma_start(w2_sb[:], w2).then_inc(ld_rest, 16)
            for c in range(2):
                self_part(0, c)
            self_stacks(0)
            sp.dma_start(wout_sb[:], wout.rearrange("(k p) n -> p k n", p=P)).then_inc(ld_rest, 16)
            load_ctx(0)
            load_masks(0)
            sp.wait_ge(mrow_chain, 11)
            sp.dma_start(d_mrow[0], mrow_q).then_inc(mrow_st, 16)
            sp.dma_start(d_mrow[1], mrow_k).then_inc(mrow_st, 16)
            self_max(0)
            self_out(0)
            sp.wait_ge(mrow_st, 32)
            sp.wait_ge(fills2, 8)
            body(0, True, False)
            with sp.Fori(1, PAIRS - 1) as i:
                body(i, True, True)
            body(PAIRS - 1, False, True)
            store_batch(TURN0, 0)
            store_batch(TURN1, 1)
            sp.wait_ge(out_st, 16 * (PAIRS + 1))

        @block.tensor
        def _(pe):
            def self_turn(j):
                pe.wait_ge(xn1_ready, j + 1)
                wait(pe, x1_ready, j)
                for k in range(KT):
                    for a in range(2):
                        mm = pe.transpose(ps[:, F0, D * k + P * a:D * k + P * (a + 1)],
                                          xn1[:, a, P * k:P * (k + 1)], id_f[:])
                mm.then_inc(xT1_ps, 1)

            def self_project(j, n):
                pe.wait_ge(xT1_sb, j + 1)
                if isinstance(j, int) and j == 0:
                    pe.wait_ge(ld_qkv[n], 16)
                for t in range(2):
                    for k in range(KT):
                        mm = pe.matmul(ps[:, (F1, F0)[n], D * t:D * (t + 1)],
                                       wqkv_sb[:, k, D * n + P * t:D * n + P * (t + 1)], xn1T[:, k, :],
                                       start=(k == 0), stop=(k == KT - 1))
                mm.then_inc(proj1, 1)

            def self_project_v(j):
                pe.wait_ge(rope_read, 2 * j + 1)
                if isinstance(j, int) and j == 0:
                    pe.wait_ge(ld_qkv[2], 16)
                for a in range(2):
                    for k in range(KT):
                        mm = pe.matmul(ps[:, F1, D * a:D * (a + 1)], xn1T[:, k, P * a:P * (a + 1)],
                                       wqkv_sb[:, k, 2 * D:3 * D], start=(k == 0), stop=(k == KT - 1))
                mm.then_inc(proj1, 1)

            def self_max_scores(j, chunks):
                for c in chunks:
                    a, h0 = c // 4, 4 * (c % 4)
                    if c == 0:
                        pe.wait_ge(stack1_ld, N_STACK1 * (j + 1))
                        pe.wait_ge(rope_read, 2 * j + 2)
                    elif c == 1:
                        pe.wait_ge(v1_ready, j + 1)
                    else:
                        pe.wait_ge(max1_done, 8 * j + c - 1)
                    bank = ps[:, (F0, F1)[c % 2], :]
                    pe.matmul(bank, id_b[:], keep_sb[:, 0].rearrange("p g s -> p (g s)"), start=True, stop=False,
                              skip_group_check=True)
                    for n in range(4):
                        cols = slice(P * a, P * (a + 1))
                        mm = pe.matmul(bank[:, P * n:P * (n + 1)], stack1[0][0:A_ROWS, h0 + n, cols],
                                       stack1[1][0:A_ROWS, h0 + n, cols], start=False, stop=(n == 3),
                                       skip_group_check=True)
                    mm.then_inc(scores_a1, 1)

            def self_turn_max(j):
                pe.wait_ge(mparts1_ready, j + 1)
                mT = ps[:, F0, :].bitcast(BF16)
                for a in range(2):
                    mm = pe.transpose(mT[:, P * a:P * (a + 1)], mparts1[:, a], id_b[:])
                mm.then_inc(mT1_ps, 1)

            def self_exp_scores(j, c):
                a, h0 = c // 4, 4 * (c % 4)
                if c == 0:
                    pe.wait_ge(mrow1_ld, 16 * (j + 1))
                    pe.wait_ge(mT1_sb, j + 1)
                elif c > 3:
                    pe.wait_ge(exp1, 8 * j + c - 3)
                bank = ps[:, SELF_BANKS[c % 4], :]
                pe.matmul(bank, id_b[:], keep_sb[:, 1].rearrange("p g s -> p (g s)"), start=True, stop=False,
                          skip_group_check=True)
                for n in range(4):
                    cols = slice(P * a, P * (a + 1))
                    mm = pe.matmul(bank[:, P * n:P * (n + 1)], stack1[1][0:B_ROWS, h0 + n, cols],
                                   stack1[0][0:B_ROWS, h0 + n, cols], start=False, stop=(n == 3),
                                   skip_group_check=True)
                mm.then_inc(scores_b1, 1)

            def self_values(j, c):
                a, g = c // 4, c % 4
                pe.wait_ge(exp1, 8 * j + c + 1)
                if c == 4:
                    pe.wait_ge(o1_sb, 2 * j + 1)
                for n in range(4):
                    mm = pe.matmul(ps[32 * n:32 * n + 32, F1, P * g:P * (g + 1)], v1[:, a, 4 * g + n, :],
                                   prob[:, c, P * n:P * (n + 1)], start=True, stop=True)
                mm.then_inc(values1, 1)

            def self_step(j, c):
                if c < 8:
                    self_exp_scores(j, c)
                if c > 0:
                    self_values(j, c - 1)

            def self_project_out(j, a):
                pe.wait_ge(attn_ready, 2 * j + a + 1)
                for k in range(KT):
                    mm = pe.matmul(ps[:, F0, D * a:D * (a + 1)], attnT[:, k, P * a:P * (a + 1)],
                                   wout_sb[:, k, :], start=(k == 0), stop=(k == KT - 1))
                mm.then_inc(oproj, 1)

            def cross_project_context(i):
                pe.wait_ge(ctx_ld, 16 * (i + 1))
                wait(pe, mT2_sb, 2 * i)
                wait(pe, exp2, 32 * i)
                for a in range(2):
                    pe.matmul(ps[:, A0 + a, D:2 * D], wx_sb[:, 1, :], ctx_sb[:, a, :], start=True, stop=True)
                for n in range(4):
                    mm = pe.matmul(ps[:, B0, P * n:P * (n + 1)], ctx_sb[:, n // 2, P * (n % 2):P * (n % 2 + 1)],
                                   wx_sb[:, 2, :], start=True, stop=True)
                mm.then_inc(ctx_proj, 1)

            def cross_project(i):
                pe.wait_ge(xn2_ready, i + 1)
                for a in range(2):
                    mm = pe.matmul(ps[:, A0 + a, 0:D], wx_sb[:, 0, :], xn2[:, a, :], start=True, stop=True)
                mm.then_inc(q2_proj, 1)

            def cross_max_scores(i, a, chunks):
                for c in chunks:
                    if c == 0:
                        pe.wait_ge(stack2_ld[a], N_STACK2 * (i + 1))
                        if a == 0:
                            pe.wait_ge(qk2_done, 2 * i + 2)
                            pe.wait_ge(v2t_ready, i + 1)
                    if a == 0 and c >= 4:
                        pe.wait_ge(max2_done, 32 * i + c - 3)
                    elif a == 1:
                        pe.wait_ge(max2_done, 32 * i + 16 + c - 1 if c >= 2 else 32 * i + 13 + c)
                    for n in range(2):
                        h = 2 * (c % 8) + n
                        mm = pe.matmul(ps[:, A_BANKS[a][c % len(A_BANKS[a])], D * n:D * (n + 1)],
                                       stack2[a][0][0:A_ROWS, h, P * (c // 8):P * (c // 8 + 1)],
                                       stack2[a][1][0:A_ROWS, h, :], start=True, stop=True)
                    mm.then_inc(scores_a2, 1)

            def cross_turn_max(i, a):
                pe.wait_ge(mparts2_ready, 2 * i + a + 1)
                if a == 0:
                    wait(pe, o2_sb, 2 * i)
                mT = ps[:, (PV, A0)[a], :].bitcast(BF16)
                for t in range(2):
                    mm = pe.transpose(mT[:, P * t:P * (t + 1)], mparts2[:, a, t], id_b[:])
                mm.then_inc(mT2_ps, 1)

            def cross_exp_scores(i, a, h0):
                if h0 == 0:
                    pe.wait_ge(mrow2_ld[a], 16 * (i + 1))
                for h in (h0, h0 + 1):
                    u = 16 * a + h
                    if u >= 2:
                        pe.wait_ge(exp2, 32 * i + u - 1)
                    for t in range(2):
                        mm = pe.matmul(ps[:, B0 + h % 2, D * t:D * (t + 1)],
                                       stack2[a][1][0:B_ROWS, h, P * t:P * (t + 1)],
                                       stack2[a][0][0:B_ROWS, h, :], start=True, stop=True)
                    mm.then_inc(scores_b2, 1)

            def cross_values(i, a, g, t):
                if t == 0:
                    pe.wait_ge(exp2, 32 * i + 16 * a + 4 * g + 4)
                    if g == 0:
                        pe.wait_ge(v2_ready, i + 1)
                        if a == 0:
                            pe.wait_ge(mT2_sb, 2 * i + 1)
                        else:
                            pe.wait_ge(o2_sb, 2 * i + 1)
                for n in range(4):
                    h = 4 * g + n
                    mm = pe.matmul(ps[32 * n:32 * n + 32, PV + g // 2, D * (g % 2):D * (g % 2 + 1)],
                                   v2[:, 2 * a + t, h, :], prob[:, h % 8, D * t:D * (t + 1)],
                                   start=(t == 0), stop=(t == 1))
                if t == 1:
                    mm.then_inc(values2, 1)

            def cross_half(i, scores, values, t):
                if scores is not None:
                    cross_exp_scores(i, scores[0], 4 * scores[1] + 2 * t)
                if values is not None:
                    cross_values(i, *values, t)

            def experts_prepare(i, batches=BOTH, has_self=False):
                bank, rows = banks_of(batches), range(batches.start, batches.stop)
                pe.wait_ge(xn3_ready, i + 1)
                for k in range(KT):
                    for a in rows:
                        mm = pe.transpose(ps[:, bank.up[0], D * k + P * a:D * k + P * (a + 1)],
                                          xn3[:, a, P * k:P * (k + 1)], id_f[:])
                mm.then_inc(xT3_ps, 1)
                pe.wait_ge(xT3_sb, i + 1)
                if has_self:
                    pe.wait_ge(o1_sb, 2 * i + 4)
                for a in rows:
                    for k in range(KT):
                        mm = pe.matmul(ps[:, bank.down, E * a:E * (a + 1)], xn3T[:, k, P * a:P * (a + 1)],
                                       gate_sb[:, k, :], start=(k == 0), stop=(k == KT - 1))
                mm.then_inc(logits, 1)

            def expert_up(i, n, batches=BOTH):
                e, u, cols = ORDER[n], 9 * i + n, columns(batches)
                if n > 1:
                    pe.wait_ge(u_ready, u - 1)
                for w in range(2):
                    for k in range(KT):
                        mm = pe.matmul(ps[:, banks_of(batches).up[n % 2], D * w + cols.start:D * w + cols.stop],
                                       w13_sb[:, e, k, w, :], xn3T[:, k, cols], start=(k == 0), stop=(k == KT - 1))
                mm.then_inc(up, 1)

            def experts_gates(i, q, batches=BOTH):
                if q == 0:
                    pe.wait_ge(gates_ready, i + 1)
                else:
                    pe.wait_ge(g_sb, 4 * i + q)
                for n in range(2):
                    for a in range(batches.start, batches.stop):
                        e = 2 * q + n
                        mm = pe.matmul(ps[:, banks_of(batches).gates, D * n + P * a:D * n + P * (a + 1)],
                                       gates[:, a, e:e + 1].broadcast_to([P, P]), id_f[:], start=True, stop=True)
                mm.then_inc(g_ps, 1)

            def expert_down(i, n, batches=BOTH):
                e = ORDER[n]
                pe.wait_ge(h_ready, 9 * i + n + 1)
                for a in range(batches.start, batches.stop):
                    mm = pe.matmul(ps[:, banks_of(batches).down, D * a:D * (a + 1)], hT[:, n % 2, P * a:P * (a + 1)],
                                   w2_sb[:, e, :], start=(n == 0 and a == batches.start), stop=(n == E),
                                   skip_group_check=True)
                mm.then_inc(down, 1)

            def experts_first(i, batches=BOTH):
                expert_up(i, 0, batches)
                experts_gates(i, 0, batches)
                expert_up(i, 1, batches)

            def experts_rest(i, batches=BOTH, has_self=False):
                expert_up(i, 2, batches)
                for n in range(E + 1):
                    if n < 3:
                        experts_gates(i, n + 1, batches)
                    if n + 3 <= E:
                        expert_up(i, n + 3, batches)
                    expert_down(i, n, batches)
                    if n == 7 and has_self:
                        self_turn(i + 2)
                    if n == 6 and batches == FIRST:
                        experts_prepare(TURN1, SECOND)

            def body(i, has_self, has_experts):
                j = i + 1
                cross_project(i)
                if has_experts:
                    experts_rest(i - 1, has_self=has_self)
                elif has_self:
                    self_turn(j)
                for step in range(3):
                    if has_experts:
                        cross_max_scores(i, 0, range(4 * step, 4 * step + 4))
                    if step == 0 and has_experts:
                        pe.wait_ge(x3_ready, i)
                    if has_self:
                        if step < 2:
                            self_project(j, step)
                        else:
                            self_project_v(j)
                cross_max_scores(i, 0, range(12 if has_experts else 0, 16))
                cross_max_scores(i, 1, range(2))
                cross_turn_max(i, 0)
                cross_max_scores(i, 1, range(2, 8))
                for t in range(2):
                    cross_half(i, (0, 0), None, t)
                    cross_max_scores(i, 1, range(8 + 2 * t, 10 + 2 * t))
                for t in range(2):
                    cross_half(i, (0, 1), (0, 0), t)
                    cross_max_scores(i, 1, range(12 + 2 * t, 14 + 2 * t))
                cross_half(i, (0, 2), (0, 1), 0)
                cross_turn_max(i, 1)
                cross_half(i, (0, 2), (0, 1), 1)
                if has_self:
                    self_max_scores(j, range(1))
                for n, (scores, values) in enumerate((((0, 3), (0, 2)), ((1, 0), (0, 3)), ((1, 1), None))):
                    for t in range(2):
                        cross_half(i, scores, values, t)
                        if has_self:
                            self_max_scores(j, range(2 * n + t + 1, 2 * n + t + 2))
                cross_half(i, None, (1, 0), 0)
                if has_self:
                    self_max_scores(j, range(7, 8))
                cross_half(i, None, (1, 0), 1)
                for g in (2, 3):
                    for t in range(2):
                        cross_half(i, (1, g), (1, g - 1), t)
                        if has_self and (g, t) == (2, 0):
                            self_turn_max(j)
                for t in range(2):
                    cross_half(i, None, (1, 3), t)
                if has_self:
                    for c in range(9):
                        self_step(j, c)
                    cross_project_context(j)
                    experts_prepare(i, has_self=True)
                    for a in range(2):
                        self_project_out(j, a)
                    experts_first(i)

            pe.wait_ge(ld_ident, 16)
            self_turn(0)
            for n in range(2):
                self_project(0, n)
            self_project_v(0)
            pe.wait_ge(consts, 2)
            pe.wait_ge(fills1, 3)
            self_max_scores(0, range(8))
            self_turn_max(0)
            for c in range(9):
                self_step(0, c)
            pe.wait_ge(ld_rest, 16 * REST)
            cross_project_context(0)
            for a in range(2):
                self_project_out(0, a)
            body(0, True, False)
            with pe.Fori(1, PAIRS - 1) as i:
                body(i, True, True)
            body(PAIRS - 1, False, True)
            experts_prepare(TURN0, FIRST)
            experts_first(TURN0, FIRST)
            experts_rest(TURN0, FIRST)
            experts_first(TURN1, SECOND)
            experts_rest(TURN1, SECOND)

        @block.scalar
        def _(act):
            def self_tokens(j):
                act.wait_ge(xT1_ps, j + 1)
                act.copy(xn1T[:].rearrange("p k s -> p (k s)"), ps[:, F0, :]).then_inc(xT1_sb, 1)

            def self_split(j):
                act.wait_ge(rope_done, 2 * j + 2)
                act.copy(parts1[:, 0], qk1[:]).then_inc(high1, 1)
                act.wait_ge(proj1, 3 * j + 3)
                if isinstance(j, int) and j == 0:
                    act.wait_ge(fills1, 3)
                act.copy(v1[:, :, :, 0:HD1], ps[:, F1, :].rearrange("p (a h d) -> p a h d", a=2, h=H)
                         ).then_inc(v1_ready, 1)
                act.wait_ge(rest1_ready, j + 1)
                act.copy(parts1[:, 1], qk1[:]).then_inc(mid1, 1)

            def self_turn_max(j):
                act.wait_ge(mT1_ps, j + 1)
                act.copy(mT1[:], ps[0:3 * H, F0, :].bitcast(BF16)[:, 0:D]).then_inc(mT1_sb, 1)

            def self_exponential(j, c):
                act.wait_ge(scores_b1, 8 * j + c + 1)
                if c == 0:
                    if isinstance(j, int) and j == 0:
                        act.wait_ge(mrow_st, 32)
                    else:
                        act.wait_ge(values2, 8 * j)
                act.activation(prob[:, c, :], ps[:, SELF_BANKS[c % 4], :], ACT.Exp,
                               scale=float(HD1) ** -0.5).then_inc(exp1, 1)

            def self_out(j, a):
                act.wait_ge(values1, 8 * j + 4 * a + 4)
                wait(act, o1_st[a], 16 * j)
                act.copy(o1[:, :, P * a:P * (a + 1)], ps[:, F1, :].rearrange("p (g s) -> p g s", g=4)
                         ).then_inc(o1_sb, 1)

            def turn_max(i, a):
                act.wait_ge(mT2_ps, 2 * i + a + 1)
                act.copy(mT2[:, a, :], ps[0:3 * H, (PV, A0)[a], :].bitcast(BF16)[:, 0:D]).then_inc(mT2_sb, 1)

            def exponentials(i, a, heads):
                for h in heads:
                    u = 16 * a + h
                    act.wait_ge(scores_b2, 32 * i + u + 1)
                    if u < 8:
                        wait(act, values2, 8 * i)
                    elif h % 4 == 0:
                        act.wait_ge(values2, 8 * i + u // 4 - 1)
                    act.activation(prob[:, h % 8, :], ps[:, B0 + h % 2, :], ACT.Exp).then_inc(exp2, 1)

            def cross_out(i, a):
                act.wait_ge(values2, 8 * i + 4 * a + 4)
                wait(act, o2_st, 16 * (2 * i + a))
                act.copy(o2[:].rearrange("p g s -> p (g s)"), ps[:, PV:PV + 2, :].rearrange("p b n -> p (b n)")
                         ).then_inc(o2_sb, 1)

            def cross_high(i):
                act.wait_ge(qk2_done, 2 * i + 2)
                for a in range(2):
                    ins = act.copy(parts2[:, 0, :, a], qk2[:, a])
                ins.then_inc(high2, 1)

            def cross_mid(i):
                act.wait_ge(rest2_ready, i + 1)
                for a in range(2):
                    ins = act.copy(parts2[:, 1, :, a], qk2[:, a])
                ins.then_inc(mid2, 1)

            def experts_tokens(i, batches=BOTH):
                cols = columns(batches)
                act.wait_ge(xT3_ps, i + 1)
                act.copy(xn3T[:, :, cols],
                         ps[:, banks_of(batches).up[0], :].rearrange("p (k s) -> p k s", k=KT)[:, :, cols]
                         ).then_inc(xT3_sb, 1)

            def experts_logits(i, batches=BOTH):
                act.wait_ge(logits, i + 1)
                act.activation(ez[:, batches, :].rearrange("p a e -> p (a e)"),
                               ps[:, banks_of(batches).down, E * batches.start:E * batches.stop], ACT.Exp, scale=-1.0
                               ).then_inc(ez_ready, 1)

            def tanh_up(i, n, batches=BOTH):
                cols = columns(batches)
                act.wait_ge(u_ready, 9 * i + n + 1)
                if n >= 2 or batches == SECOND:
                    act.wait_ge(h_ready, 9 * i + n - 1)
                act.activation(tanh_u[:, n % 2, cols], u13[:, n % 2, 0, cols], ACT.Tanh, scale=0.5
                               ).then_inc(th_ready, 1)

            def experts_gates(i, q, batches=BOTH):
                cols = columns(batches)
                act.wait_ge(g_ps, 4 * i + q + 1)
                act.copy(g_bc[:, 2 * q:2 * q + 2, cols],
                         ps[:, banks_of(batches).gates, :].rearrange("p (e t) -> p e t", e=2)[:, :, cols]
                         ).then_inc(g_sb, 1)

            def experts_rest(i, first, batches=BOTH):
                for n in range(first, E + 1):
                    tanh_up(i, n, batches)
                    if 0 < n < 3:
                        experts_gates(i, n + 1, batches)
                    if n == 7 and batches == FIRST:
                        experts_tokens(TURN1, SECOND)

            def residual_base(i):
                act.wait_ge(x1_ready, i + 1)
                wait(act, out_st, 16 * i)
                act.copy(x2[:], x1[:]).then_inc(x2_based, 1)

            def body(i, has_self, has_experts):
                j, f = i + 1, i - 1
                if has_experts:
                    experts_gates(f, 1)
                cross_high(i)
                if has_experts:
                    tanh_up(f, 1)
                    experts_gates(f, 2)
                cross_mid(i)
                if has_experts:
                    experts_rest(f, 2)
                if has_self:
                    self_tokens(j)
                    self_split(j)
                turn_max(i, 0)
                residual_base(i)
                exponentials(i, 0, range(10))
                turn_max(i, 1)
                exponentials(i, 0, range(10, 16))
                exponentials(i, 1, range(4))
                cross_out(i, 0)
                exponentials(i, 1, range(4, 10))
                if has_self:
                    self_turn_max(j)
                exponentials(i, 1, range(10, 16))
                cross_out(i, 1)
                if has_self:
                    for c in range(8):
                        self_exponential(j, c)
                        if c == 4:
                            self_out(j, 0)
                    self_out(j, 1)
                    experts_tokens(i)
                    experts_logits(i)
                    experts_gates(i, 0)
                    tanh_up(i, 0)

            act.dma_start(cos_sb[:], cos).then_inc(ld_tables, 16)
            act.dma_start(sin_sb[:], sin).then_inc(ld_tables, 16)
            act.dma_start(keep_f[:, 0, :], keep_qk).then_inc(ld_keep, 16)
            act.dma_start(keep_f[:, 1, :], keep_kq).then_inc(ld_keep, 16)
            act.dma_start(m_all[:], mask.rearrange("b o t -> b (o t)")).then_inc(mall_ld, 16)
            self_tokens(0)
            for n, w in enumerate((wq, wk, wv)):
                act.dma_start(wx_sb[:, n, :], w).then_inc(ld_rest, 16)
            act.dma_start(bqk_sb[:, 0:1], bq).then_inc(ld_rest, 16)
            act.dma_start(bqk_sb[:, 1:2], bk).then_inc(ld_rest, 16)
            act.dma_start(bv_sb[:], bv.broadcast_to([P, P])).then_inc(ld_rest, 16)
            act.dma_start(ebias_sb[:], ebias.broadcast_to([P, E])).then_inc(ld_rest, 16)
            act.dma_start(gate_sb[:], gate.rearrange("(k p) n -> p k n", p=P)).then_inc(ld_rest, 16)
            act.dma_start(lower_sb[:].rearrange("p e f -> p (e f)"), lower.broadcast_to([P, E * E])
                          ).then_inc(ld_rest, 16)
            self_split(0)
            self_turn_max(0)
            for c in range(8):
                self_exponential(0, c)
                if c == 4:
                    self_out(0, 0)
            self_out(0, 1)
            body(0, True, False)
            with act.Fori(1, PAIRS - 1) as i:
                body(i, True, True)
            body(PAIRS - 1, False, True)
            experts_tokens(TURN0, FIRST)
            for turn, batches in ((TURN0, FIRST), (TURN1, SECOND)):
                experts_logits(turn, batches)
                experts_gates(turn, 0, batches)
                tanh_up(turn, 0, batches)
                experts_gates(turn, 1, batches)
                experts_rest(turn, 1, batches)

        @block.gpsimd
        def _(pool):
            nc.gpsimd.memset(minus_half[:], -0.5).then_inc(small_fills, 1)

            def inverse_deviation(which, turn):
                pool.wait_ge(var_ready[which], turn + 1)
                nc.gpsimd.tensor_tensor(rstd[:], var_eps[:], minus_half[:], ALU.pow).then_inc(rstd_ready[which], 1)

            def self_sine(j):
                for n in range(2):
                    pool.wait_ge(rope_read, 2 * j + n + 1)
                    part = swapped[:, n, :].rearrange("p (g s) -> p g s", g=4)
                    nc.gpsimd.tensor_tensor(part, part, sin_sb[:].rearrange("p (o s) -> p o s", o=1)
                                            .broadcast_to([P, 4, P]), ALU.mult).then_inc(sin_done, 1)

            def cross_mask_values(i):
                pool.wait_ge(v2t_ready, i + 1)
                pool.wait_ge(mbc_ld, 48 * (i + 1))
                wait(pool, values2, 8 * i)
                for n in range(4):
                    keep = m_col[:, n // 2, n % 2:n % 2 + 1].rearrange("p (o u) -> p o u", o=1)
                    ins = nc.gpsimd.tensor_tensor(v2[:, n, :, 0:HD2], v2t[:, n, :].rearrange("p (h d) -> p h d", h=H),
                                                  keep.broadcast_to([P, H, HD2]), ALU.mult)
                ins.then_inc(v2_ready, 1)

            def expert_product(i, n, batches=BOTH):
                u, cols = 9 * i + n, columns(batches)
                pool.wait_ge(u_ready, u + 1)
                if n >= 2 or batches == SECOND:
                    pool.wait_ge(h_ready, u - 1)
                nc.gpsimd.tensor_tensor(u_times_u3[:, n % 2, cols], u13[:, n % 2, 0, cols],
                                        u13[:, n % 2, 1, cols], ALU.mult
                                        ).then_inc(wu_ready, 1)

            def body(i, has_self, has_experts):
                j, f = i + 1, i - 1
                inverse_deviation(1, i)
                if has_experts:
                    expert_product(f, 0)
                    expert_product(f, 1)
                cross_mask_values(i)
                if has_experts:
                    for n in range(2, NORM_AT + 1):
                        expert_product(f, n)
                if has_self:
                    inverse_deviation(0, j)
                if has_experts:
                    for n in range(NORM_AT + 1, E + 1):
                        expert_product(f, n)
                if has_self:
                    self_sine(j)
                    self_parts(pool, nc.gpsimd, j)
                inverse_deviation(2, i)

            pool.wait_ge(small_fills, 1)
            inverse_deviation(0, 0)
            nc.gpsimd.memset(v1[:], 1.0).then_inc(fills1, 1)
            nc.gpsimd.memset(mparts1[:], 0.0).then_inc(fills1, 1)
            pool.wait_ge(fills1, 2)
            nc.gpsimd.memset(stack1[1][MAX_ROW:P], 1.0).then_inc(fills1, 1)
            pool.wait_ge(fills1, 3)
            pool.wait_ge(ld_tables, 32)
            self_sine(0)
            nc.gpsimd.memset(v2[:], 1.0).then_inc(fills2, 1)
            nc.gpsimd.memset(mparts2[:], 0.0).then_inc(fills2, 1)
            for a in range(2):
                for n in range(2):
                    nc.gpsimd.memset(stack2[a][n][:].bitcast(F32), 0.0).then_inc(fills2, 1)
            pool.wait_ge(fills2, 6)
            for a in range(2):
                nc.gpsimd.memset(stack2[a][1][MAX_ROW:P], 1.0).then_inc(fills2, 1)
            pool.wait_ge(fills2, 8)
            body(0, True, False)
            with pool.Fori(1, PAIRS - 1) as i:
                body(i, True, True)
            body(PAIRS - 1, False, True)
            for n in range(E + 1):
                expert_product(TURN0, n, FIRST)
                if n == SECOND_AT:
                    inverse_deviation(2, TURN1)
            for n in range(E + 1):
                expert_product(TURN1, n, SECOND)

        @block.vector
        def _(dve):
            v = nc.vector

            ln = [Chain(dve, s, 2) for s in (ln1_chain, ln2_chain, ln3_chain)]

            def layer_norm(which, turn, src, xn, ready, batches=BOTH):
                chain = ln[which]
                chain.start(turn)
                for a in range(batches.start, batches.stop):
                    ins = v.bn_stats(stats[:, a, :], src[:, a, :])
                chain.link(ins)
                v.memset(settled[:], 0.0)
                for a in range(batches.start, batches.stop):
                    ins = v.bn_aggr(moments[:, a, :], stats[:, a, :])
                chain.link(ins)
                v.tensor_scalar(var_eps[:, batches], moments[:, batches, 1:2], EPS, None, ALU.add
                                ).then_inc(var_ready[which], 1)
                dve.wait_ge(rstd_ready[which], turn + 1)
                for a in range(batches.start, batches.stop):
                    ins = v.tensor_scalar(xn[:, a, :], src[:, a, :], moments[:, a, 0:1], rstd[:, a, :],
                                          ALU.subtract, ALU.mult)
                ins.then_inc(ready, 1)
                chain.end()

            mrow = Chain(dve, mrow_chain, 11)

            def mask_rows():
                mrow.start(0)
                dve.wait_ge(mall_ld, 16)
                v.memset(mrow_k[:, 0:3, :], 1.0)
                mrow.link(v.tensor_scalar(m_pen[:], m_all[:], -1.0, 1.0, ALU.mult, ALU.add))
                mrow.link(v.tensor_scalar(m_pen[:], m_pen[:], -NEG, None, ALU.mult))
                for n, src in enumerate((m_pen, m_all)):
                    part = [mrow_q[:, 3 * n + c, :] for c in range(3)]
                    mrow.link(v.tensor_copy(part[0], src[:]))
                    mrow.link(v.tensor_tensor(m_r[:, n, :], src[:], part[0], ALU.subtract))
                    mrow.link(v.tensor_copy(part[1], m_r[:, n, :]))
                    if n == 0:
                        mrow.link(v.tensor_tensor(part[2], m_r[:, n, :], part[1], ALU.subtract))
                v.tensor_tensor(mrow_q[:, 5, :], m_r[:, 1, :], mrow_q[:, 4, :], ALU.subtract).then_inc(mrow_chain, 1)
                mrow.n += 1
                dve.wait_ge(mrow_chain, mrow.n)
                for r in (2, 3):
                    v.tensor_copy(mrow_q[:, 3 * r:3 * r + 3, :], mrow_q[:, 3:6, :])
                for c in range(3):
                    src = mrow_q[:, c:c + 1, :]
                    ins = v.tensor_copy(mrow_k[:, 3 + 3 * c:6 + 3 * c, :], src.broadcast_to([B, 3, D]))
                assert mrow.n == 10
                ins.then_inc(mrow_chain, 1)

            mp1 = Chain(dve, mp1_chain, 3)
            mp2 = Chain(dve, mp2_chain, 3)

            def max_parts(chain, turn, top, rest, parts, ready):
                parts = parts[:, :, 0:3 * H].rearrange("p t (c h) -> p t c h", c=3)
                chain.start(turn)
                chain.link(v.tensor_scalar(parts[:, :, 0, :], top, -1.0, None, ALU.mult))
                chain.link(v.scalar_tensor_tensor(rest, top, -1.0, parts[:, :, 0, :], ALU.mult, ALU.subtract))
                chain.link(v.tensor_copy(parts[:, :, 1, :], rest))
                v.tensor_tensor(parts[:, :, 2, :], rest, parts[:, :, 1, :], ALU.subtract).then_inc(ready, 1)
                chain.end()

            def self_norm(j):
                dve.wait_ge(x_ld, 16 * (j + 1))
                wait(dve, xT1_ps, j)
                layer_norm(0, j, x_in, xn1, xn1_ready)

            def self_rope(j, n):
                dve.wait_ge(proj1, 3 * j + n + 1)
                v.tensor_tensor(qk1[:, n, :].rearrange("p (g s) -> p g s", g=4),
                                ps[:, (F1, F0)[n], :].rearrange("p (g s) -> p g s", g=4),
                                cos_sb[:].rearrange("p (o s) -> p o s", o=1).broadcast_to([P, 4, P]), ALU.mult)
                v.stream_shuffle(swapped[:, n, :], ps[:, (F1, F0)[n], :], [lane ^ H for lane in range(32)]
                                 ).then_inc(rope_read, 1)

            def self_rope_sum(j, n):
                dve.wait_ge(rope_read, 2 * j + n + 1)
                dve.wait_ge(sin_done, 2 * j + n + 1)
                v.tensor_tensor(qk1[:, n, :], qk1[:, n, :], swapped[:, n, :], ALU.add).then_inc(rope_done, 1)

            def self_max(j):
                for c in range(8):
                    a, h0 = c // 4, 4 * (c % 4)
                    dve.wait_ge(scores_a1, 8 * j + c + 1)
                    v.tensor_reduce(max1[:, a, h0:h0 + 4], ps[:, (F0, F1)[c % 2], :].rearrange("p (g s) -> p g s", g=4),
                                    AX.X, ALU.max).then_inc(max1_done, 1)
                dve.wait_ge(max1_done, 8 * (j + 1))
                max_parts(mp1, j, max1[:], mrest1[:], mparts1, mparts1_ready)

            def self_normalise(j, a):
                cols = slice(P * a, P * (a + 1))
                dve.wait_ge(o1_ld[a], 64 * (j + 1))
                v.reciprocal(o1s[:, :, cols], o1s[:, :, cols]).then_inc(o1_inverse, 1)
                dve.wait_ge(o1_inverse, 2 * j + a + 1)
                v.tensor_tensor(attnT[:, :, cols], o1d[:, :, cols], o1s[:, :, cols], ALU.mult).then_inc(attn_ready, 1)

            def self_residual(j):
                dve.wait_ge(oproj, 2 * j + 2)
                wait(dve, x2_based, j)
                v.tensor_tensor(x1[:].rearrange("p a d -> p (a d)"), ps[:, F0, :],
                                x_in[:].rearrange("p a d -> p (a d)"), ALU.add).then_inc(x1_ready, 1)

            x2c = Chain(dve, x2_chain, 3)

            def cross_norm(i):
                dve.wait_ge(x1_ready, i + 1)
                wait(dve, q2_proj, i)
                layer_norm(1, i, x1, xn2, xn2_ready)

            def cross_bias(i):
                dve.wait_ge(mbc_ld, 48 * (i + 1))
                v.tensor_scalar(m_bcs[:], m_bc[:], float(HD2) ** -0.5, None, ALU.mult).then_inc(mbcs_ready, 1)
                dve.wait_ge(mbcs_ready, i + 1)
                dve.wait_ge(ctx_proj, i + 1)
                dve.wait_ge(q2_proj, i + 1)
                for a in range(2):
                    v.scalar_tensor_tensor(qk2[:, a, 0, :], ps[:, A0 + a, 0:D], bqk_sb[:, 0:1], m_bcs[:, a, :],
                                           ALU.add, ALU.mult)
                    v.scalar_tensor_tensor(qk2[:, a, 1, :], ps[:, A0 + a, D:2 * D], bqk_sb[:, 1:2], m_bc[:, a, :],
                                           ALU.add, ALU.mult).then_inc(qk2_done, 1)

            def cross_value_bias(i):
                dve.wait_ge(ctx_proj, i + 1)
                wait(dve, v2_ready, i)
                v.tensor_tensor(v2t[:], ps[:, B0, :].rearrange("p (n c) -> p n c", n=4),
                                bv_sb[:].rearrange("p (o c) -> p o c", o=1).broadcast_to([P, 4, P]), ALU.add
                                ).then_inc(v2t_ready, 1)

            def cross_rest(i):
                dve.wait_ge(high2, i + 1)
                for a in range(2):
                    ins = v.tensor_tensor(qk2[:, a], qk2[:, a], parts2[:, 0, :, a], ALU.subtract)
                ins.then_inc(rest2_ready, 1)

            def cross_low(i):
                dve.wait_ge(mid2, i + 1)
                dve.wait_ge(rest2_ready, i + 1)
                for a in range(2):
                    ins = v.tensor_tensor(parts2[:, 2, :, a], qk2[:, a], parts2[:, 1, :, a], ALU.subtract)
                ins.then_inc(parts2_ready, 1)

            def cross_max_parts(i, a):
                dve.wait_ge(max2_done, 32 * i + 16 * a + 16)
                max_parts(mp2, 2 * i + a, max2[:, a], mrest2[:, a], mparts2[:, a], mparts2_ready)

            def cross_max(i, a, chunks):
                for c in chunks:
                    dve.wait_ge(scores_a2, 32 * i + 16 * a + c + 1)
                    v.tensor_reduce(max2[:, a, c // 8, 2 * (c % 8):2 * (c % 8) + 2],
                                    ps[:, A_BANKS[a][c % len(A_BANKS[a])], :].rearrange("p (g s) -> p g s", g=2), AX.X, ALU.max
                                    ).then_inc(max2_done, 1)

            def cross_out(i, a):
                x2c.start(2 * i + a)
                dve.wait_ge(o2_ld[a], 32 * (i + 1))
                x2c.link(v.reciprocal(o2s[:, a, :], o2s[:, a, :]))
                x2c.link(v.tensor_tensor(o2d[:, a, :], o2d[:, a, :], o2s[:, a, :], ALU.mult))
                x2c.link(v.tensor_tensor(o2d[:, a, :], o2d[:, a, :], m_bc[:, a, :], ALU.mult))
                dve.wait_ge(x2_based, i + 1)
                v.tensor_tensor(x2[:, a, :], x2[:, a, :], o2d[:, a, :], ALU.add).then_inc(x2_ready, 1)
                x2c.end()

            route = Chain(dve, route_chain, 7)

            def experts_norm(i, batches=BOTH):
                dve.wait_ge(x2_ready, 2 * PAIRS if batches == SECOND else 2 * i + batches.stop)
                layer_norm(2, i, x2, xn3, xn3_ready, batches)

            def read_up(i, n, batches=BOTH):
                cols = columns(batches)
                dve.wait_ge(up, 9 * i + n + 1)
                if n >= 2 or batches == SECOND:
                    dve.wait_ge(th_ready, 9 * i + n - 1)
                    dve.wait_ge(wu_ready, 9 * i + n - 1)
                src = ps[:, banks_of(batches).up[n % 2], :].rearrange("p (w t) -> p w t", w=2)[:, :, cols]
                if ORDER[n] == E:
                    ins = v.tensor_copy(u13[:, n % 2, :, cols], src)
                else:
                    dve.wait_ge(g_sb, 4 * i + ORDER[n] // 2 + 1)
                    gate_row = g_bc[:, ORDER[n]:ORDER[n] + 1, cols]
                    ins = v.tensor_tensor(u13[:, n % 2, :, cols], src,
                                          gate_row.broadcast_to([P, 2, cols.stop - cols.start]), ALU.mult)
                ins.then_inc(u_ready, 1)

            def hidden(i, n, batches=BOTH):
                cols = columns(batches)
                dve.wait_ge(th_ready, 9 * i + n + 1)
                dve.wait_ge(wu_ready, 9 * i + n + 1)
                if n >= 2 or batches == SECOND:
                    dve.wait_ge(down, 9 * i + n - 1)
                v.scalar_tensor_tensor(hT[:, n % 2, cols], tanh_u[:, n % 2, cols], 1.0, u_times_u3[:, n % 2, cols],
                                       ALU.add, ALU.mult).then_inc(h_ready, 1)

            def experts_route(i, batches=BOTH):
                b, nb = batches, batches.stop - batches.start
                dve.wait_ge(ez_ready, i + 1)
                route.start(i)
                route.link(v.tensor_scalar(den[:, b], ez[:, b], 1.0, None, ALU.add))
                route.link(v.reciprocal(score[:, b], den[:, b]))
                route.link(v.tensor_tensor(biased[:, b], score[:, b],
                                           ebias_sb[:].rearrange("p (o e) -> p o e", o=1).broadcast_to([P, nb, E]),
                                           ALU.add))
                other = biased[:, b].rearrange("p a (o f) -> p a o f", o=1).broadcast_to([P, nb, E, E])
                own = biased[:, b].rearrange("p a (e o) -> p a e o", o=1).broadcast_to([P, nb, E, E])
                v.tensor_tensor(above[:, b], other, own, ALU.is_gt)
                route.link(v.tensor_tensor(equal[:, b], other, own, ALU.is_equal))
                route.link(v.tensor_tensor(equal[:, b], equal[:, b],
                                           lower_sb[:].rearrange("p (o e) f -> p o e f", o=1)
                                           .broadcast_to([P, nb, E, E]), ALU.mult))
                route.link(v.tensor_tensor(above[:, b], above[:, b], equal[:, b], ALU.add))
                route.link(v.tensor_reduce(rank[:, b], above[:, b], AX.X, ALU.add))
                v.scalar_tensor_tensor(gates[:, b], rank[:, b], 2.0, score[:, b], ALU.is_lt, ALU.mult
                                       ).then_inc(gates_ready, 1)
                route.end()

            def experts_rest(i, first, batches=BOTH, meanwhile=None):
                for n in range(first, E + 1):
                    read_up(i, n, batches)
                    hidden(i, n - 1, batches)
                    if n == NORM_AT and meanwhile is not None:
                        self_norm(meanwhile)
                    if n == SECOND_AT and batches == FIRST:
                        cross_out(PAIRS - 1, 1)
                        experts_norm(TURN1, SECOND)
                hidden(i, E, batches)
                if batches == FIRST:
                    experts_route(TURN1, SECOND)
                dve.wait_ge(down, 9 * (i + 1))
                v.scalar_tensor_tensor(x2[:, batches], ps[:, banks_of(batches).down, :]
                                       .rearrange("p (a d) -> p a d", a=2)[:, batches], 0.5,
                                       x2[:, batches], ALU.mult, ALU.add).then_inc(x3_ready, 1)

            def body(i, has_self, has_experts):
                j, f = i + 1, i - 1
                cross_norm(i)
                if has_experts:
                    read_up(f, 0)
                    read_up(f, 1)
                cross_bias(i)
                if has_experts:
                    hidden(f, 0)
                cross_rest(i)
                if has_experts:
                    read_up(f, 2)
                    hidden(f, 1)
                cross_low(i)
                if has_experts:
                    experts_rest(f, 3, meanwhile=j if has_self else None)
                    for step in range(4):
                        cross_max(i, 0, range(4 * step, 4 * step + 4))
                        if has_self and step < 2:
                            self_rope(j, step)
                        if has_self and 0 < step < 3:
                            self_rope_sum(j, step - 1)
                else:
                    self_norm(j)
                    for n in range(2):
                        self_rope(j, n)
                    for n in range(2):
                        self_rope_sum(j, n)
                    cross_max(i, 0, range(16))
                cross_max_parts(i, 0)
                cross_max(i, 1, range(16))
                cross_max_parts(i, 1)
                if has_self:
                    self_max(j)
                cross_out(i, 0)
                if has_self:
                    cross_out(i, 1)
                    experts_norm(i)
                    cross_value_bias(j)
                    for a in range(2):
                        self_normalise(j, a)
                    experts_route(i)
                    self_residual(j)

            dve.wait_ge(small_fills, 1)
            self_norm(0)
            dve.wait_ge(ld_ident, 16)
            dve.wait_ge(ld_keep, 32)
            v.tensor_copy(id_b[:], id_f[:]).then_inc(consts, 1)
            v.tensor_copy(keep_sb[:], keep_f[:].rearrange("p n (o s) -> p n o s", o=1).broadcast_to([P, 2, 4, P])
                          ).then_inc(consts, 1)
            dve.wait_ge(ld_tables, 32)
            for n in range(2):
                self_rope(0, n)
            for n in range(2):
                self_rope_sum(0, n)
            self_parts(dve, v, 0)
            mask_rows()
            dve.wait_ge(fills1, 3)
            self_max(0)
            for a in range(2):
                self_normalise(0, a)
            dve.wait_ge(ld_rest, 16 * REST)
            cross_value_bias(0)
            self_residual(0)
            dve.wait_ge(fills2, 6)
            body(0, True, False)
            with dve.Fori(1, PAIRS - 1) as i:
                body(i, True, True)
            body(PAIRS - 1, False, True)
            experts_norm(TURN0, FIRST)
            experts_route(TURN0, FIRST)
            for turn, batches in ((TURN0, FIRST), (TURN1, SECOND)):
                read_up(turn, 0, batches)
                experts_rest(turn, 1, batches)


def _tables():
    inv = 1.0 / 10000.0 ** (np.arange(0, HD1, 2, dtype=np.float32) / HD1)
    angle = np.outer(inv, np.arange(P, dtype=np.float32)).astype(np.float32)
    sign = np.where(np.arange(HD1 // 2) % 2 == 0, -1.0, 1.0)[:, None]
    cos = np.repeat(np.cos(angle), H, axis=0).astype(np.float32)
    sin = np.repeat(np.sin(angle) * sign, H, axis=0).astype(np.float32)
    q, k = np.arange(P)[:, None], np.arange(P)[None, :]
    keep = np.where((q - k >= 0) & (q - k < WINDOW), 0.0, MASKED).astype(np.float32)
    lower = (np.arange(E)[None, :] < np.arange(E)[:, None]).astype(np.float32).reshape(1, E * E)
    return cos, sin, keep, np.ascontiguousarray(keep.T), np.eye(P, dtype=np.float32), lower


def kernel(**inputs):
    import concourse.bacc as _bacc
    from concourse.bass_utils import run_bass_kernel_spmd as _run

    get = {k: np.asarray(v) for k, v in inputs.items()}
    depth, head = np.arange(HD1)[:, None], np.arange(H)[None, :]
    own = (head * HD1 + depth).reshape(-1)
    wqkv = get["L0_attn_w_qkv"]
    rows = np.concatenate([own, D + own, 2 * D + np.arange(D)])
    cross = (np.arange(H)[None, :] * HD2 + np.arange(HD2)[:, None]).reshape(-1)
    w1 = np.concatenate([get["L0_ffn_w1"], get["L0_ffn_sw1"][None]])
    w3 = np.concatenate([get["L0_ffn_w3"], get["L0_ffn_sw3"][None]])
    w2 = np.concatenate([get["L0_ffn_w2"], get["L0_ffn_sw2"][None]])
    w13 = np.stack([w1, w3]).reshape(2, E + 1, P, KT, P).transpose(4, 1, 3, 0, 2)
    arrays = {
        "x": get["x"], "ctx": get["ctx_2048"], "mask": get["mask_Bx1x2048_fk1"],
        "wqkv": wqkv[rows].T, "wout": get["L0_attn_w_out"].T,
        "wq": get["L0_xattn_Wq"][cross].T, "wk": get["L0_xattn_Wk"][cross].T, "wv": get["L0_xattn_Wv"].T,
        "bq": get["L0_xattn_bq"][cross][:, None], "bk": get["L0_xattn_bk"][cross][:, None],
        "bv": get["L0_xattn_bv"][None], "ebias": get["L0_ffn_expert_bias"][None],
        "gate": get["L0_ffn_gate_w"].T, "w13": w13, "w2": w2.transpose(2, 0, 1),
    }
    arrays.update(zip(("cos", "sin", "keep_qk", "keep_kq", "ident", "lower"), _tables()))
    nc = _bacc.Bacc("TRN2", target_bir_lowering=False, num_devices=1)
    feed, args = {}, []
    for name, a in arrays.items():
        a = np.ascontiguousarray(a)
        feed[f"in_{name}"] = a
        args.append(nc.dram_tensor(f"in_{name}", a.shape, mybir.dt.from_np(a.dtype), kind="ExternalInput").ap())
    args.append(nc.dram_tensor("out_0", (B, P, D), F32, kind="ExternalOutput").ap())
    decoder(nc, *args)
    r = _run(nc, [feed], core_ids=[0])
    return r.results[0]["out_0"]
```
